# Optimizing a Trainium2 kernel written in Bass

```python
import numpy as np
import jax
import jax.numpy as jnp

def _softmax(x, axis=-1):
    return jax.nn.softmax(x, axis=axis)

def _gelu(x):
    return jax.nn.gelu(x, approximate=True)

def _silu(x):
    return jax.nn.silu(x)

def _sigmoid(x):
    return jax.nn.sigmoid(x)

def _layernorm(x, axis=-1, eps=1e-05):
    m = jnp.mean(x, axis=axis, keepdims=True)
    v = jnp.var(x, axis=axis, keepdims=True)
    return (x - m) / jnp.sqrt(v + eps)

def _scatter_add(tgt, idx, src, axis=0):
    return tgt.at[idx].add(src)

def _segment_sum(src, seg, n):
    return jax.ops.segment_sum(src, seg, n)
kernel_name = 'mk_decoder_postln_d1_seqx_r4_c6a8c0'

def setup_inputs(seed: int=0):
    np.random.seed(seed)
    _w = jnp.asarray

    def _rec_inputs():
        import jax
        import jax.numpy as jnp
        _rk = jax.random.key(seed)
        x = -0.0002928 + 1 * jax.random.normal(jax.random.fold_in(_rk, 1), (16, 128, 256), jnp.float32)
        _lenS = 128 - jax.random.randint(jax.random.fold_in(_rk, 7), (16,), 0, max(1, 128 // 4) + 1, jnp.int32)
        _lenS2 = 128 - jax.random.randint(jax.random.fold_in(_rk, 8), (16,), 0, max(1, 128 // 4) + 1, jnp.int32)
        _ctx_1024P = jax.random.normal(jax.random.fold_in(_rk, 11), (16, 16, 256), jnp.float32)
        _ctx_1024c = jax.random.dirichlet(jax.random.fold_in(_rk, 511), 0.3 * jnp.ones((16,), jnp.float32), (16, 128))
        _ctx_1024t = jnp.einsum('bsk,bkd->bsd', _ctx_1024c, _ctx_1024P)
        _ctx_1024t = _ctx_1024t * jax.lax.rsqrt(jnp.mean(jnp.square(_ctx_1024t)) + 1e-12) * 0.953939
        ctx_1024 = -1.39393e-06 + 0.999914 * (_ctx_1024t + 0.3 * jax.random.normal(jax.random.fold_in(_rk, 611), (16, 128, 256), jnp.float32))
        return (x, ctx_1024)
    x, ctx_1024 = _rec_inputs()

    def _L0_attn_setup():
        import jax, jax.numpy as jnp
        import numpy as np
        SEGMENT_LENGTH = 64
        DILATION_RATE = 4
        NUM_HEADS = 16
        HEAD_DIM = 64

        def dilated_mask(seq_len):
            pos = jnp.arange(seq_len)
            seg = pos // SEGMENT_LENGTH
            local = seg[None, :] == seg[:, None]
            diff = jnp.abs(pos[None, :] - pos[:, None])
            dil = (diff > 0) & (diff % DILATION_RATE == 0) & (diff <= DILATION_RATE * SEGMENT_LENGTH)
            allowed = local | dil
            return jnp.where(allowed, 0.0, -jnp.inf).astype(jnp.float32)
        key = jax.random.key(seed)
        ks = jax.random.split(key, 5)
        B, S, D = (2, 512, 256)
        scale = 1.0 / np.sqrt(D)
        return {'hidden_states': jax.random.normal(ks[0], (B, S, D), jnp.float32), 'w_q': jax.random.normal(ks[1], (D, NUM_HEADS * HEAD_DIM), jnp.float32) * scale, 'w_k': jax.random.normal(ks[2], (D, NUM_HEADS * HEAD_DIM), jnp.float32) * scale, 'w_v': jax.random.normal(ks[3], (D, NUM_HEADS * HEAD_DIM), jnp.float32) * scale, 'w_o': jax.random.normal(ks[4], (NUM_HEADS * HEAD_DIM, D), jnp.float32) * scale}
    _L0_attn_all = _L0_attn_setup()
    _L0_attn_in = {k: v for k, v in _L0_attn_all.items() if k in ('w_q', 'w_k', 'w_v', 'w_o')}
    del _L0_attn_all

    def _L0_xattn_setup():
        import jax, jax.numpy as jnp
        import numpy as np
        B, S, D = (1, 1024, 256)
        NUM_HEADS, HEAD_DIM = (16, 64)
        WINDOW = 128
        EMBED = NUM_HEADS * HEAD_DIM
        key = jax.random.key(seed)
        ks = jax.random.split(key, 7)
        scale_in = 1.0 / np.sqrt(D)
        scale_e = 1.0 / np.sqrt(EMBED)
        return {'query': jax.random.normal(ks[0], (B, S, D), dtype=jnp.float32), 'key': jax.random.normal(ks[1], (B, S, D), dtype=jnp.float32), 'value': jax.random.normal(ks[2], (B, S, D), dtype=jnp.float32), 'Wq': jax.random.normal(ks[3], (D, EMBED), dtype=jnp.float32) * scale_in, 'Wk': jax.random.normal(ks[4], (D, EMBED), dtype=jnp.float32) * scale_in, 'Wv': jax.random.normal(ks[5], (D, EMBED), dtype=jnp.float32) * scale_in, 'Wo': jax.random.normal(ks[6], (EMBED, D), dtype=jnp.float32) * scale_e}
    _L0_xattn_all = _L0_xattn_setup()
    _L0_xattn_in = {k: v for k, v in _L0_xattn_all.items() if k in ('Wq', 'Wk', 'Wv', 'Wo')}
    del _L0_xattn_all

    def _L0_ffn_setup():
        import jax, jax.numpy as jnp
        import numpy as np
        TOP_K = 2
        key = jax.random.key(seed)
        k1, k2, k3, k4, k5 = jax.random.split(key, 5)
        B, S, D, F, E = (2, 256, 256, 512, 8)
        return {'x': jax.random.normal(k1, (B, S, D), dtype=jnp.float32), 'router_kernel_DE': jax.random.normal(k2, (D, E), dtype=jnp.float32) * 0.02, 'kernel_gating_EDF': jax.random.normal(k3, (E, D, F), dtype=jnp.float32) * 0.02, 'kernel_up_EDF': jax.random.normal(k4, (E, D, F), dtype=jnp.float32) * 0.02, 'kernel_down_EFD': jax.random.normal(k5, (E, F, D), dtype=jnp.float32) * 0.02}
    _L0_ffn_all = _L0_ffn_setup()
    _L0_ffn_in = {k: v for k, v in _L0_ffn_all.items() if k in ('router_kernel_DE', 'kernel_gating_EDF', 'kernel_up_EDF', 'kernel_down_EFD')}
    del _L0_ffn_all
    return {'x': x, 'ctx_1024': ctx_1024, 'L0_attn_w_q': _L0_attn_in['w_q'], 'L0_attn_w_k': _L0_attn_in['w_k'], 'L0_attn_w_v': _L0_attn_in['w_v'], 'L0_attn_w_o': _L0_attn_in['w_o'], 'L0_xattn_Wq': _L0_xattn_in['Wq'], 'L0_xattn_Wk': _L0_xattn_in['Wk'], 'L0_xattn_Wv': _L0_xattn_in['Wv'], 'L0_xattn_Wo': _L0_xattn_in['Wo'], 'L0_ffn_router_kernel_DE': _L0_ffn_in['router_kernel_DE'], 'L0_ffn_kernel_gating_EDF': _L0_ffn_in['kernel_gating_EDF'], 'L0_ffn_kernel_up_EDF': _L0_ffn_in['kernel_up_EDF'], 'L0_ffn_kernel_down_EFD': _L0_ffn_in['kernel_down_EFD']}

def reference(x, ctx_1024, L0_attn_w_q, L0_attn_w_k, L0_attn_w_v, L0_attn_w_o, L0_xattn_Wq, L0_xattn_Wk, L0_xattn_Wv, L0_xattn_Wo, L0_ffn_router_kernel_DE, L0_ffn_kernel_gating_EDF, L0_ffn_kernel_up_EDF, L0_ffn_kernel_down_EFD):
    import jax
    import jax.numpy as jnp

    def _L0_attn_ref(hidden_states, w_q, w_k, w_v, w_o):
        import jax, jax.numpy as jnp
        import numpy as np
        SEGMENT_LENGTH = 64
        DILATION_RATE = 4
        NUM_HEADS = 16
        HEAD_DIM = 64

        def dilated_mask(seq_len):
            pos = jnp.arange(seq_len)
            seg = pos // SEGMENT_LENGTH
            local = seg[None, :] == seg[:, None]
            diff = jnp.abs(pos[None, :] - pos[:, None])
            dil = (diff > 0) & (diff % DILATION_RATE == 0) & (diff <= DILATION_RATE * SEGMENT_LENGTH)
            allowed = local | dil
            return jnp.where(allowed, 0.0, -jnp.inf).astype(jnp.float32)
        B, S, D = hidden_states.shape
        H, Dh = (NUM_HEADS, HEAD_DIM)
        scaling = Dh ** (-0.5)
        q = (hidden_states @ w_q).reshape(B, S, H, Dh)
        k = (hidden_states @ w_k).reshape(B, S, H, Dh)
        v = (hidden_states @ w_v).reshape(B, S, H, Dh)
        mask = dilated_mask(S)
        scores = jnp.einsum('bqhd,bkhd->bhqk', q, k) * scaling + mask[None, None]
        attn = jax.nn.softmax(scores.astype(jnp.float32), axis=-1).astype(q.dtype)
        out = jnp.einsum('bhqk,bkhd->bqhd', attn, v).reshape(B, S, H * Dh)
        return out @ w_o

    def _L0_xattn_ref(query, key, value, Wq, Wk, Wv, Wo):
        import jax, jax.numpy as jnp
        import numpy as np
        B, S, D = (1, 1024, 256)
        NUM_HEADS, HEAD_DIM = (16, 64)
        WINDOW = 128
        EMBED = NUM_HEADS * HEAD_DIM
        Bq, Sq, _ = query.shape
        q = (query @ Wq).reshape(Bq, Sq, NUM_HEADS, HEAD_DIM).transpose(0, 2, 1, 3)
        k = (key @ Wk).reshape(Bq, Sq, NUM_HEADS, HEAD_DIM).transpose(0, 2, 1, 3)
        v = (value @ Wv).reshape(Bq, Sq, NUM_HEADS, HEAD_DIM).transpose(0, 2, 1, 3)
        idx = jnp.arange(Sq)
        local_mask = jnp.abs(idx[:, None] - idx[None, :]) > WINDOW
        scores = jnp.einsum('bhqd,bhkd->bhqk', q, k) / jnp.sqrt(jnp.float32(HEAD_DIM))
        scores = jnp.where(local_mask, -jnp.inf, scores)
        attn = jax.nn.softmax(scores, axis=-1)
        out = jnp.einsum('bhqk,bhkd->bhqd', attn, v)
        out = out.transpose(0, 2, 1, 3).reshape(Bq, Sq, EMBED)
        return out @ Wo

    def _L0_ffn_ref(x, router_kernel_DE, kernel_gating_EDF, kernel_up_EDF, kernel_down_EFD):
        import jax, jax.numpy as jnp
        import numpy as np
        TOP_K = 2
        E = router_kernel_DE.shape[-1]
        x = x.astype(jnp.float32)
        logits_BSE = jnp.einsum('BSD,DE->BSE', x, router_kernel_DE)
        probs_BSE = jax.nn.softmax(logits_BSE.astype(jnp.float32), axis=-1)
        weights_BSK, indices_BSK = jax.lax.top_k(probs_BSE, TOP_K)
        norm_weights_BSK = jax.nn.softmax(weights_BSK, axis=-1)
        one_hot_BSKE = jax.nn.one_hot(indices_BSK, num_classes=E, dtype=x.dtype)
        full_weights_BSE = jnp.sum(one_hot_BSKE * norm_weights_BSK[..., None], axis=2)
        gating_BSEF = jnp.einsum('BSD,EDF->BSEF', x, kernel_gating_EDF)
        act_BSEF = jax.nn.silu(gating_BSEF)
        up_BSEF = jnp.einsum('BSD,EDF->BSEF', x, kernel_up_EDF)
        fuse_BSEF = act_BSEF * up_BSEF
        down_BSED = jnp.einsum('BSEF,EFD->BSED', fuse_BSEF, kernel_down_EFD)
        out_BSD = jnp.einsum('BSED,BSE->BSD', down_BSED, full_weights_BSE)
        return out_BSD.astype(jnp.float32)
    x = _layernorm(x + _L0_attn_ref(x, L0_attn_w_q, L0_attn_w_k, L0_attn_w_v, L0_attn_w_o), axis=-1)
    x = _layernorm(x + _L0_xattn_ref(x, ctx_1024, ctx_1024, L0_xattn_Wq, L0_xattn_Wk, L0_xattn_Wv, L0_xattn_Wo), axis=-1)
    x = _layernorm(x + _L0_ffn_ref(x, L0_ffn_router_kernel_DE, L0_ffn_kernel_gating_EDF, L0_ffn_kernel_up_EDF, L0_ffn_kernel_down_EFD), axis=-1)
    return x

_drawn_inputs = setup_inputs


def setup_inputs(seed=0):
    import zlib

    import numpy as np

    out = dict(_drawn_inputs(seed))
    spreads = {}
    factors = {'L0_ffn_router_kernel_DE': 3.931,
     'L0_ffn_kernel_gating_EDF': 3.395,
     'L0_ffn_kernel_up_EDF': 3.357,
     'L0_ffn_kernel_down_EFD': 3.365}
    for name, (base, spread) in spreads.items():
        noise = np.random.default_rng([zlib.crc32(name.encode()), seed]).standard_normal(out[name].shape)
        drawn = base * np.exp(spread * noise) if base else spread * noise
        out[name] = jnp.asarray(drawn.astype(out[name].dtype))
    for name, factor in factors.items():
        out[name] = (out[name] * factor).astype(out[name].dtype)
    return out
```

```python
from contextlib import ExitStack

import concourse.bass as bass
from concourse import mybir

ALU = mybir.AluOpType
ACT = mybir.ActivationFunctionType
AX = mybir.AxisListType
F32 = mybir.dt.float32
F32R = mybir.dt.float32r
BF16 = mybir.dt.bfloat16

P = 128
HEADS = 16
DH = 64
SEG = 64
DIL = 4
EPS = 1e-5
OUT_SLOT = 3
NORM_SLOT = 5
MASKED = -1e30
PAIR = 2
UNIT_HEADS = 4
GROUPS = HEADS // UNIT_HEADS
UNITS = GROUPS * PAIR
RING = 4
CHUNKS = UNIT_HEADS // 2


def terms(hi_a, lo_a, hi_b, lo_b):
    return ((hi_a, hi_b), (hi_a, lo_b), (lo_a, hi_b))


class Count:

    def __init__(self, before, first, per):
        self.before, self.first, self.per = before, first, per

    def at(self, it, n):
        if isinstance(it, int) and it == 0:
            return self.before + n
        return it * self.per + (self.before + self.first - self.per + n)


def schedule(cross, first, last):
    slots = [[("Q", 1), ("K", 1)],
             [("V", 0, 0), ("V", 1, 0)],
             [("Q", 2), ("K", 2)],
             [],
             [("Q", 3), ("K", 3)],
             [("V", 0, 1), ("V", 1, 1)],
             [("Q", 0), ("K", 0)],
             []]
    if not first:
        slots[OUT_SLOT] += [("OUT", 0), ("OUT", 1)] if cross else [("OUT", None)]
    if not last:
        slots[5] += [("XT", 0)] + ([("XT", 1)] if cross else [])
    if last:
        slots[6] = []
    return slots


def banked(cross, slots):
    full = [j for s in schedule(cross, False, False) for j in s]
    return [[(j, full.index(j) % 2) for j in s] for s in slots]


def hi_ops(job):
    return {"K": 2, "OUT": 0}.get(job[0], 1)


def attention_stage(nc, ctx, tag, cross, x_dram, kv_dram, w_sb, mask, ident, ident16, psum, sb_of, y_drams, w_ready,
                    each_pass_sync=None, each_pass_vector=None):
    NIT = x_dram.shape[0] // PAIR
    D = x_dram.shape[2]
    KT = D // P
    full = [j for s in schedule(cross, False, False) for j in s]
    JOBS = len(full)
    OUTS = len([j for j in full if j[0] == "OUT"])
    PRE = [("XT", 0)] + ([("XT", 1)] if cross else []) + [("Q", 0), ("K", 0)]
    HIS = sum(map(hi_ops, full))

    def sem(name):
        return ctx.enter_context(nc.semaphore(f"{tag}_{name}"))

    x_in, kv_in, res_in = sem("x_in"), sem("kv_in"), sem("res_in")
    job_mm, job_hi, job_free = sem("job_mm"), sem("job_hi"), sem("job_free")
    scores_ready, max_ready, exp_done = sem("scores_ready"), sem("max_ready"), sem("exp_done")
    recip_ready, probs_ready = sem("recip_ready"), sem("probs_ready")
    tr_done, pt_hi_done, pt_lo_done = sem("tr_done"), sem("pt_hi_done"), sem("pt_lo_done")
    pv_done, o_hi_done, o_lo_done = sem("pv_done"), sem("o_hi_done"), sem("o_lo_done")
    var_ready, stats_ready, moments_ready, rstd_ready, y_ready, y_stored = (
        sem("var_ready"), sem("stats_ready"), sem("moments_ready"), sem("rstd_ready"), sem("y_ready"), sem("y_stored"))

    C_job = Count(len(PRE), JOBS - OUTS, JOBS)
    C_hi = Count(sum(map(hi_ops, PRE)), HIS, HIS)
    C_unit = Count(0, UNITS, UNITS)

    T = sb_of
    wq_hi, wq_lo, wk_hi, wk_lo, wv_hi, wv_lo, wo_hi, wo_lo = w_sb
    job_bank, S, PT, OT = psum

    x_pairs = x_dram.rearrange("(i b) p d -> i p b d", b=PAIR)
    kv_pairs = kv_dram.rearrange("(i b) p d -> i p b d", b=PAIR)
    y_pairs = [y.rearrange("(i b) p d -> i p b d", b=PAIR) for y in y_drams]
    STORED = 16 * len(y_pairs)
    xT = [(T["xT_hi"], T["xT_lo"])]
    xT.append((T["cT_hi"], T["cT_lo"]) if cross else xT[0])
    raw = [T["x_raw"], T["c_raw"]]
    raw_in = [x_in, kv_in]

    def passes(emit, epilogue, eng):
        emit(0, True, False)
        with eng.Fori(1, NIT - 1) as it:
            emit(it, False, False)
        emit(NIT - 1, False, True)
        epilogue()

    def lagged(it, k, lag, first):
        if k >= lag:
            return [(it, k - lag)]
        return [] if first else [(it - 1, k - lag + UNITS)]

    def numbered(first, last):
        n, out = 0, []
        for s in banked(cross, schedule(cross, first, last)):
            row = []
            for job, bank in s:
                row.append((n, job, bank))
                n += 1
            out.append(row)
        return out

    def bank_history(first, last):
        pre = [(j, full.index(j) % 2) for j in PRE]
        seen = {}
        for k, (j, b) in enumerate(pre):
            seen[b] = k - len(pre)
        before = {}
        for row in numbered(first, last):
            for n, job, b in row:
                before[n] = seen[b]
                seen[b] = n
        return before

    def sync_program(sp):
        def xt_jobs(i, first):
            return C_job.at(i, [n for row in numbered(first, False) for n, j, _ in row if j[0] == "XT"][-1] + 1)

        def load_x(i):
            sp.dma_start(raw[0][:, :, :], x_pairs[i]).then_inc(x_in, 16)
            if cross:
                sp.dma_start(raw[1][:, :, :], kv_pairs[i]).then_inc(kv_in, 16)

        def store_y_load_res(i):
            sp.wait_ge(y_ready, i * PAIR)
            for y in y_pairs:
                sp.dma_start(y[i - 1], T["y_out"][:, :, :]).then_inc(y_stored, 16)
            sp.wait_ge(y_stored, i * STORED)
            sp.dma_start(T["x_res"][:, :, :], x_pairs[i]).then_inc(res_in, 16)

        def also(i):
            if each_pass_sync is not None:
                each_pass_sync(sp, i)

        load_x(0)
        sp.dma_start(T["x_res"][:, :, :], x_pairs[0]).then_inc(res_in, 16)
        sp.wait_ge(job_mm, len(PRE) - 2)
        load_x(1)
        sp.wait_ge(job_mm, xt_jobs(0, True))
        load_x(2)
        also(0)
        store_y_load_res(1)
        also(1)
        with sp.Fori(2, NIT - 1) as i:
            sp.wait_ge(job_mm, xt_jobs(i - 1, False))
            load_x(i + 1)
            store_y_load_res(i)
            also(i)
        store_y_load_res(NIT - 1)
        also(NIT - 1)
        sp.wait_ge(y_ready, NIT * PAIR)
        for y in y_pairs:
            sp.dma_start(y[NIT - 1], T["y_out"][:, :, :]).then_inc(y_stored, 16)
        sp.wait_ge(y_stored, NIT * STORED)

    def tensor_program(pe):
        weight_of = {("Q", 0): 1, ("K", 0): 2, ("V", 0, 0): 3, [j for j in full if j[0] == "OUT"][0]: 4}

        def job_matmuls(job, bank, it, xt_of):
            ps = job_bank[bank]
            kind = job[0]
            if job in weight_of:
                pe.wait_ge(w_ready[0], w_ready[1] + weight_of.pop(job))
            if kind == "XT":
                src, n = job[1], xt_of
                pe.wait_ge(raw_in[src], 16 * n + 16)
                for k in range(KT):
                    for b in range(PAIR):
                        mm = pe.transpose(ps[:, (k * PAIR + b) * P:(k * PAIR + b + 1) * P],
                                          raw[src][:, b, k * P:(k + 1) * P], ident[:, :])
                return mm
            if kind in "QK":
                g = job[1]
                w_hi, w_lo = (wq_hi, wq_lo) if kind == "Q" else (wk_hi, wk_lo)
                t_hi, t_lo = xT[0] if kind == "Q" else xT[1]
                for c in range(CHUNKS):
                    cols = slice((g * CHUNKS + c) * P, (g * CHUNKS + c + 1) * P)
                    n = 0
                    for k in range(KT):
                        for w, t in terms(w_hi, w_lo, t_hi, t_lo):
                            mm = pe.matmul(ps[:, c * PAIR * P:(c + 1) * PAIR * P], w[:, k, cols], t[:, k, :],
                                           start=(n == 0), stop=(n == 3 * KT - 1))
                            n += 1
                return mm
            if kind == "V":
                _, b, half = job
                t_hi, t_lo = xT[1]
                n = 0
                for k in range(KT):
                    for t, w in terms(t_hi, t_lo, wv_hi, wv_lo):
                        mm = pe.matmul(ps[:, :], t[:, k, b * P:(b + 1) * P], w[:, k, half * 512:(half + 1) * 512],
                                       start=(n == 0), stop=(n == 3 * KT - 1))
                        n += 1
                return mm
            bs = range(PAIR) if job[1] is None else [job[1]]
            NC = GROUPS * CHUNKS
            for at, b in enumerate(bs):
                n = 0
                for c in range(NC):
                    for o, w in terms(T["oT_hi"], T["oT_lo"], wo_hi, wo_lo):
                        mm = pe.matmul(ps[:, at * D:(at + 1) * D], o[:, c, b, :], w[:, c, :],
                                       start=(n == 0), stop=(n == 3 * NC - 1))
                        n += 1
            return mm

        def qk(it, k):
            g, b = divmod(k, PAIR)
            n_k = K_jobs(it)[g]
            if b == 0:
                pe.wait_ge(job_free, n_k)
            if not (isinstance(it, int) and it == 0 and k < 2):
                pe.wait_ge(exp_done, C_unit.at(it, k - 1))
            for c in range(CHUNKS):
                out = S[k % 2][:, c * 2 * P:(c + 1) * 2 * P]
                n = 0
                for q, kk in terms(T["qT_hi"], T["qT_lo"], T["kT_hi"], T["kT_lo"]):
                    mm = pe.matmul(out, q[:, g % 2, c, b, :],
                                   kk[:, g % 2, c, b, :, :].rearrange("p h t -> p (h t)"),
                                   start=(n == 0), stop=(n == 2 and cross))
                    n += 1
                if not cross:
                    mm = pe.matmul(out, ident16[:, :], mask[:, :], start=False, stop=True)
            mm.then_inc(scores_ready, 1)

        def K_jobs(it):
            first, last = (isinstance(it, int) and it == 0), (isinstance(it, int) and it == NIT - 1)
            out = {0: C_job.at(it, 0)}
            for row in numbered(first, last):
                for n, j, _ in row:
                    if j[0] == "K" and j[1]:
                        out[j[1]] = C_job.at(it, n + 1)
            return out

        def transposes(it, k):
            pe.wait_ge(probs_ready, C_unit.at(it, k + 1))
            if not (isinstance(it, int) and it == 0 and k < 2):
                pe.wait_ge(pt_lo_done, C_unit.at(it, k - 1))
            for h in range(UNIT_HEADS):
                mm = pe.transpose(PT[k % 2][:, h * P:(h + 1) * P], T["probs"][:, k % RING, h, :], ident[:, :])
            mm.then_inc(tr_done, 1)

        def pv(it, k):
            g, b = divmod(k % UNITS, PAIR)
            pe.wait_ge(pt_lo_done, C_unit.at(it, k + 1))
            if not (isinstance(it, int) and it == 0 and k < 2):
                pe.wait_ge(o_lo_done, C_unit.at(it, k - 1))
            if k in (0, 1, UNITS // 2, UNITS // 2 + 1):
                first, last = (isinstance(it, int) and it == 0), (isinstance(it, int) and it == NIT - 1)
                n = [n for row in numbered(first, last) for n, j, _ in row
                     if j == ("V", b, k // (UNITS // 2))][0]
                pe.wait_ge(job_free, C_job.at(it, n + 1))
            for c in range(CHUNKS):
                cols = slice((g * CHUNKS + c) * P, (g * CHUNKS + c + 1) * P)
                n = 0
                for v, p in terms(T["v_hi"], T["v_lo"], T["pT_hi"], T["pT_lo"]):
                    mm = pe.matmul(OT[k % 2][:, c * 2 * P:(c + 1) * 2 * P], v[:, b, cols],
                                   p[:, k % 2, 2 * c:2 * c + 2, :].rearrange("p h t -> p (h t)"),
                                   start=(n == 0), stop=(n == 2))
                    n += 1
            mm.then_inc(pv_done, 1)

        def run_job(it, n, job, bank, before, pre_xt=None):
            if before is not None:
                pe.wait_ge(job_free, C_job.at(it, before + 1))
            if job[0] == "OUT":
                pe.wait_ge(o_lo_done, C_unit.at(it, 0))
            if job == ("Q", 0):
                pe.wait_ge(job_free, C_job.at(it, n))
            xt = None
            if job[0] == "XT":
                xt = 0 if pre_xt is not None else it + 1
            job_matmuls(job, bank, it, xt).then_inc(job_mm, 1)

        hist = {}
        for k, job in enumerate(PRE):
            bank = full.index(job) % 2
            if bank in hist:
                pe.wait_ge(job_free, hist[bank] + 1)
            if job == ("Q", 0):
                pe.wait_ge(job_free, k)
            hist[bank] = k
            job_matmuls(job, bank, 0, 0).then_inc(job_mm, 1)

        def one_pass(it, first, last):
            before = bank_history(first, last)
            for k, row in enumerate(numbered(first, last)):
                qk(it, k)
                outs = [r for r in row if r[1][0] == "OUT"]
                for n, job, bank in row:
                    if job[0] != "OUT":
                        run_job(it, n, job, bank, before[n])
                for u in lagged(it, k, 2, first):
                    transposes(*u)
                for n, job, bank in outs:
                    run_job(it, n, job, bank, before[n])
                for u in lagged(it, k, 3, first):
                    pv(*u)

        def finish():
            last = NIT - 1
            transposes(last, UNITS - 2)
            pv(last, UNITS - 3)
            transposes(last, UNITS - 1)
            pv(last, UNITS - 2)
            pv(last, UNITS - 1)
            done = C_job.at(last, JOBS - len(PRE))
            for k, j in enumerate([j for j in full if j[0] == "OUT"]):
                pe.wait_ge(job_free, done + min(k, 0))
                pe.wait_ge(o_lo_done, UNITS * NIT)
                job_matmuls(j, full.index(j) % 2, last, None).then_inc(job_mm, 1)

        passes(one_pass, finish, pe)

    def k_views(ps, half):
        rows = slice(half * DH, (half + 1) * DH)
        return rows, ps[rows, :].rearrange("p (c t) -> p c t", t=P)

    def job_dst(job):
        kind = job[0]
        if kind == "XT":
            hi, lo = xT[job[1]]
            return hi[:, :, :].rearrange("p k t -> p (k t)"), lo[:, :, :].rearrange("p k t -> p (k t)")
        if kind == "Q":
            return [t[:, job[1] % 2, :, :, :].rearrange("p c b t -> p (c b t)") for t in (T["qT_hi"], T["qT_lo"])]
        if kind == "V":
            _, b, half = job
            return [t[:, b, half * 512:(half + 1) * 512] for t in (T["v_hi"], T["v_lo"])]
        g = job[1]
        return [[t[h * DH:(h + 1) * DH, g % 2, :, :, h, :].rearrange("p c b t -> p (c b) t") for h in range(2)]
                for t in (T["kT_hi"], T["kT_lo"])]

    def scalar_program(act):
        def job_part(job, bank, number, it):
            if job[0] == "OUT":
                return
            act.wait_ge(job_mm, number)
            ps = job_bank[bank]
            hi = job_dst(job)[0]
            if job[0] == "K":
                for h in range(2):
                    rows, src = k_views(ps, h)
                    act.activation(hi[h], src, ACT.Copy).then_inc(job_hi, 1)
            else:
                act.activation(hi, ps[:, :], ACT.Copy).then_inc(job_hi, 1)

        def exp(it, k):
            act.wait_ge(max_ready, C_unit.at(it, k + 1))
            if not (isinstance(it, int) and it == 0 and k < RING):
                act.wait_ge(tr_done, C_unit.at(it, k - RING + 1))
            for h in range(UNIT_HEADS):
                a = act.activation(T["probs"][:, k % RING, h, :], S[k % 2][:, h * P:(h + 1) * P], ACT.Exp,
                                   bias=T["neg_max"][:, k % RING, h:h + 1],
                                   accum_out=T["row_sum"][:, k % RING, h:h + 1])
            a.then_inc(exp_done, 1)

        def pt_hi(it, k):
            act.wait_ge(tr_done, C_unit.at(it, k + 1))
            if not (isinstance(it, int) and it == 0 and k < 2):
                act.wait_ge(pv_done, C_unit.at(it, k - 1))
            act.activation(T["pT_hi"][:, k % 2, :, :].rearrange("p h t -> p (h t)"), PT[k % 2][:, :],
                           ACT.Copy).then_inc(pt_hi_done, 1)

        def o_hi(it, k):
            g, b = divmod(k, PAIR)
            act.wait_ge(pv_done, C_unit.at(it, k + 1))
            src = OT[k % 2][:, :].rearrange("p (c h t) -> p c h t", c=CHUNKS, h=2)
            for h in range(2):
                rows = slice(h * DH, (h + 1) * DH)
                act.activation(T["oT_hi"][rows, g * CHUNKS:(g + 1) * CHUNKS, b, :], src[rows, :, h, :],
                               ACT.Copy).then_inc(o_hi_done, 1)

        for k, job in enumerate(PRE):
            job_part(job, full.index(job) % 2, k + 1, 0)

        def one_pass(it, first, last):
            for k, row in enumerate(numbered(first, last)):
                for u in lagged(it, k, 1, first):
                    exp(*u)
                for u in lagged(it, k, 4, first):
                    o_hi(*u)
                for n, job, bank in row:
                    job_part(job, bank, C_job.at(it, n + 1), it)
                for u in lagged(it, k, 2, first):
                    pt_hi(*u)

        def finish():
            last = NIT - 1
            exp(last, UNITS - 1)
            o_hi(last, UNITS - 4)
            pt_hi(last, UNITS - 2)
            o_hi(last, UNITS - 3)
            pt_hi(last, UNITS - 1)
            o_hi(last, UNITS - 2)
            o_hi(last, UNITS - 1)

        passes(one_pass, finish, act)

    def vector_program(dve):
        def job_lo(job, bank, his):
            ps = job_bank[bank]
            dve.wait_ge(job_hi, his)
            hi, lo = job_dst(job)
            if job[0] == "K":
                for h in range(2):
                    rows, src = k_views(ps, h)
                    v = dve.tensor_tensor(lo[h], src, hi[h].bitcast(F32), ALU.subtract)
                v.then_inc(job_free, 1)
            else:
                dve.tensor_tensor(lo, ps[:, :], hi.bitcast(F32), ALU.subtract).then_inc(job_free, 1)

        def out_part(job, bank, jobs_done, pair):
            bs = list(range(PAIR)) if job[1] is None else [job[1]]
            dve.wait_ge(job_mm, jobs_done)
            dve.wait_ge(res_in, 16 * pair + 16)
            dve.tensor_tensor(T["y_sum"][:, bs[0]:bs[-1] + 1, :],
                              job_bank[bank][:, 0:len(bs) * D].rearrange("p (b d) -> p b d", d=D),
                              T["x_res"][:, bs[0]:bs[-1] + 1, :], ALU.add).then_inc(job_free, 1)

        def row_stats():
            for b in range(PAIR):
                dve.bn_stats(T["bn"][:, b, :], T["y_sum"][:, b, :]).then_inc(stats_ready, 1)

        def moments():
            for b in range(PAIR):
                dve.bn_aggr(T["mv"][:, b, :], T["bn"][:, b, :]).then_inc(moments_ready, 1)

        def normalise(pair):
            dve.wait_ge(rstd_ready, pair + 1)
            for b in range(PAIR):
                dve.tensor_scalar(T["y_out"][:, b, :], T["y_sum"][:, b, :], T["mv"][:, b, 0:1], T["rstd"][:, b:b + 1],
                                  ALU.subtract, ALU.mult).then_inc(y_ready, 1)

        def neg_max(it, k):
            dve.wait_ge(scores_ready, C_unit.at(it, k + 1))
            dve.tensor_reduce(T["neg_max"][:, k % RING, :], S[k % 2][:, :].rearrange("p (h t) -> p h t", t=P),
                              AX.X, ALU.max, negate=True).then_inc(max_ready, 1)

        def recip(it, k):
            dve.wait_ge(exp_done, C_unit.at(it, k + 1))
            if not (isinstance(it, int) and it == 0 and k < RING):
                dve.wait_ge(probs_ready, C_unit.at(it, k - RING + 1))
            dve.reciprocal(T["row_inv"][:, k % RING, :], T["row_sum"][:, k % RING, :]).then_inc(recip_ready, 1)

        def pt_lo(it, k):
            dve.wait_ge(pt_hi_done, C_unit.at(it, k + 1))
            dve.tensor_tensor(T["pT_lo"][:, k % 2, :, :].rearrange("p h t -> p (h t)"), PT[k % 2][:, :],
                              T["pT_hi"][:, k % 2, :, :].rearrange("p h t -> p (h t)").bitcast(F32),
                              ALU.subtract).then_inc(pt_lo_done, 1)

        def o_lo(it, k):
            g, b = divmod(k, PAIR)
            dve.wait_ge(o_hi_done, C_unit.at(it, k + 1) * 2)
            src = OT[k % 2][:, :].rearrange("p (c h t) -> p c h t", c=CHUNKS, h=2)
            for h in range(2):
                rows = slice(h * DH, (h + 1) * DH)
                v = dve.tensor_tensor(T["oT_lo"][rows, g * CHUNKS:(g + 1) * CHUNKS, b, :], src[rows, :, h, :],
                                      T["oT_hi"][rows, g * CHUNKS:(g + 1) * CHUNKS, b, :].bitcast(F32), ALU.subtract)
            v.then_inc(o_lo_done, 1)

        his = 0
        for k, job in enumerate(PRE):
            his += hi_ops(job)
            job_lo(job, full.index(job) % 2, his)

        def one_pass(it, first, last):
            his = 0
            for k, row in enumerate(numbered(first, last)):
                if k == OUT_SLOT + 1 and not first:
                    dve.wait_ge(stats_ready, it * PAIR)
                neg_max(it, k)
                if k == OUT_SLOT + 1 and not first:
                    moments()
                for u in lagged(it, k, 1, first):
                    recip(*u)
                for u in lagged(it, k, 4, first):
                    o_lo(*u)
                for n, job, bank in row:
                    his += hi_ops(job)
                    if job[0] != "OUT":
                        job_lo(job, bank, C_hi.at(it, his))
                for u in lagged(it, k, 2, first):
                    pt_lo(*u)
                if k == UNITS - 1 and each_pass_vector is not None:
                    each_pass_vector(dve, it)
                outs = [r for r in row if r[1][0] == "OUT"]
                for n, job, bank in outs:
                    out_part(job, bank, C_job.at(it, n + 1), it - 1)
                if outs:
                    ln_start(it)
                    row_stats()
                if k == NORM_SLOT and not first:
                    normalise(it - 1)

        def ln_start(it):
            dve.wait_ge(job_free, ln_count(it))

        def ln_count(it):
            first, last = False, (isinstance(it, int) and it == NIT - 1)
            n = [n for row in numbered(first, last) for n, j, _ in row if j[0] == "OUT"][-1]
            return C_job.at(it, n + 1)

        def finish():
            last = NIT - 1
            recip(last, UNITS - 1)
            o_lo(last, UNITS - 4)
            pt_lo(last, UNITS - 2)
            o_lo(last, UNITS - 3)
            pt_lo(last, UNITS - 1)
            o_lo(last, UNITS - 2)
            o_lo(last, UNITS - 1)
            done = C_job.at(last, JOBS - len(PRE))
            for k, j in enumerate([j for j in full if j[0] == "OUT"]):
                out_part(j, full.index(j) % 2, done + k + 1, last)
            dve.wait_ge(job_free, done + OUTS)
            row_stats()
            dve.wait_ge(stats_ready, NIT * PAIR)
            moments()
            normalise(last)

        passes(one_pass, finish, dve)

    def gpsimd_program(pool):
        def normalise_probs(it, k):
            pool.wait_ge(recip_ready, C_unit.at(it, k + 1))
            p = T["probs"][:, k % RING, :, :]
            pool.tensor_tensor(p, p, T["row_inv"][:, k % RING, :].unsqueeze(2).to_broadcast([P, UNIT_HEADS, P]),
                               ALU.mult).then_inc(probs_ready, 1)

        def rstd(pair):
            pool.wait_ge(moments_ready, pair * PAIR + PAIR)
            pool.tensor_tensor(T["var_eps"][:, :], T["mv"][:, :, 1], T["eps"][:, :], ALU.add).then_inc(var_ready, 1)
            pool.wait_ge(var_ready, pair + 1)
            pool.tensor_tensor(T["rstd"][:, :], T["var_eps"][:, :], T["minus_half"][:, :], ALU.pow)\
                .then_inc(rstd_ready, 1)

        def one_pass(it, first, last):
            for k in range(UNITS):
                for u in lagged(it, k, 1, first):
                    normalise_probs(*u)
                if k == NORM_SLOT - 1 and not first:
                    rstd(it - 1)

        def finish():
            normalise_probs(NIT - 1, UNITS - 1)
            rstd(NIT - 1)

        passes(one_pass, finish, pool)

    finals = {"pe": (job_mm, C_job.at(NIT - 1, JOBS - len(PRE)) + OUTS),
              "dve": (job_free, C_job.at(NIT - 1, JOBS - len(PRE)) + OUTS)}
    return sync_program, tensor_program, scalar_program, vector_program, gpsimd_program, finals


WEIGHT_NAMES = ("wq", "wk", "wv", "wo")
X_SCALE = 256.0
W_TOP = 2.0 ** -13
TINY = 2.0 ** -100


def build(nc, args, out):
    (x, ctxt, a_wq, a_wk, a_wv, a_wo, c_wq, c_wk, c_wv, c_wo, router, w_gate, w_up, w_down) = args
    B, S, D = x.shape
    KT = D // P
    E = HEADS * DH
    NX, _, F = w_gate.shape
    FT = F // P
    TOK = B * S
    NT = TOK // P
    TILES = (2 * TOK) // P + NX - 1
    AHEAD = 4
    META = 2
    H16 = mybir.dt.float16
    I32 = mybir.dt.int32
    assert B // PAIR == NX and P == S

    x1 = nc.dram_tensor("x1_scratch", (B, S, D), F32).ap()
    x2 = nc.dram_tensor("x2_scratch", (TOK + P, D), F32).ap()
    acc = nc.dram_tensor("acc_scratch", (TOK + P, D), F32).ap()
    slots = nc.dram_tensor("slots_scratch", (TILES * P, META), F32).ap()

    with ExitStack() as ctx:
        def sb(name, shape, dt=F32, stack=ctx):
            return stack.enter_context(nc.sbuf_tensor(name, shape, dt))

        def sem(name):
            return ctx.enter_context(nc.semaphore(name))

        T = {}
        for n in ("x_raw", "c_raw", "x_res", "y_sum", "y_out"):
            T[n] = sb(n, [P, PAIR, D])
        T["neg_max"] = sb("neg_max", [P, RING, UNIT_HEADS])
        T["row_sum"] = sb("row_sum", [P, RING, UNIT_HEADS])
        T["row_inv"] = sb("row_inv", [P, RING, UNIT_HEADS])
        T["bn"] = sb("bn", [P, PAIR, 6])
        T["mv"] = sb("mv", [P, PAIR, 2])
        for n in ("rstd", "var_eps", "minus_half", "eps"):
            T[n] = sb(n, [P, PAIR])
        ident = sb("ident", [P, P])
        ident16 = sb("ident16", [P, P], BF16)
        mask = sb("mask", [P, 2 * P], BF16)
        absmax = sb("absmax", [P, NX, 2])

        def table(name, *shape, dt=F32, stack=ctx):
            return sb(name, [P, *shape], dt, stack)

        wr = table("router_w", KT, NX)
        e_of = table("e_of", NX)
        tie = table("tie", NX)
        below = table("below", NX, NX)
        edges = table("edges", NT)
        tile_no = table("tile_no", TILES)
        earlier = table("earlier", P, dt=BF16)
        ones16 = table("ones16", P, dt=BF16)
        zero_row = table("zero_row", D)
        unused = table("unused_slots", TILES, META)
        meta = [table(f"meta{i}", NT, META) for i in range(2)]
        slot = table("slot_meta", TILES + 1, META)
        col, col2, p1, p2, wt1, wt2 = (table(n, NT) for n in ("col", "col2", "p1", "p2", "wt1", "wt2"))
        ntok, tiles_e, cum0, cum1, end_e = (table(n, NX) for n in ("ntok", "tiles_e", "cum0", "cum1", "end_e"))
        cmp16 = table("cmp16", NX, NT)
        cmp8 = table("cmp8", NX, NX)
        slot_f = [table(f"slot_f{i}", NT) for i in range(2)]
        slot_i = [table(f"slot_i{i}", NT, dt=I32) for i in range(2)]
        expert_f = table("expert_f", TILES)
        expert_i = table("expert_i", TILES, dt=I32)
        get_tok = [table(f"get_tok{i}", 1, dt=I32) for i in range(AHEAD)]
        put_tok = [table(f"put_tok{i}", 1, dt=I32) for i in range(2)]
        row_w = [table(f"row_w{i}", 1) for i in range(2)]
        wmax, wall, w_exp, w_inv, w_scale, act_inv = (table(n, 2) for n in (
            "wmax", "wall", "w_exp", "w_inv", "w_scale", "act_inv"))
        fbn, fmv = table("fbn", 4, 6), table("fmv", 4, 2)
        fvar, frstd, f_half = table("fvar", 4), table("frstd", 4), table("f_half", 4)

        att = ExitStack()
        for n in ("xT", "cT"):
            for part in ("hi", "lo"):
                T[f"{n}_{part}"] = sb(f"{n}_{part}", [P, KT, PAIR * P], F32R, att)
        for part in ("hi", "lo"):
            T[f"qT_{part}"] = sb(f"qT_{part}", [P, 2, CHUNKS, PAIR, P], F32R, att)
            T[f"kT_{part}"] = sb(f"kT_{part}", [P, 2, CHUNKS, PAIR, 2, P], F32R, att)
            T[f"v_{part}"] = sb(f"v_{part}", [P, PAIR, E], F32R, att)
            T[f"pT_{part}"] = sb(f"pT_{part}", [P, 2, UNIT_HEADS, P], F32R, att)
            T[f"oT_{part}"] = sb(f"oT_{part}", [P, E // P, PAIR, P], F32R, att)
        T["probs"] = sb("probs", [P, RING, UNIT_HEADS, P], F32, att)
        raw_w = [sb(f"raw_{n}", [P, KT * E], F32, att) for n in WEIGHT_NAMES]
        w_sb = []
        for n, (a, b) in zip(WEIGHT_NAMES, [(KT, E)] * 3 + [(E // P, D)]):
            w_sb += [sb(f"{n}_hi", [P, a, b], F32R, att), sb(f"{n}_lo", [P, a, b], F32R, att)]
        scan_w = sb("scan_w", [P, 2, KT, F], F32, att)
        att.close()

        wg = [sb(f"wg_{part}", [P, NX, KT, F], H16) for part in ("hi", "lo")]
        wu = [sb(f"wu_{part}", [P, NX, KT, F], H16) for part in ("hi", "lo")]
        wd = [sb(f"wd_{part}", [P, NX, FT, D], F32R) for part in ("hi", "lo")]
        raw_x = [[sb(f"raw_expert{i}_{n}", [P, KT * F]) for n in ("gate", "up", "down")] for i in range(2)]
        late = ExitStack()
        rows2 = sb("rows2", [P, NT, D], F32, late)
        x2T = [sb(f"x2T{i}", [P, KT, 512], F32, late) for i in range(2)]
        logT = sb("logits_T", [NX, TOK], F32, late)
        lg, pr, sub, one1, one2, tmp8, tmp8b = (table(n, NT, NX, stack=late) for n in (
            "lg", "pr", "sub", "one1", "one2", "tmp8", "tmp8b"))
        both16 = table("both16", NT, NX, dt=BF16, stack=late)
        pad = [table(f"pad{i}", NT // 2 + NT, NX, stack=late) for i in range(2)]
        mine, mine2 = (t[:, :, :].rearrange("p k t -> p (k t)")[:, 0:TILES * NX].rearrange("p (j e) -> p j e", e=NX)
                       for t in x2T)
        late.close()
        xrow = [sb(f"xrow{i}", [P, D]) for i in range(AHEAD)]
        xt16 = [[sb(f"xt16_{part}{i}", [P, KT, P], H16) for part in ("hi", "lo")] for i in range(2)]
        gated = sb("gated", [P, F])
        hid = [sb(f"hidden{i}", [P, F]) for i in range(2)]
        hidT = [sb(f"hiddenT_{part}", [P, FT, P], F32R) for part in ("hi", "lo")]
        yrow = [sb(f"yrow{i}", [P, D]) for i in range(2)]
        fin_in, fin_out = ([raw_x[i][n][:, :].rearrange("p (t d) -> p t d", d=D) for i in range(2)] for n in range(2))

        psum = [[ctx.enter_context(nc.psum_tensor(f"{n}{i}", [P, 512], F32)) for i in range(2)]
                for n in ("job", "scores", "probsT", "outT")]
        xt_ps, g_ps, u_ps, (ht_ps, y_ps) = psum

        w_in = [[sem(f"{tag}_{n}_in") for n in WEIGHT_NAMES] for tag in ("self", "cross")]
        w_hi_done, w_ready = sem("w_hi_done"), sem("w_ready")
        consts, zeroed, k_zeroed = sem("consts"), sem("zeroed"), sem("k_zeroed")
        tables, tables_pool = sem("tables"), sem("tables_pool")
        scan_in, scan_done, max_all, scale_ready = sem("scan_in"), sem("scan_done"), sem("max_all"), sem("scale_ready")
        wr_in, rows_in = sem("wr_in"), sem("rows_in")
        raw_in = [sem("raw_in_even"), sem("raw_in_odd")]
        raw_hi, raw_lo = sem("raw_hi"), sem("raw_lo")
        x2T_mm, x2T_sb, log_mm, log_sb, logits_mm = (
            sem("x2T_mm"), sem("x2T_sb"), sem("log_mm"), sem("log_sb"), sem("logits_mm"))
        chain, exp1_in, exp1, exp2_in, exp2 = sem("chain"), sem("exp1_in"), sem("exp1"), sem("exp2_in"), sem("exp2")
        picked, ranks, slots_ready, plan_ready = sem("picked"), sem("ranks"), sem("slots_ready"), sem("plan_ready")
        unused_out, dispatched, slots_in = sem("unused_out"), sem("dispatched"), sem("slots_in")
        get_ready, put_ready, w_kept, pool_step = sem("get_ready"), sem("put_ready"), sem("w_kept"), sem("pool_step")
        xt_mm, xt_hi, xt_lo = sem("xt_mm"), sem("xt_hi"), sem("xt_lo")
        x_gathered = [sem(f"x_gathered{i}") for i in range(AHEAD)]
        g_mm, u_mm, silu_done, hid_done, ht_mm, ht_hi, ht_lo = (
            sem("g_mm"), sem("u_mm"), sem("silu_done"), sem("hid_done"), sem("ht_mm"), sem("ht_hi"), sem("ht_lo"))
        y_mm, y_sb, y_added = sem("y_mm"), sem("y_sb"), sem("y_added")
        f_in, f_stats, f_mom, f_var, f_rstd, f_done, f_out = (
            sem("f_in"), sem("f_stats"), sem("f_mom"), sem("f_var"), sem("f_rstd"), sem("f_done"), sem("f_out"))

        def scan_load(sp, i):
            if not (isinstance(i, int) and i == 0):
                sp.wait_ge(scan_done, i)
            for n, w in enumerate((w_gate, w_up)):
                sp.dma_start(scan_w[:, n, :, :], w[i].rearrange("(k p) f -> p k f", p=P)).then_inc(scan_in, 16)

        def scan_max(dve, i):
            dve.wait_ge(scan_in, 32 * i + 32)
            dve.wait_ge(k_zeroed, 2)
            dve.tensor_reduce(absmax[:, i, :] if isinstance(i, int) else
                              absmax[:, bass.ds(i, 1), :].rearrange("p a b -> p (a b)"),
                              scan_w[:, :, :, :].rearrange("p n k f -> p n (k f)"), AX.X, ALU.max,
                              apply_absolute_value=True).then_inc(scan_done, 1)

        self_att = attention_stage(nc, ctx, "self", False, x, x, w_sb, mask, ident, ident16, psum, T, [x1],
                                   (w_ready, 0), scan_load, scan_max)
        cross_att = attention_stage(nc, ctx, "cross", True, x1, ctxt, w_sb, mask, ident, ident16, psum, T,
                                    [t[0:TOK, :].rearrange("(b p) d -> b p d", p=S) for t in (x2, acc)],
                                    (w_ready, 4))
        pe_end_self, pe_end_cross = self_att[5]["pe"], cross_att[5]["pe"]

        def load_weights(eng, ws, w_in):
            for n, w in enumerate(ws):
                k = KT if n < 3 else E // P
                eng.dma_start(raw_w[n][:, :].rearrange("p (k n) -> p k n", k=k),
                              w.rearrange("(k p) n -> p k n", p=P)).then_inc(w_in[n], 16)

        def flat(t):
            return t[:, :, :].rearrange("p k n -> p (k n)")

        def split_hi(act, stage):
            for n in range(4):
                act.wait_ge(w_in[stage][n], 16)
                act.activation(flat(w_sb[2 * n]), raw_w[n][:, :], ACT.Copy,
                               scale=DH ** -0.5 if n == 0 else 1.0).then_inc(w_hi_done, 1)

        def split_lo(dve, stage, n):
            dve.wait_ge(w_hi_done, stage * 4 + n + 1)
            dve.scalar_tensor_tensor(flat(w_sb[2 * n + 1]), raw_w[n][:, :], DH ** -0.5 if n == 0 else 1.0,
                                     flat(w_sb[2 * n]).bitcast(F32), ALU.mult, ALU.subtract).then_inc(w_ready, 1)

        def experts2(t, e):
            return t[:, e, :, :].rearrange("p k n -> p (k n)")

        TOK_CHUNK = 512
        NCH = TOK // TOK_CHUNK
        CT = TOK_CHUNK // P
        SPLIT_FIRST = 3
        LOOP = TILES // AHEAD

        def expert_steps(eng, step):
            for j in range(AHEAD):
                step(j, j)
            with eng.Fori(1, LOOP) as m:
                for c in range(AHEAD):
                    step(m * AHEAD + c, c)
            for j in range(LOOP * AHEAD, TILES):
                step(j, j % AHEAD)

        def within(j):
            return not isinstance(j, int) or j < TILES

        def splits_at(j):
            if not isinstance(j, int) or j >= AHEAD:
                return []
            e = SPLIT_FIRST + j
            return list(range(e, NX)) if j == AHEAD - 1 else [e]
        assert LOOP * AHEAD + 1 < TILES

        block = ctx.enter_context(nc.Block())

        @block.sync
        def _(sp):
            load_weights(sp, (a_wq, a_wk, a_wv, a_wo), w_in[0])
            sp.dma_start(wr[:, :, :], router.rearrange("(k p) e -> p k e", p=P)).then_inc(wr_in, 16)
            self_att[0](sp)
            cross_att[0](sp)
            sp.wait_ge(*pe_end_cross)
            sp.dma_start(rows2[:, :, :], x2[0:TOK, :].rearrange("(t p) d -> p t d", p=P)).then_inc(rows_in, 16)
            for e in range(NX):
                if e >= 2:
                    sp.wait_ge(raw_lo, 3 * (e - 1))
                for n, w in enumerate((w_gate, w_up, w_down)):
                    k = KT if n < 2 else FT
                    sp.dma_start(raw_x[e % 2][n][:, :].rearrange("p (k f) -> p k f", k=k),
                                 w[e].rearrange("(k p) f -> p k f", p=P)).then_inc(raw_in[e % 2], 16)
            sp.wait_ge(y_added, 16 * TILES)
            fin_src = acc[0:TOK, :].rearrange("(c t p) d -> c p t d", p=P, t=4)
            fin_dst = out.rearrange("b p d -> (b p) d").rearrange("(c t p) d -> c p t d", p=P, t=4)
            NC = NT // 4
            for c in range(NC + 1):
                if c < NC:
                    if c >= 2:
                        sp.wait_ge(f_done, 4 * (c - 1))
                    sp.dma_start(fin_in[c % 2][:, :, :], fin_src[c]).then_inc(f_in, 16)
                    sp.wait_ge(f_in, 16 * (c + 1))
                if c >= 1:
                    sp.wait_ge(f_done, 4 * c)
                    if c >= 2:
                        sp.wait_ge(f_out, 16 * (c - 1))
                    sp.dma_start(fin_dst[c - 1], fin_out[(c - 1) % 2][:, :, :]).then_inc(f_out, 16)
            sp.wait_ge(f_out, 16 * NC)

        @block.gpsimd
        def _(pool):
            pool.memset(ident[:, :], 0.0).then_inc(zeroed, 1)
            pool.memset(ident16[:, :], 0.0).then_inc(zeroed, 1)
            pool.memset(mask[:, :], 0.0).then_inc(zeroed, 1)
            pool.wait_ge(zeroed, 3)
            for m in (ident, ident16):
                pool.affine_select(out=m[:, :], in_=m[:, :], compare_op=ALU.not_equal, fill=1.0, base=0,
                                   pattern=[[-1, P]], channel_multiplier=1).then_inc(consts, 1)
            pool.wait_ge(consts, 2)
            n = 3
            for s in range(P // SEG):
                for r in range(P // SEG):
                    if r != s:
                        for h in range(2):
                            pool.memset(mask[s * SEG:(s + 1) * SEG, h * P + r * SEG:h * P + (r + 1) * SEG],
                                        MASKED).then_inc(zeroed, 1)
                            n += 1
                            pool.wait_ge(zeroed, n)
            both_heads = mask[:, :].rearrange("p (h t) -> p h t", t=P)
            for d in range(-(P // DIL) + 1, P // DIL):
                pool.affine_select(out=both_heads, in_=both_heads, compare_op=ALU.not_equal, fill=0.0, base=DIL * d,
                                   pattern=[[0, 2], [-1, P]], channel_multiplier=1).then_inc(zeroed, 1)
                n += 1
                pool.wait_ge(zeroed, n)
            pool.memset(T["minus_half"][:, :], -0.5).then_inc(consts, 1)
            pool.memset(T["eps"][:, :], EPS).then_inc(consts, 1)
            pool.wait_ge(consts, 4)
            pool.wait_ge(w_ready, 4)
            load_weights(pool, (c_wq, c_wk, c_wv, c_wo), w_in[1])
            n = 0
            for t, pattern, base, per_partition in (
                    (e_of[:, :], [[1, NX]], 0, 0), (tie[:, :], [[-1, NX]], NX, 0),
                    (edges[:, :], [[P, NT]], 0, 0), (tile_no[:, :], [[1, TILES]], 0, 0),
                    (unused[:, :, 1].bitcast(I32), [[0, TILES]], TOK, 1),
                    (meta[0][:, :, 1].bitcast(I32), [[P, NT]], 0, 1),
                    (meta[1][:, :, 1].bitcast(I32), [[P, NT]], 0, 1)):
                pool.iota(t, pattern, base=base, channel_multiplier=per_partition,
                          allow_small_or_imprecise_dtypes=True).then_inc(tables_pool, 1)
                n += 1
                pool.wait_ge(tables_pool, n)
            for t, v in ((below[:, :, :], 1.0), (earlier[:, :], 1.0), (ones16[:, :], 1.0), (zero_row[:, :], 0.0), (unused[:, :, 0], 0.0),
                         (f_half[:, :], -0.5)):
                pool.memset(t, v).then_inc(tables_pool, 1)
                n += 1
                pool.wait_ge(tables_pool, n)
            pool.tensor_copy(slot[:, TILES:TILES + 1, :], unused[:, 0:1, :]).then_inc(tables_pool, 1)
            n += 1
            pool.affine_select(out=below[:, :, :], in_=below[:, :, :], compare_op=ALU.is_gt, fill=0.0, base=0,
                               pattern=[[1, NX], [-1, NX]], channel_multiplier=0).then_inc(tables_pool, 1)
            pool.affine_select(out=earlier[:, :], in_=earlier[:, :], compare_op=ALU.is_gt, fill=0.0, base=0,
                               pattern=[[1, P]], channel_multiplier=-1).then_inc(tables_pool, 1)
            n += 2
            pool.wait_ge(tables_pool, n)
            pool.dma_start(slots.rearrange("(j p) c -> p j c", p=P), unused[:, :, :]).then_inc(unused_out, 16)
            pool.dma_start(x2[TOK:TOK + P, :], zero_row[:, :]).then_inc(unused_out, 16)
            pool.dma_start(acc[TOK:TOK + P, :], zero_row[:, :]).then_inc(unused_out, 16)
            pool.sem_inc(tables, 1)
            self_att[4](pool)
            pool.wait_ge(max_all, 1)
            pool.partition_all_reduce(wall[:, :], wmax[:, :], P, bass.bass_isa.ReduceOp.max).then_inc(max_all, 1)
            cross_att[4](pool)

            pool.wait_ge(unused_out, 48)
            for which in range(2):
                pool.wait_ge(slots_ready, which + 1)
                for t in range(NT):
                    pool.indirect_dma_start(out=slots, out_offset=bass.IndirectOffsetOnAxis(
                        ap=slot_i[which][:, t:t + 1], axis=0), in_=meta[which][:, t, :], in_offset=None)\
                        .then_inc(dispatched, 16)
            pool.wait_ge(dispatched, 32 * NT)
            pool.dma_start(slot[:, 0:TILES, :], slots.rearrange("(j p) c -> p j c", p=P)).then_inc(slots_in, 16)
            pool.wait_ge(slots_in, 16)
            def step():
                pool.sem_inc(pool_step, 1)

            def gather(j, c):
                if not isinstance(j, int) or j >= AHEAD:
                    pool.wait_ge(xt_mm, j - AHEAD + 1)
                pool.tensor_copy(get_tok[c][:, :], slot[:, bass.ds(j, 1), 1].bitcast(I32)).then_inc(get_ready, 1)
                pool.wait_ge(get_ready, j + 1)
                step()
                pool.indirect_dma_start(out=xrow[c][:, :], out_offset=None, in_=x2,
                                        in_offset=bass.IndirectOffsetOnAxis(ap=get_tok[c][:, :], axis=0))\
                    .then_inc(x_gathered[c], 16)

            def add_rows(j, s):
                if not isinstance(j, int) or j >= 1:
                    pool.wait_ge(y_added, 16 * j)
                pool.tensor_copy(put_tok[s][:, :], slot[:, bass.ds(j, 1), 1].bitcast(I32)).then_inc(put_ready, 1)
                pool.wait_ge(put_ready, j + 1)
                pool.wait_ge(y_sb, j + 1)
                step()
                pool.indirect_dma_start(out=acc, out_offset=bass.IndirectOffsetOnAxis(ap=put_tok[s][:, :], axis=0),
                                        in_=yrow[s][:, :], in_offset=None, compute_op=ALU.add).then_inc(y_added, 16)

            for c in range(AHEAD):
                gather(c, c)

            def expert_step(j, c):
                if within(j + AHEAD if isinstance(j, int) else j):
                    gather(j + AHEAD, c)
                add_rows(j, c % 2)

            expert_steps(pool, expert_step)
            for c in range(NT // 4):
                pool.wait_ge(f_var, c + 1)
                pool.tensor_tensor(frstd[:, :], fvar[:, :], f_half[:, :], ALU.pow).then_inc(f_rstd, 1)

        @block.scalar
        def _(act):
            split_hi(act, 0)
            self_att[2](act)
            act.wait_ge(*pe_end_self)
            split_hi(act, 1)
            cross_att[2](act)
            act.wait_ge(*pe_end_cross)

            for c in range(NCH):
                for k in range(KT):
                    act.wait_ge(x2T_mm, c * KT + k + 1)
                    if c >= 2 and k == 0:
                        act.wait_ge(log_mm, c - 1)
                    act.activation(x2T[c % 2][:, k, :], psum[0][k][:, :], ACT.Copy).then_inc(x2T_sb, 1)
            act.wait_ge(exp1_in, 1)
            act.activation(pr[:, :, :], sub[:, :, :], ACT.Exp).then_inc(exp1, 1)
            act.wait_ge(exp2_in, 1)
            act.activation(wt2[:, :], col[:, :], ACT.Exp).then_inc(exp2, 1)

            act.wait_ge(scale_ready, 1)

            def expert_hi(e):
                act.wait_ge(raw_in[e % 2], 48 * (e // 2 + 1))
                for n, w in enumerate((wg, wu)):
                    act.activation(experts2(w[0], e), raw_x[e % 2][n][:, :], ACT.Copy,
                                   scale=w_scale[:, n:n + 1]).then_inc(raw_hi, 1)
                act.activation(experts2(wd[0], e), raw_x[e % 2][2][:, :], ACT.Copy).then_inc(raw_hi, 1)

            def turn_x(j, s):
                act.wait_ge(xt_mm, j + 1)
                if not isinstance(j, int) or j >= 2:
                    act.wait_ge(u_mm, j - 1)
                act.activation(xt16[s][0][:, :, :].rearrange("p k t -> p (k t)"), xt_ps[s][:, 0:KT * P], ACT.Copy,
                               scale=X_SCALE).then_inc(xt_hi, 1)

            def silu(j, s):
                act.wait_ge(g_mm, j + 1)
                if not isinstance(j, int) or j >= 1:
                    act.wait_ge(hid_done, j)
                act.activation(gated[:, :], g_ps[s][:, :], ACT.Silu, scale=act_inv[:, 0:1]).then_inc(silu_done, 1)

            def turn_h(j):
                act.wait_ge(ht_mm, j + 1)
                if not isinstance(j, int) or j >= 1:
                    act.wait_ge(y_mm, j)
                act.activation(hidT[0][:, :, :].rearrange("p k t -> p (k t)"), ht_ps[:, :], ACT.Copy)\
                    .then_inc(ht_hi, 1)

            for e in range(SPLIT_FIRST):
                expert_hi(e)
            turn_x(0, 0)
            turn_x(1, 1)
            silu(0, 0)

            def expert_step(j, c):
                for e in splits_at(j):
                    expert_hi(e)
                turn_h(j)
                if within(j + 1):
                    silu(j + 1, (c + 1) % 2)
                if within(j + 2):
                    turn_x(j + 2, c % 2)

            expert_steps(act, expert_step)

        @block.vector
        def _(dve):
            for part in ("hi", "lo"):
                dve.memset(T[f"kT_{part}"][:, :, :, :, :, :].rearrange("p a c b h t -> p (a c b h t)").bitcast(F32),
                           0.0).then_inc(k_zeroed, 1)
            dve.wait_ge(k_zeroed, 2)
            for n in range(4):
                split_lo(dve, 0, n)
            self_att[3](dve)
            for n in range(4):
                split_lo(dve, 1, n)
            done = [0]

            def link(ins):
                done[0] += 1
                ins.then_inc(chain, 1)
                dve.wait_ge(chain, done[0])

            dve.wait_ge(scan_done, NX)
            dve.tensor_reduce(wmax[:, :], absmax[:, :, :].rearrange("p e n -> p n e"), AX.X, ALU.max)\
                .then_inc(max_all, 1)
            dve.wait_ge(max_all, 2)
            link(dve.tensor_scalar(w_exp[:, :], wall[:, :], TINY, None, ALU.max))
            link(dve.tensor_single_scalar(w_inv[:, :].bitcast(I32), w_exp[:, :].bitcast(I32), 0x7F800000,
                                          ALU.bitwise_and))
            link(dve.tensor_scalar(w_exp[:, :], w_inv[:, :], W_TOP, None, ALU.mult))
            link(dve.tensor_scalar(act_inv[:, :], w_exp[:, :], 1.0 / X_SCALE, None, ALU.mult))
            dve.reciprocal(w_scale[:, :], w_exp[:, :]).then_inc(scale_ready, 1)
            cross_att[3](dve)
            dve.wait_ge(*pe_end_cross)

            for c in range(NCH):
                dve.wait_ge(log_mm, c + 1)
                dve.tensor_copy(logT[:, c * TOK_CHUNK:(c + 1) * TOK_CHUNK], psum[3][0][0:NX, :]).then_inc(log_sb, 1)
            dve.wait_ge(logits_mm, 1)
            dve.wait_ge(tables, 1)

            def over(t, n=NX):
                return t.unsqueeze(2).to_broadcast([P, t.shape[1], n])

            def under(t, m):
                return t.unsqueeze(1).to_broadcast([P, m, t.shape[1]])

            TTs = dve.tensor_tensor
            link(dve.tensor_copy(lg[:, :, :], psum[3][1][:, 0:NT * NX].rearrange("p (t e) -> p t e", e=NX)))
            link(dve.tensor_reduce(col[:, :], lg[:, :, :], AX.X, ALU.max))
            TTs(sub[:, :, :], lg[:, :, :], over(col[:, :]), ALU.subtract).then_inc(exp1_in, 1)
            dve.wait_ge(exp1, 1)
            link(dve.tensor_reduce(col[:, :], pr[:, :, :], AX.X, ALU.add))
            link(dve.reciprocal(col2[:, :], col[:, :]))
            link(TTs(lg[:, :, :], pr[:, :, :], over(col2[:, :]), ALU.mult))

            def pick(probs, top, one):
                link(dve.tensor_reduce(top, probs, AX.X, ALU.max))
                link(TTs(tmp8[:, :, :], probs, over(top), ALU.is_equal))
                link(TTs(tmp8b[:, :, :], tmp8[:, :, :], under(tie[:, :], NT), ALU.mult))
                link(dve.tensor_reduce(col2[:, :], tmp8b[:, :, :], AX.X, ALU.max))
                link(TTs(one, tmp8b[:, :, :], over(col2[:, :]), ALU.is_equal))

            pick(lg[:, :, :], p1[:, :], one1[:, :, :])
            link(dve.scalar_tensor_tensor(sub[:, :, :], one1[:, :, :], -2.0, lg[:, :, :], ALU.mult, ALU.add))
            pick(sub[:, :, :], p2[:, :], one2[:, :, :])
            TTs(both16[:, :, :], one1[:, :, :], one2[:, :, :], ALU.add).then_inc(picked, 1)
            TTs(col[:, :], p2[:, :], p1[:, :], ALU.subtract).then_inc(exp2_in, 1)
            dve.wait_ge(exp2, 1)
            link(dve.tensor_scalar(col2[:, :], wt2[:, :], 1.0, None, ALU.add))
            link(dve.reciprocal(wt1[:, :], col2[:, :]))
            link(TTs(wt2[:, :], wt2[:, :], wt1[:, :], ALU.mult))
            link(dve.tensor_copy(meta[0][:, :, 0], wt1[:, :]))
            link(dve.tensor_copy(meta[1][:, :, 0], wt2[:, :]))

            dve.wait_ge(ranks, 1)
            before_ps = psum[2][0][:, 0:NT * NX].rearrange("p (t e) -> p t e", e=NX)
            tot_ps = psum[2][1][:, 0:NT * NX].rearrange("p (t e) -> p t e", e=NX)
            H = NT // 2
            link(dve.memset(pad[0][:, 0:H, :], 0.0))
            link(dve.memset(pad[1][:, 0:H, :], 0.0))
            link(dve.tensor_copy(pad[0][:, H:H + NT, :], tot_ps))
            src = 0
            step = 1
            while step < NT:
                link(TTs(pad[1 - src][:, H:H + NT, :], pad[src][:, H:H + NT, :], pad[src][:, H - step:H + NT - step, :],
                         ALU.add))
                src, step = 1 - src, 2 * step
            total = pad[src][:, H + NT - 1, :]
            link(dve.tensor_copy(ntok[:, :], total))
            link(TTs(tmp8[:, :, :], pad[src][:, H:H + NT, :], tot_ps, ALU.subtract))
            link(TTs(tmp8b[:, :, :], tmp8[:, :, :], before_ps, ALU.add))
            link(TTs(cmp16[:, :, :], over(ntok[:, :], NT), under(edges[:, :], NX), ALU.is_gt))
            link(dve.tensor_reduce(cum1[:, :], cmp16[:, :, :], AX.X, ALU.add))
            link(dve.tensor_scalar(tiles_e[:, :], cum1[:, :], 1.0, None, ALU.max))
            link(TTs(cmp8[:, :, :], below[:, :, :], under(tiles_e[:, :], NX), ALU.mult))
            link(dve.tensor_reduce(cum0[:, :], cmp8[:, :, :], AX.X, ALU.add))
            link(dve.tensor_scalar(end_e[:, :], cum0[:, :], float(P), None, ALU.mult))
            link(TTs(tmp8[:, :, :], tmp8b[:, :, :], under(end_e[:, :], NT), ALU.add))
            for which, one in enumerate((one1, one2)):
                link(TTs(tmp8b[:, :, :], tmp8[:, :, :], one[:, :, :], ALU.mult))
                link(dve.tensor_reduce(slot_f[which][:, :], tmp8b[:, :, :], AX.X, ALU.add))
                dve.tensor_copy(slot_i[which][:, :], slot_f[which][:, :]).then_inc(slots_ready, 1)
            link(TTs(cum1[:, :], cum0[:, :], tiles_e[:, :], ALU.add))
            link(TTs(mine[:, :, :], over(tile_no[:, :]), under(cum0[:, :], TILES), ALU.is_ge))
            link(TTs(mine2[:, :, :], over(tile_no[:, :]), under(cum1[:, :], TILES), ALU.is_ge))
            link(TTs(mine[:, :, :], mine[:, :, :], mine2[:, :, :], ALU.subtract))
            link(TTs(mine2[:, :, :], mine[:, :, :], under(e_of[:, :], TILES), ALU.mult))
            link(dve.tensor_reduce(expert_f[:, :], mine2[:, :, :], AX.X, ALU.add))
            dve.tensor_copy(expert_i[:, :], expert_f[:, :]).then_inc(plan_ready, 1)

            def expert_lo(e):
                for n, w in enumerate((wg, wu)):
                    dve.wait_ge(raw_hi, 3 * e + n + 1)
                    dve.scalar_tensor_tensor(experts2(w[1], e), raw_x[e % 2][n][:, :], w_scale[:, n:n + 1],
                                             experts2(w[0], e), ALU.mult, ALU.subtract).then_inc(raw_lo, 1)
                dve.wait_ge(raw_hi, 3 * e + 3)
                TTs(experts2(wd[1], e), raw_x[e % 2][2][:, :], experts2(wd[0], e).bitcast(F32),
                    ALU.subtract).then_inc(raw_lo, 1)

            def turn_x(j, s):
                dve.wait_ge(xt_hi, j + 1)
                dve.scalar_tensor_tensor(xt16[s][1][:, :, :].rearrange("p k t -> p (k t)"), xt_ps[s][:, 0:KT * P],
                                         X_SCALE, xt16[s][0][:, :, :].rearrange("p k t -> p (k t)"),
                                         ALU.mult, ALU.subtract).then_inc(xt_lo, 1)

            def hidden(j, s):
                dve.wait_ge(u_mm, j + 1)
                dve.wait_ge(silu_done, j + 1)
                dve.scalar_tensor_tensor(hid[s][:, :], u_ps[s][:, :], act_inv[:, 1:2], gated[:, :],
                                         ALU.mult, ALU.mult).then_inc(hid_done, 1)

            def turn_h(j):
                dve.wait_ge(ht_hi, j + 1)
                TTs(hidT[1][:, :, :].rearrange("p k t -> p (k t)"), ht_ps[:, :],
                    hidT[0][:, :, :].rearrange("p k t -> p (k t)").bitcast(F32), ALU.subtract).then_inc(ht_lo, 1)

            def weigh(j, s):
                dve.tensor_copy(row_w[s][:, :], slot[:, bass.ds(j, 1), 0]).then_inc(w_kept, 1)
                if not isinstance(j, int) or j >= 2:
                    dve.wait_ge(y_added, 16 * (j - 1))
                dve.wait_ge(y_mm, j + 1)
                dve.wait_ge(w_kept, j + 1)
                dve.tensor_scalar(yrow[s][:, :], y_ps[:, 0:D], row_w[s][:, :], None, ALU.mult).then_inc(y_sb, 1)

            for e in range(SPLIT_FIRST):
                expert_lo(e)
            dve.wait_ge(slots_in, 16)
            turn_x(0, 0)
            turn_x(1, 1)
            hidden(0, 0)

            def expert_step(j, c):
                for e in splits_at(j):
                    expert_lo(e)
                turn_h(j)
                if within(j + 1):
                    hidden(j + 1, (c + 1) % 2)
                if within(j + 2):
                    turn_x(j + 2, c % 2)
                weigh(j, c % 2)

            expert_steps(dve, expert_step)

            for c in range(NT // 4):
                src = fin_in[c % 2]
                dve.wait_ge(f_in, 16 * (c + 1))
                for t in range(4):
                    dve.bn_stats(fbn[:, t, :], src[:, t, :]).then_inc(f_stats, 1)
                dve.wait_ge(f_stats, 4 * (c + 1))
                for t in range(4):
                    dve.bn_aggr(fmv[:, t, :], fbn[:, t, :]).then_inc(f_mom, 1)
                dve.wait_ge(f_mom, 4 * (c + 1))
                dve.tensor_scalar(fvar[:, :], fmv[:, :, 1], EPS, None, ALU.add).then_inc(f_var, 1)
                dve.wait_ge(f_rstd, c + 1)
                if c >= 2:
                    dve.wait_ge(f_out, 16 * (c - 1))
                for t in range(4):
                    dve.tensor_scalar(fin_out[c % 2][:, t, :], src[:, t, :], fmv[:, t, 0:1], frstd[:, t:t + 1],
                                      ALU.subtract, ALU.mult).then_inc(f_done, 1)

        @block.tensor
        def _(pe):
            def router_chunk(c):
                pe.wait_ge(x2T_sb, (c + 1) * KT)
                if c:
                    pe.wait_ge(log_sb, c)
                for k in range(KT):
                    mm = pe.matmul(psum[3][0][0:NX, :], wr[:, k, :], x2T[c % 2][:, k, :], start=(k == 0),
                                   stop=(k == KT - 1))
                mm.then_inc(log_mm, 1)

            pe.wait_ge(consts, 4)
            self_att[1](pe)
            cross_att[1](pe)
            pe.wait_ge(*cross_att[5]["dve"])
            pe.wait_ge(rows_in, 16)
            pe.wait_ge(wr_in, 16)
            for c in range(NCH):
                for k in range(KT):
                    if c:
                        pe.wait_ge(x2T_sb, (c - 1) * KT + k + 1)
                    for t in range(CT):
                        mm = pe.transpose(psum[0][k][:, t * P:(t + 1) * P], rows2[:, c * CT + t, k * P:(k + 1) * P],
                                          ident[:, :])
                    mm.then_inc(x2T_mm, 1)
                if c:
                    router_chunk(c - 1)
            router_chunk(NCH - 1)
            pe.wait_ge(log_sb, NCH)
            for t in range(NT):
                mm = pe.transpose(psum[3][1][:, t * NX:(t + 1) * NX], logT[:, t * P:(t + 1) * P], ident[0:NX, 0:NX])
            mm.then_inc(logits_mm, 1)
            pe.wait_ge(picked, 1)
            m = both16[:, :, :].rearrange("p t e -> p (t e)")
            pe.matmul(psum[2][0][:, 0:NT * NX], earlier[:, :], m, start=True, stop=True)
            pe.matmul(psum[2][1][:, 0:NT * NX], ones16[:, :], m, start=True, stop=True).then_inc(ranks, 1)
            pe.wait_ge(plan_ready, 1)

            def turn_x(j, c):
                pe.wait_ge(x_gathered[c], (j - c) * (16 // AHEAD) + 16)
                if not isinstance(j, int) or j >= 2:
                    pe.wait_ge(xt_lo, j - 1)
                for k in range(KT):
                    mm = pe.transpose(xt_ps[c % 2][:, k * P:(k + 1) * P], xrow[c][:, k * P:(k + 1) * P], ident[:, :])
                mm.then_inc(xt_mm, 1)

            def gate_up(j, s):
                e = pe.value_load(expert_i[0:1, bass.ds(j, 1)], min_val=0, max_val=NX - 1)
                pe.wait_ge(raw_lo, e * 3 + 3)
                pe.wait_ge(xt_lo, j + 1)
                for ps, w, done in ((g_ps[s], wg, g_mm), (u_ps[s], wu, u_mm)):
                    n = 0
                    for k in range(KT):
                        for xx, ww in terms(xt16[s][0], xt16[s][1], w[0], w[1]):
                            mm = pe.matmul(ps[:, :], xx[:, k, :], ww[:, bass.ds(e, 1), k, :].rearrange("p a f -> p (a f)"),
                                           start=(n == 0), stop=(n == 3 * KT - 1))
                            n += 1
                    mm.then_inc(done, 1)

            def turn_h(j, s):
                pe.wait_ge(hid_done, j + 1)
                for k in range(FT):
                    mm = pe.transpose(ht_ps[:, k * P:(k + 1) * P], hid[s][:, k * P:(k + 1) * P], ident[:, :])
                mm.then_inc(ht_mm, 1)

            def down(j):
                e = pe.value_load(expert_i[0:1, bass.ds(j, 1)], min_val=0, max_val=NX - 1)
                pe.wait_ge(ht_lo, j + 1)
                if not isinstance(j, int) or j >= 1:
                    pe.wait_ge(y_sb, j)
                n = 0
                for k in range(FT):
                    for hh, ww in terms(hidT[0], hidT[1], wd[0], wd[1]):
                        mm = pe.matmul(y_ps[:, 0:D], hh[:, k, :], ww[:, bass.ds(e, 1), k, :].rearrange("p a d -> p (a d)"),
                                       start=(n == 0), stop=(n == 3 * FT - 1))
                        n += 1
                mm.then_inc(y_mm, 1)

            turn_x(0, 0)
            turn_x(1, 1)
            gate_up(0, 0)

            def expert_step(j, c):
                turn_h(j, c % 2)
                if within(j + 1):
                    gate_up(j + 1, (c + 1) % 2)
                if within(j + 2):
                    turn_x(j + 2, (c + 2) % AHEAD)
                down(j)

            expert_steps(pe, expert_step)


_INS = ["x", "ctx_1024", "L0_attn_w_q", "L0_attn_w_k", "L0_attn_w_v", "L0_attn_w_o", "L0_xattn_Wq", "L0_xattn_Wk",
        "L0_xattn_Wv", "L0_xattn_Wo", "L0_ffn_router_kernel_DE", "L0_ffn_kernel_gating_EDF", "L0_ffn_kernel_up_EDF",
        "L0_ffn_kernel_down_EFD"]
_OUTS = [((16, 128, 256), "float32")]


def kernel(**inputs):
    import numpy as _np
    import concourse.bacc as _bacc
    from concourse import mybir as _mybir
    from concourse.bass_utils import run_bass_kernel_spmd as _run

    nc = _bacc.Bacc("TRN2", target_bir_lowering=False, num_devices=1)
    arrays, args = {}, []
    for name in _INS:
        a = _np.ascontiguousarray(inputs[name])
        arrays[f"in_{name}_dram"] = a
        args.append(nc.dram_tensor(f"in_{name}_dram", a.shape, _mybir.dt.from_np(a.dtype), kind="ExternalInput").ap())
    outs = []
    for i, (shape, dtype) in enumerate(_OUTS):
        dt = _mybir.dt.from_np(_np.dtype(dtype))
        outs.append(nc.dram_tensor(f"out_{i}_dram", shape, dt, kind="ExternalOutput").ap())
    build(nc, args, outs[0])
    r = _run(nc, [arrays], core_ids=[0])
    got = tuple(r.results[0][f"out_{i}_dram"] for i in range(len(_OUTS)))
    return got[0]
```

```python
from contextlib import ExitStack

import concourse.bass as bass
from concourse import mybir

ALU = mybir.AluOpType
ACT = mybir.ActivationFunctionType
AX = mybir.AxisListType
F32 = mybir.dt.float32
F32R = mybir.dt.float32r
BF16 = mybir.dt.bfloat16

P = 128
HEADS = 16
DH = 64
SEG = 64
DIL = 4
EPS = 1e-5
OUT_SLOT = 3
NORM_SLOT = 4
MASKED = -1e30
PAIR = 2
UNIT_HEADS = 4
GROUPS = HEADS // UNIT_HEADS
UNITS = GROUPS * PAIR
RING = 4
CHUNKS = UNIT_HEADS // 2


def terms(hi_a, lo_a, hi_b, lo_b):
    return ((hi_a, hi_b), (hi_a, lo_b), (lo_a, hi_b))


class Count:

    def __init__(self, before, first, per):
        self.before, self.first, self.per = before, first, per

    def at(self, it, n):
        if isinstance(it, int) and it == 0:
            return self.before + n
        return it * self.per + (self.before + self.first - self.per + n)


def schedule(cross, first, last):
    slots = [[("Q", 1), ("K", 1)],
             [("V", 1, 0)],
             [("Q", 2)],
             [("K", 2)],
             [("Q", 3), ("V", 0, 1)],
             [("K", 3), ("V", 1, 1)],
             [("Q", 0)],
             [("K", 0), ("V", 0, 0)]]
    if not first:
        slots[OUT_SLOT - 1] += [("OUT", 0)] if cross else []
        slots[OUT_SLOT] += [("OUT", 1)] if cross else [("OUT", None)]
    routed = cross and not first
    slots[5] += [("YT", 0)] if routed else []
    if last:
        slots[6], slots[7] = [], []
    else:
        slots[5] += [("XT", 0)] + ([("XT", 1)] if cross else [])
    slots[5] += [("LG", 0)] if routed else []
    slots[6] += [("RK", 0)] if routed else []
    return slots


def banked(cross, slots):
    full = [j for s in schedule(cross, False, False) for j in s]
    return [[(j, full.index(j) % 2) for j in s] for s in slots]


def hi_ops(job):
    return {"K": 2, "OUT": 0, "YT": 0, "LG": 0, "RK": 0}.get(job[0], 1)


def attention_stage(nc, ctx, tag, cross, x_dram, kv_dram, w_sb, mask, ident, ident16, psum, sb_of, y_drams, w_ready,
                    each_pass_sync=None, each_pass_vector=None, route=None):
    NIT = x_dram.shape[0] // PAIR
    D = x_dram.shape[2]
    KT = D // P
    full = [j for s in schedule(cross, False, False) for j in s]
    JOBS = len(full)
    OUTS = len([j for j in full if j[0] == "OUT"])
    PRE = [("XT", 0)] + ([("XT", 1)] if cross else []) + [("Q", 0), ("K", 0), ("V", 0, 0)]
    HIS = sum(map(hi_ops, full))

    def sem(name):
        return ctx.enter_context(nc.semaphore(f"{tag}_{name}"))

    x_in, kv_in, res_in = sem("x_in"), sem("kv_in"), sem("res_in")
    job_mm, job_hi, job_free = sem("job_mm"), sem("job_hi"), sem("job_free")
    scores_ready, max_ready, exp_done = sem("scores_ready"), sem("max_ready"), sem("exp_done")
    recip_ready, probs_ready = sem("recip_ready"), sem("probs_ready")
    tr_done, pt_hi_done, pt_lo_done = sem("tr_done"), sem("pt_hi_done"), sem("pt_lo_done")
    pv_done, o_hi_done, o_lo_done = sem("pv_done"), sem("o_hi_done"), sem("o_lo_done")
    var_ready, stats_ready, moments_ready, rstd_ready, y_ready, y_stored = (
        sem("var_ready"), sem("stats_ready"), sem("moments_ready"), sem("rstd_ready"), sem("y_ready"), sem("y_stored"))

    ROUTED = [j for j in full if j[0] in ("YT", "LG", "RK")]
    C_job = Count(len(PRE), JOBS - OUTS - len(ROUTED), JOBS)
    C_hi = Count(sum(map(hi_ops, PRE)), HIS, HIS)
    C_unit = Count(0, UNITS, UNITS)

    T = sb_of
    wq_hi, wq_lo, wk_hi, wk_lo, wv_hi, wv_lo, wo_hi, wo_lo = w_sb
    job_bank, S, PT, OT = psum

    x_pairs = x_dram.rearrange("(i b) p d -> i p b d", b=PAIR)
    kv_pairs = kv_dram.rearrange("(i b) p d -> i p b d", b=PAIR)
    y_pairs = [y.rearrange("(i b) p d -> i p b d", b=PAIR) for y in y_drams]
    STORED = 16 * len(y_pairs)
    xT = [(T["xT_hi"], T["xT_lo"])]
    xT.append((T["cT_hi"], T["cT_lo"]) if cross else xT[0])
    raw = [T["x_raw"], T["c_raw"]]
    raw_in = [x_in, kv_in]

    def passes(emit, epilogue, eng):
        emit(0, True, False)
        with eng.Fori(1, NIT - 1) as it:
            emit(it, False, False)
        emit(NIT - 1, False, True)
        epilogue()

    def lagged(it, k, lag, first):
        if k >= lag:
            return [(it, k - lag)]
        return [] if first else [(it - 1, k - lag + UNITS)]

    def numbered(first, last):
        n, out = 0, []
        for s in banked(cross, schedule(cross, first, last)):
            row = []
            for job, bank in s:
                row.append((n, job, bank))
                n += 1
            out.append(row)
        return out

    def bank_history(first, last):
        pre = [(j, full.index(j) % 2) for j in PRE]
        seen = {}
        for k, (j, b) in enumerate(pre):
            seen[b] = k - len(pre)
        if not first:
            for was_first in (True, False):
                rows = numbered(was_first, False)
                total = sum(map(len, rows))
                for row in rows:
                    for n, job, b in row:
                        seen[b] = max(seen[b], n - total)
        before = {}
        for row in numbered(first, last):
            for n, job, b in row:
                before[n] = seen[b]
                seen[b] = n
        return before

    def sync_program(sp):
        def xt_jobs(i, first):
            return C_job.at(i, [n for row in numbered(first, False) for n, j, _ in row if j[0] == "XT"][-1] + 1)

        def load_x(i):
            sp.dma_start(raw[0][:, :, :], x_pairs[i]).then_inc(x_in, 16)
            if cross:
                sp.dma_start(raw[1][:, :, :], kv_pairs[i]).then_inc(kv_in, 16)

        def store_y_load_res(i):
            sp.wait_ge(y_ready, i * PAIR)
            for y in y_pairs:
                sp.dma_start(y[i - 1], T["y_out"][:, :, :]).then_inc(y_stored, 16)
            sp.wait_ge(y_stored, i * STORED)
            sp.dma_start(T["x_res"][:, :, :], x_pairs[i]).then_inc(res_in, 16)

        def also(i):
            if each_pass_sync is not None:
                each_pass_sync(sp, i)

        load_x(0)
        sp.dma_start(T["x_res"][:, :, :], x_pairs[0]).then_inc(res_in, 16)
        sp.wait_ge(job_mm, len([j for j in PRE if j[0] == "XT"]))
        load_x(1)
        sp.wait_ge(job_mm, xt_jobs(0, True))
        load_x(2)
        also(0)
        store_y_load_res(1)
        also(1)
        with sp.Fori(2, NIT - 1) as i:
            sp.wait_ge(job_mm, xt_jobs(i - 1, False))
            load_x(i + 1)
            store_y_load_res(i)
            also(i)
        store_y_load_res(NIT - 1)
        also(NIT - 1)
        sp.wait_ge(y_ready, NIT * PAIR)
        for y in y_pairs:
            sp.dma_start(y[NIT - 1], T["y_out"][:, :, :]).then_inc(y_stored, 16)
        sp.wait_ge(y_stored, NIT * STORED)

    def free_of(it, kind):
        rows = numbered(isinstance(it, int) and it == 0, isinstance(it, int) and it == NIT - 1)
        return C_job.at(it, [n for row in rows for n, j, _ in row if j[0] == kind][0] + 1)

    DONE = C_job.at(NIT - 1, JOBS - len(PRE))
    LAST_JOBS = [j for j in full if j[0] == "OUT"] + ROUTED

    def tensor_program(pe):
        weight_of = {("Q", 0): 1, ("K", 0): 2, ("V", 0, 0): 3, [j for j in full if j[0] == "OUT"][0]: 4}

        def job_matmuls(job, bank, it, xt_of):
            ps = job_bank[bank]
            kind = job[0]
            if job in weight_of:
                pe.wait_ge(w_ready[0], w_ready[1] + weight_of.pop(job))
            if kind == "XT":
                src, n = job[1], xt_of
                pe.wait_ge(raw_in[src], 16 * n + 16)
                for k in range(KT):
                    for b in range(PAIR):
                        mm = pe.transpose(ps[:, (k * PAIR + b) * P:(k * PAIR + b + 1) * P],
                                          raw[src][:, b, k * P:(k + 1) * P], ident[:, :])
                return mm
            if kind in "QK":
                g = job[1]
                w_hi, w_lo = (wq_hi, wq_lo) if kind == "Q" else (wk_hi, wk_lo)
                t_hi, t_lo = xT[0] if kind == "Q" else xT[1]
                for c in range(CHUNKS):
                    cols = slice((g * CHUNKS + c) * P, (g * CHUNKS + c + 1) * P)
                    n = 0
                    for k in range(KT):
                        for w, t in terms(w_hi, w_lo, t_hi, t_lo):
                            mm = pe.matmul(ps[:, c * PAIR * P:(c + 1) * PAIR * P], w[:, k, cols], t[:, k, :],
                                           start=(n == 0), stop=(n == 3 * KT - 1))
                            n += 1
                return mm
            if kind == "V":
                _, b, half = job
                t_hi, t_lo = xT[1]
                n = 0
                for k in range(KT):
                    for t, w in terms(t_hi, t_lo, wv_hi, wv_lo):
                        mm = pe.matmul(ps[:, :], t[:, k, b * P:(b + 1) * P], w[:, k, half * 512:(half + 1) * 512],
                                       start=(n == 0), stop=(n == 3 * KT - 1))
                        n += 1
                return mm
            if kind == "YT":
                for k in range(KT):
                    for b in range(PAIR):
                        mm = pe.transpose(ps[:, (k * PAIR + b) * P:(k * PAIR + b + 1) * P],
                                          T["y_out"][:, b, k * P:(k + 1) * P], ident[:, :])
                return mm
            if kind in ("LG", "RK"):
                return route.tensor(pe, kind, ps)
            bs = range(PAIR) if job[1] is None else [job[1]]
            NC = GROUPS * CHUNKS
            for at, b in enumerate(bs):
                n = 0
                for c in range(NC):
                    for o, w in terms(T["oT_hi"], T["oT_lo"], wo_hi, wo_lo):
                        mm = pe.matmul(ps[:, at * D:(at + 1) * D], o[:, c, b, :], w[:, c, :],
                                       start=(n == 0), stop=(n == 3 * NC - 1))
                        n += 1
            return mm

        def qk(it, k):
            g, b = divmod(k, PAIR)
            n_k = K_jobs(it)[g]
            if b == 0:
                pe.wait_ge(job_free, n_k)
            if not (isinstance(it, int) and it == 0 and k < 2):
                pe.wait_ge(exp_done, C_unit.at(it, k - 1))
            for c in range(CHUNKS):
                out = S[k % 2][:, c * 2 * P:(c + 1) * 2 * P]
                n = 0
                for q, kk in terms(T["qT_hi"], T["qT_lo"], T["kT_hi"], T["kT_lo"]):
                    mm = pe.matmul(out, q[:, g % 2, c, b, :],
                                   kk[:, g % 2, c, b, :, :].rearrange("p h t -> p (h t)"),
                                   start=(n == 0), stop=(n == 2 and cross))
                    n += 1
                if not cross:
                    mm = pe.matmul(out, ident16[:, :], mask[:, :], start=False, stop=True)
            mm.then_inc(scores_ready, 1)

        def K_jobs(it):
            first, last = (isinstance(it, int) and it == 0), (isinstance(it, int) and it == NIT - 1)
            out = {0: C_job.at(it, 0)}
            for row in numbered(first, last):
                for n, j, _ in row:
                    if j[0] == "K" and j[1]:
                        out[j[1]] = C_job.at(it, n + 1)
            return out

        def transposes(it, k):
            pe.wait_ge(probs_ready, C_unit.at(it, k + 1))
            if not (isinstance(it, int) and it == 0 and k < 2):
                pe.wait_ge(pt_lo_done, C_unit.at(it, k - 1))
            for h in range(UNIT_HEADS):
                mm = pe.transpose(PT[k % 2][:, h * P:(h + 1) * P], T["probs"][:, k % RING, h, :], ident[:, :])
            mm.then_inc(tr_done, 1)

        def pv(it, k):
            g, b = divmod(k % UNITS, PAIR)
            pe.wait_ge(pt_lo_done, C_unit.at(it, k + 1))
            if not (isinstance(it, int) and it == 0 and k < 2):
                pe.wait_ge(o_lo_done, C_unit.at(it, k - 1))
            if k in (0, 1, UNITS // 2, UNITS // 2 + 1):
                first, last = (isinstance(it, int) and it == 0), (isinstance(it, int) and it == NIT - 1)
                n = [n for row in numbered(first, last) for n, j, _ in row
                     if j == ("V", b, k // (UNITS // 2)) and k]
                pe.wait_ge(job_free, C_job.at(it, n[0] + 1 if n else 0))
            for c in range(CHUNKS):
                cols = slice((g * CHUNKS + c) * P, (g * CHUNKS + c + 1) * P)
                n = 0
                for v, p in terms(T["v_hi"], T["v_lo"], T["pT_hi"], T["pT_lo"]):
                    mm = pe.matmul(OT[k % 2][:, c * 2 * P:(c + 1) * 2 * P], v[:, b, cols],
                                   p[:, k % 2, 2 * c:2 * c + 2, :].rearrange("p h t -> p (h t)"),
                                   start=(n == 0), stop=(n == 2))
                    n += 1
            mm.then_inc(pv_done, 1)

        def run_job(it, n, job, bank, before, pre_xt=None):
            if before is not None:
                pe.wait_ge(job_free, C_job.at(it, before + 1))
            if job[0] == "OUT":
                pe.wait_ge(o_lo_done, C_unit.at(it, -1 if job[1] == 0 else 0))
            if job == ("Q", 0):
                pe.wait_ge(job_free, C_job.at(it, n))
            if job[0] == "YT":
                pe.wait_ge(y_ready, it * PAIR)
            if job[0] == "LG":
                pe.wait_ge(job_free, free_of(it, "YT"))
            if job[0] == "RK":
                route.tensor_wait(pe, it - 1)
            xt = None
            if job[0] == "XT":
                xt = 0 if pre_xt is not None else it + 1
            job_matmuls(job, bank, it, xt).then_inc(job_mm, 1)

        hist = {}
        for k, job in enumerate(PRE):
            bank = full.index(job) % 2
            if bank in hist:
                pe.wait_ge(job_free, hist[bank] + 1)
            if job == ("Q", 0):
                pe.wait_ge(job_free, k)
            hist[bank] = k
            job_matmuls(job, bank, 0, 0).then_inc(job_mm, 1)

        def one_pass(it, first, last):
            before = bank_history(first, last)
            for k, row in enumerate(numbered(first, last)):
                qk(it, k)
                outs = [r for r in row if r[1][0] == "OUT"]
                for n, job, bank in row:
                    if job[0] != "OUT":
                        run_job(it, n, job, bank, before[n])
                for u in lagged(it, k, 2, first):
                    transposes(*u)
                for n, job, bank in outs:
                    run_job(it, n, job, bank, before[n])
                for u in lagged(it, k, 3, first):
                    pv(*u)

        def finish():
            last = NIT - 1
            transposes(last, UNITS - 2)
            pv(last, UNITS - 3)
            transposes(last, UNITS - 1)
            pv(last, UNITS - 2)
            pv(last, UNITS - 1)
            for k, j in enumerate(LAST_JOBS):
                pe.wait_ge(job_free, DONE + (0 if j[0] == "OUT" else k))
                if j[0] == "OUT":
                    pe.wait_ge(o_lo_done, UNITS * NIT)
                if j[0] == "YT":
                    pe.wait_ge(y_ready, NIT * PAIR)
                if j[0] == "RK":
                    route.tensor_wait(pe, last)
                job_matmuls(j, k % 2, last, None).then_inc(job_mm, 1)

        passes(one_pass, finish, pe)

    def k_views(ps, half):
        rows = slice(half * DH, (half + 1) * DH)
        return rows, ps[rows, :].rearrange("p (c t) -> p c t", t=P)

    def job_dst(job):
        kind = job[0]
        if kind == "XT":
            hi, lo = xT[job[1]]
            return hi[:, :, :].rearrange("p k t -> p (k t)"), lo[:, :, :].rearrange("p k t -> p (k t)")
        if kind == "Q":
            return [t[:, job[1] % 2, :, :, :].rearrange("p c b t -> p (c b t)") for t in (T["qT_hi"], T["qT_lo"])]
        if kind == "V":
            _, b, half = job
            return [t[:, b, half * 512:(half + 1) * 512] for t in (T["v_hi"], T["v_lo"])]
        g = job[1]
        return [[t[h * DH:(h + 1) * DH, g % 2, :, :, h, :].rearrange("p c b t -> p (c b) t") for h in range(2)]
                for t in (T["kT_hi"], T["kT_lo"])]

    def scalar_program(act):
        def job_part(job, bank, number, it):
            if not hi_ops(job):
                return
            act.wait_ge(job_mm, number)
            ps = job_bank[bank]
            hi = job_dst(job)[0]
            if job[0] == "K":
                for h in range(2):
                    rows, src = k_views(ps, h)
                    act.activation(hi[h], src, ACT.Copy).then_inc(job_hi, 1)
            else:
                act.activation(hi, ps[:, :], ACT.Copy).then_inc(job_hi, 1)

        def exp(it, k):
            act.wait_ge(max_ready, C_unit.at(it, k + 1))
            if not (isinstance(it, int) and it == 0 and k < RING):
                act.wait_ge(tr_done, C_unit.at(it, k - RING + 1))
            for h in range(UNIT_HEADS):
                a = act.activation(T["probs"][:, k % RING, h, :], S[k % 2][:, h * P:(h + 1) * P], ACT.Exp,
                                   bias=T["neg_max"][:, k % RING, h:h + 1],
                                   accum_out=T["row_sum"][:, k % RING, h:h + 1])
            a.then_inc(exp_done, 1)

        def pt_hi(it, k):
            act.wait_ge(tr_done, C_unit.at(it, k + 1))
            if not (isinstance(it, int) and it == 0 and k < 2):
                act.wait_ge(pv_done, C_unit.at(it, k - 1))
            act.activation(T["pT_hi"][:, k % 2, :, :].rearrange("p h t -> p (h t)"), PT[k % 2][:, :],
                           ACT.Copy).then_inc(pt_hi_done, 1)

        def o_hi(it, k):
            g, b = divmod(k, PAIR)
            act.wait_ge(pv_done, C_unit.at(it, k + 1))
            src = OT[k % 2][:, :].rearrange("p (c h t) -> p c h t", c=CHUNKS, h=2)
            for h in range(2):
                rows = slice(h * DH, (h + 1) * DH)
                act.activation(T["oT_hi"][rows, g * CHUNKS:(g + 1) * CHUNKS, b, :], src[rows, :, h, :],
                               ACT.Copy).then_inc(o_hi_done, 1)

        for k, job in enumerate(PRE):
            job_part(job, full.index(job) % 2, k + 1, 0)

        def one_pass(it, first, last):
            for k, row in enumerate(numbered(first, last)):
                for u in lagged(it, k, 1, first):
                    exp(*u)
                for u in lagged(it, k, 4, first):
                    o_hi(*u)
                for n, job, bank in row:
                    job_part(job, bank, C_job.at(it, n + 1), it)
                for u in lagged(it, k, 2, first):
                    pt_hi(*u)
                if route is not None and not first:
                    route.scalar(act, k, it - 1)

        def finish():
            last = NIT - 1
            exp(last, UNITS - 1)
            o_hi(last, UNITS - 4)
            pt_hi(last, UNITS - 2)
            o_hi(last, UNITS - 3)
            pt_hi(last, UNITS - 1)
            o_hi(last, UNITS - 2)
            o_hi(last, UNITS - 1)
            if route is not None:
                for k in (6, 7):
                    route.scalar(act, k, last)

        passes(one_pass, finish, act)

    def vector_program(dve):
        def job_lo(job, bank, his):
            ps = job_bank[bank]
            dve.wait_ge(job_hi, his)
            hi, lo = job_dst(job)
            if job[0] == "K":
                for h in range(2):
                    rows, src = k_views(ps, h)
                    v = dve.tensor_tensor(lo[h], src, hi[h].bitcast(F32), ALU.subtract)
                v.then_inc(job_free, 1)
            else:
                dve.tensor_tensor(lo, ps[:, :], hi.bitcast(F32), ALU.subtract).then_inc(job_free, 1)

        def out_part(job, bank, jobs_done, pair):
            bs = list(range(PAIR)) if job[1] is None else [job[1]]
            dve.wait_ge(job_mm, jobs_done)
            dve.wait_ge(res_in, 16 * pair + 16)
            dve.tensor_tensor(T["y_sum"][:, bs[0]:bs[-1] + 1, :],
                              job_bank[bank][:, 0:len(bs) * D].rearrange("p (b d) -> p b d", d=D),
                              T["x_res"][:, bs[0]:bs[-1] + 1, :], ALU.add).then_inc(job_free, 1)

        def row_stats():
            for b in range(PAIR):
                dve.bn_stats(T["bn"][:, b, :], T["y_sum"][:, b, :]).then_inc(stats_ready, 1)

        def moments():
            for b in range(PAIR):
                dve.bn_aggr(T["mv"][:, b, :], T["bn"][:, b, :]).then_inc(moments_ready, 1)

        def normalise(pair):
            dve.wait_ge(rstd_ready, pair + 1)
            for b in range(PAIR):
                dve.tensor_scalar(T["y_out"][:, b, :], T["y_sum"][:, b, :], T["mv"][:, b, 0:1], T["rstd"][:, b:b + 1],
                                  ALU.subtract, ALU.mult).then_inc(y_ready, 1)

        def neg_max(it, k):
            dve.wait_ge(scores_ready, C_unit.at(it, k + 1))
            dve.tensor_reduce(T["neg_max"][:, k % RING, :], S[k % 2][:, :].rearrange("p (h t) -> p h t", t=P),
                              AX.X, ALU.max, negate=True).then_inc(max_ready, 1)

        def recip(it, k):
            dve.wait_ge(exp_done, C_unit.at(it, k + 1))
            if not (isinstance(it, int) and it == 0 and k < RING):
                dve.wait_ge(probs_ready, C_unit.at(it, k - RING + 1))
            dve.reciprocal(T["row_inv"][:, k % RING, :], T["row_sum"][:, k % RING, :]).then_inc(recip_ready, 1)

        def pt_lo(it, k):
            dve.wait_ge(pt_hi_done, C_unit.at(it, k + 1))
            dve.tensor_tensor(T["pT_lo"][:, k % 2, :, :].rearrange("p h t -> p (h t)"), PT[k % 2][:, :],
                              T["pT_hi"][:, k % 2, :, :].rearrange("p h t -> p (h t)").bitcast(F32),
                              ALU.subtract).then_inc(pt_lo_done, 1)

        def o_lo(it, k):
            g, b = divmod(k, PAIR)
            dve.wait_ge(o_hi_done, C_unit.at(it, k + 1) * 2)
            src = OT[k % 2][:, :].rearrange("p (c h t) -> p c h t", c=CHUNKS, h=2)
            for h in range(2):
                rows = slice(h * DH, (h + 1) * DH)
                v = dve.tensor_tensor(T["oT_lo"][rows, g * CHUNKS:(g + 1) * CHUNKS, b, :], src[rows, :, h, :],
                                      T["oT_hi"][rows, g * CHUNKS:(g + 1) * CHUNKS, b, :].bitcast(F32), ALU.subtract)
            v.then_inc(o_lo_done, 1)

        his = 0
        for k, job in enumerate(PRE):
            his += hi_ops(job)
            job_lo(job, full.index(job) % 2, his)

        def one_pass(it, first, last):
            his = 0
            for k, row in enumerate(numbered(first, last)):
                if k == OUT_SLOT + 1 and not first:
                    dve.wait_ge(stats_ready, it * PAIR)
                neg_max(it, k)
                if k == OUT_SLOT + 1 and not first:
                    moments()
                for u in lagged(it, k, 1, first):
                    recip(*u)
                for u in lagged(it, k, 4, first):
                    o_lo(*u)
                if route is not None and not first and k == UNITS - 1:
                    route.vector_slots(dve, it - 1)
                for n, job, bank in row:
                    his += hi_ops(job)
                    if job in ROUTED:
                        dve.wait_ge(job_mm, C_job.at(it, n + 1))
                        route.vector_job(dve, job[0], job_bank[bank]).then_inc(job_free, 1)
                    elif job[0] != "OUT":
                        job_lo(job, bank, C_hi.at(it, his))
                for u in lagged(it, k, 2, first):
                    pt_lo(*u)
                if k == 5 and route is not None and not first:
                    route.vector_pick(dve, it - 1, job_free, free_of(it, "LG"))
                if k == UNITS - 1 and each_pass_vector is not None:
                    each_pass_vector(dve, it)
                outs = [r for r in row if r[1][0] == "OUT"]
                for n, job, bank in outs:
                    out_part(job, bank, C_job.at(it, n + 1), it - 1)
                if outs and k == OUT_SLOT:
                    ln_start(it)
                    row_stats()
                if k == NORM_SLOT and not first:
                    normalise(it - 1)
                if route is not None and not first and k == UNITS - 1:
                    route.vector_weights(dve, it - 1)

        def ln_start(it):
            dve.wait_ge(job_free, ln_count(it))

        def ln_count(it):
            first, last = False, (isinstance(it, int) and it == NIT - 1)
            n = [n for row in numbered(first, last) for n, j, _ in row if j[0] == "OUT"][-1]
            return C_job.at(it, n + 1)

        def finish():
            last = NIT - 1
            recip(last, UNITS - 1)
            o_lo(last, UNITS - 4)
            pt_lo(last, UNITS - 2)
            o_lo(last, UNITS - 3)
            pt_lo(last, UNITS - 1)
            o_lo(last, UNITS - 2)
            o_lo(last, UNITS - 1)
            for k, j in enumerate(LAST_JOBS[:OUTS]):
                out_part(j, k % 2, DONE + k + 1, last)
            dve.wait_ge(job_free, DONE + OUTS)
            row_stats()
            dve.wait_ge(stats_ready, NIT * PAIR)
            moments()
            normalise(last)
            for k, j in enumerate(LAST_JOBS):
                if j in ROUTED:
                    dve.wait_ge(job_mm, DONE + k + 1)
                    route.vector_job(dve, j[0], job_bank[k % 2]).then_inc(job_free, 1)
                    if j[0] == "LG":
                        route.vector_pick(dve, last, job_free, DONE + k + 1)
            if route is not None:
                route.vector_slots(dve, last)
                route.vector_weights(dve, last)

        passes(one_pass, finish, dve)

    def gpsimd_program(pool):
        def normalise_probs(it, k):
            pool.wait_ge(recip_ready, C_unit.at(it, k + 1))
            p = T["probs"][:, k % RING, :, :]
            pool.tensor_tensor(p, p, T["row_inv"][:, k % RING, :].unsqueeze(2).to_broadcast([P, UNIT_HEADS, P]),
                               ALU.mult).then_inc(probs_ready, 1)

        def rstd(pair):
            pool.wait_ge(moments_ready, pair * PAIR + PAIR)
            pool.tensor_tensor(T["var_eps"][:, :], T["mv"][:, :, 1], T["eps"][:, :], ALU.add).then_inc(var_ready, 1)
            pool.wait_ge(var_ready, pair + 1)
            pool.tensor_tensor(T["rstd"][:, :], T["var_eps"][:, :], T["minus_half"][:, :], ALU.pow)\
                .then_inc(rstd_ready, 1)

        def one_pass(it, first, last):
            for k in range(UNITS):
                if k == OUT_SLOT + 1 and not first:
                    rstd(it - 1)
                for u in lagged(it, k, 1, first):
                    normalise_probs(*u)
                if route is not None and not first:
                    route.gpsimd(pool, k, it - 1, job_free, free_of(it, "RK"))

        def finish():
            normalise_probs(NIT - 1, UNITS - 1)
            rstd(NIT - 1)
            if route is not None:
                for k in (5, 6, 7):
                    route.gpsimd(pool, k, NIT - 1, job_free, DONE + OUTS + 3)

        passes(one_pass, finish, pool)

    finals = {"pe": (job_mm, DONE + len(LAST_JOBS)), "dve": (job_free, DONE + len(LAST_JOBS)),
              "stored": (y_stored, NIT * STORED)}
    return sync_program, tensor_program, scalar_program, vector_program, gpsimd_program, finals


class Chain:

    def __init__(self, eng, sem, per, pair, steps=None):
        self.eng, self.sem, self.start, self.per, self.n, self.steps = eng, sem, pair * per, per, 0, steps

    def link(self, ins):
        self.n += 1
        ins.then_inc(self.sem, 1)
        self.eng.wait_ge(self.sem, self.start + self.n)

    def step(self):
        self.eng.sem_inc(self.steps, 1)

    def end(self):
        assert self.n == self.per, self.n


def over(t, n):
    return t.unsqueeze(2).to_broadcast([P, t.shape[1], n])


def under(t, m):
    return t.unsqueeze(1).to_broadcast([P, m, t.shape[1]])


class Router:
    POOL_LINKS = 7
    DVE_LINKS = 18

    def __init__(self, nc, R, sems, lists, KT, NX):
        self.nc, self.R, self.s, self.lists, self.KT, self.NX = nc, R, sems, lists, KT, NX

    def tensor_wait(self, pe, pair):
        pe.wait_ge(self.s["picked"], pair + 1)

    def tensor(self, pe, kind, ps):
        R, NX = self.R, self.NX
        if kind == "LG":
            for b in range(PAIR):
                for k in range(self.KT):
                    mm = pe.matmul(ps[:, b * NX:(b + 1) * NX], R["yT"][:, k * PAIR + b, :], R["wr"][:, k, :],
                                   start=(k == 0), stop=(k == self.KT - 1))
            return mm
        for b in range(PAIR):
            out = ps[:, b * NX:(b + 1) * NX]
            pe.matmul(out, R["earlier"][:, :], R["both16"][:, b, :], start=True, stop=(b == 0))
            for a in range(b):
                pe.matmul(out, R["ones16"][:, :], R["both16"][:, a, :], start=False, stop=(a == b - 1))
        for a in range(PAIR):
            mm = pe.matmul(ps[:, PAIR * NX:(PAIR + 1) * NX], R["ones16"][:, :], R["both16"][:, a, :],
                           start=(a == 0), stop=(a == PAIR - 1))
        return mm

    def vector_job(self, dve, kind, ps):
        R, NX = self.R, self.NX
        if kind == "YT":
            return dve.tensor_copy(R["yT"][:, :, :].rearrange("p k t -> p (k t)"), ps[:, :])
        if kind == "LG":
            return dve.tensor_copy(R["lg"][:, :, :].rearrange("p t e -> p (t e)"), ps[:, 0:PAIR * NX])
        return dve.tensor_copy(R["ranks"][:, :], ps[:, 0:(PAIR + 1) * NX])

    def vector_pick(self, dve, pair, job_free, logits):
        R, NX, s = self.R, self.NX, self.s
        self.dchain = chain = Chain(dve, s["dve_chain"], self.DVE_LINKS, pair)
        link = chain.link
        TT = dve.tensor_tensor
        dve.wait_ge(job_free, logits)
        src = R["lg"]
        top, eq, tq, tm = R["top"], R["eq"], R["tq"], R["tm"]
        for w in range(2):
            one = R["one"][:, w, :, :]
            link(dve.tensor_reduce(top[:, w, :], src[:, :, :], AX.X, ALU.max))
            link(TT(eq[:, :, :], src[:, :, :], over(top[:, w, :], NX), ALU.is_equal))
            link(TT(tq[:, :, :], eq[:, :, :], under(R["tie"][:, :], PAIR), ALU.mult))
            link(dve.tensor_reduce(tm[:, :], tq[:, :, :], AX.X, ALU.max))
            link(TT(one, tq[:, :, :], over(tm[:, :], NX), ALU.is_equal))
            if w == 0:
                link(dve.scalar_tensor_tensor(R["rest"][:, :, :], one, -HUGE, src[:, :, :], ALU.mult, ALU.add))
                src = R["rest"]
        TT(R["both16"][:, :, :], R["one"][:, 0, :, :], R["one"][:, 1, :, :], ALU.add).then_inc(s["picked"], 1)

    def gpsimd(self, pool, slot, pair, job_free, ranks):
        R, NX, s = self.R, self.NX, self.s
        TT = pool.tensor_tensor
        if slot == 5:
            self.chain = Chain(pool, s["pool_chain"], self.POOL_LINKS, pair, s["pool_step"])
            pool.wait_ge(s["picked"], pair + 1)
            lg, top = R["lg"], R["top"]
            self.chain.link(TT(R["less"][:, :, NX], top[:, 1, :], top[:, 0, :], ALU.subtract))
            TT(R["less"][:, :, 0:NX], lg[:, :, :], over(top[:, 0, :], NX), ALU.subtract).then_inc(s["exp1_in"], 1)
        if slot == 6:
            chain, link = self.chain, self.chain.link
            pool.wait_ge(s["exp1"], pair + 1)
            link(TT(R["drop"][:, :], R["exps"][:, :, NX], R["ones"][:, :], ALU.subtract))
            pool.sem_inc(s["sums_ready"], 1)
            pool.wait_ge(job_free, ranks)
            link(TT(R["rank"][:, :, :], R["ranks"][:, 0:PAIR * NX].rearrange("p (t e) -> p t e", e=NX),
                    under(R["base"][:, :], PAIR), ALU.add))
            link(TT(R["base"][:, :], R["base"][:, :], R["ranks"][:, PAIR * NX:(PAIR + 1) * NX], ALU.add))
            for w in range(2):
                m = TT(R["mine_of"][:, w, :, :], R["one"][:, w, :, :], R["rank"][:, :, :], ALU.mult)
            link(m)
            pool.wait_ge(s["dispatched"], pair * (32 * PAIR) + 48)
            link(TT(R["token_f"][:, :], R["token_f"][:, :], R["pair_tokens"][:, :], ALU.add))
            chain.step()
            for w in range(2):
                m = pool.tensor_copy(R["meta"][:, w, :, 1].bitcast(mybir.dt.int32), R["token_f"][:, :])
            link(m)
            pool.sem_inc(s["ranks_ready"], 1)
        if slot == 7:
            pool.wait_ge(s["slots_ready"], pair + 1)
            pool.wait_ge(s["wt_ready"], pair + 1)
            self.chain.step()
            for w in range(2):
                for t in range(PAIR):
                    pool.indirect_dma_start(out=self.lists, out_offset=bass.IndirectOffsetOnAxis(
                        ap=R["place_i"][:, w * PAIR + t:w * PAIR + t + 1], axis=0), in_=R["meta"][:, w, t, :],
                        in_offset=None).then_inc(s["dispatched"], 16)
            self.chain.end()

    def scalar(self, act, slot, pair):
        R, s = self.R, self.s
        if slot == 6:
            act.wait_ge(s["exp1_in"], pair + 1)
            act.activation(R["exps"][:, :, :], R["less"][:, :, :], ACT.Exp).then_inc(s["exp1"], 1)
        if slot == 7:
            act.wait_ge(s["exp2_in"], pair + 1)
            act.activation(R["exp2"][:, :], R["diff"][:, :], ACT.Exp).then_inc(s["exp2"], 1)

    def vector_slots(self, dve, pair):
        R, s = self.R, self.s
        link = self.dchain.link
        dve.wait_ge(s["sums_ready"], pair + 1)
        link(dve.tensor_reduce(R["sum"][:, :], R["exps"][:, :, 0:self.NX], AX.X, ALU.add))
        link(dve.reciprocal(R["inv"][:, :], R["sum"][:, :]))
        dve.tensor_tensor(R["diff"][:, :], R["drop"][:, :], R["inv"][:, :], ALU.mult).then_inc(s["exp2_in"], 1)
        dve.wait_ge(s["ranks_ready"], pair + 1)
        link(dve.tensor_reduce(R["place_f"][:, :], R["mine_of"][:, :, :, :].rearrange("p w t e -> p (w t) e"),
                               AX.X, ALU.add))
        link(dve.tensor_copy(R["place_i"][:, :], R["place_f"][:, :]))
        dve.tensor_scalar(R["column"][:, :], R["place_i"][:, :], 7, None, ALU.logical_shift_right)\
            .then_inc(s["dve_parts"], 1)
        dve.tensor_scalar(R["row"][:, :], R["place_i"][:, :], P - 1, 7, ALU.bitwise_and, ALU.logical_shift_left)\
            .then_inc(s["dve_parts"], 1)
        dve.wait_ge(s["dve_parts"], pair * 2 + 2)
        dve.tensor_tensor(R["place_i"][:, :], R["row"][:, :], R["column"][:, :], ALU.bitwise_or).then_inc(s["slots_ready"], 1)

    def vector_weights(self, dve, pair):
        R, s = self.R, self.s
        link = self.dchain.link
        dve.wait_ge(s["exp2"], pair + 1)
        link(dve.tensor_scalar(R["inv"][:, :], R["exp2"][:, :], 1.0, None, ALU.add))
        link(dve.reciprocal(R["meta"][:, 0, :, 0], R["inv"][:, :]))
        link(dve.tensor_tensor(R["meta"][:, 1, :, 0], R["exp2"][:, :], R["meta"][:, 0, :, 0], ALU.mult))
        dve.sem_inc(s["wt_ready"], 1)
        self.dchain.end()


WEIGHT_NAMES = ("wq", "wk", "wv", "wo")
X_SCALE = 256.0
W_TOP = 2.0 ** -13
HUGE = 1e30
TINY = 2.0 ** -100


def build(nc, args, out):
    (x, ctxt, a_wq, a_wk, a_wv, a_wo, c_wq, c_wk, c_wv, c_wo, router, w_gate, w_up, w_down) = args
    B, S, D = x.shape
    KT = D // P
    E = HEADS * DH
    NX, _, F = w_gate.shape
    FT = F // P
    TOK = B * S
    NT = TOK // P
    TILES = (2 * TOK) // P + NX - 1
    AHEAD = 4
    META = 2
    H16 = mybir.dt.float16
    I32 = mybir.dt.int32
    assert B // PAIR == NX and P == S

    x1 = nc.dram_tensor("x1_scratch", (B, S, D), F32).ap()
    x2 = nc.dram_tensor("x2_scratch", (TOK + P, D), F32).ap()
    acc = nc.dram_tensor("acc_scratch", (TOK + P, D), F32).ap()
    COLS = NX * NT
    lists = nc.dram_tensor("lists_scratch", (P * COLS, META), F32).ap()

    with ExitStack() as ctx:
        def sb(name, shape, dt=F32, stack=ctx):
            return stack.enter_context(nc.sbuf_tensor(name, shape, dt))

        def sem(name):
            return ctx.enter_context(nc.semaphore(name))

        T = {}
        for n in ("x_raw", "c_raw", "x_res", "y_sum", "y_out"):
            T[n] = sb(n, [P, PAIR, D])
        T["neg_max"] = sb("neg_max", [P, RING, UNIT_HEADS])
        T["row_sum"] = sb("row_sum", [P, RING, UNIT_HEADS])
        T["row_inv"] = sb("row_inv", [P, RING, UNIT_HEADS])
        T["bn"] = sb("bn", [P, PAIR, 6])
        T["mv"] = sb("mv", [P, PAIR, 2])
        for n in ("rstd", "var_eps", "minus_half", "eps"):
            T[n] = sb(n, [P, PAIR])
        ident = sb("ident", [P, P])
        ident16 = sb("ident16", [P, P], BF16)
        mask = sb("mask", [P, 2 * P], BF16)
        absmax = sb("absmax", [P, NX, 2])

        def table(name, *shape, dt=F32, stack=ctx):
            return sb(name, [P, *shape], dt, stack)

        e_of = table("e_of", NX)
        below = table("below", NX, NX)
        edges = table("edges", NT)
        tile_no = table("tile_no", TILES + 1)
        first_place = table("first_place", NX)
        first_col = table("first_col", NX)
        zero_row = table("zero_row", D)
        slot = table("slot_meta", COLS + 1, META)
        R = {"wr": table("router_w", KT, NX), "tie": table("tie", NX), 
             "earlier": table("earlier", P, dt=BF16), "ones16": table("ones16", P, dt=BF16),
             "ones": table("ones", PAIR), "pair_tokens": table("pair_tokens", PAIR), "base": table("base", NX),
             "token_f": table("token_f", PAIR), "yT": table("yT", KT * PAIR, P), "lg": table("lg", PAIR, NX),
             "top": table("top", 2, PAIR), "eq": table("eq", PAIR, NX), "tq": table("tq", PAIR, NX),
             "tm": table("tm", PAIR), "one": table("one", 2, PAIR, NX), "rest": table("rest", PAIR, NX),
             "both16": table("both16", PAIR, NX, dt=BF16), "less": table("less", PAIR, NX + 1),
             "exps": table("exps", PAIR, NX + 1), "drop": table("drop", PAIR), "sum": table("sum", PAIR),
             "inv": table("inv", PAIR), "diff": table("diff", PAIR), "exp2": table("exp2", PAIR),
             "ranks": table("ranks", (PAIR + 1) * NX), "rank": table("rank", PAIR, NX),
             "mine_of": table("mine_of", 2, PAIR, NX), "place_f": table("place_f", 2 * PAIR),
             "place_i": table("place_i", 2 * PAIR, dt=I32), "column": table("column", 2 * PAIR, dt=I32),
             "row": table("row", 2 * PAIR, dt=I32), "meta": table("meta", 2, PAIR, META)}
        ntok, some, tiles_e, cum0, cum1, offset = (table(n, NX) for n in (
            "ntok", "some", "tiles_e", "cum0", "cum1", "offset"))
        cmp16 = table("cmp16", NX, NT)
        cmp8 = table("cmp8", NX, NX)
        expert_f, col_f = table("expert_f", TILES + 1), table("col_f", TILES + 1)
        expert_i, col_i = table("expert_i", TILES + 1, dt=I32), table("col_i", TILES + 1, dt=I32)
        get_tok = [table(f"get_tok{i}", 1, dt=I32) for i in range(AHEAD)]
        get_w = [table(f"get_w{i}", 1) for i in range(AHEAD)]
        put_tok = [table(f"put_tok{i}", 1, dt=I32) for i in range(2)]
        put_w = [table(f"put_w{i}", 1) for i in range(2)]
        wmax, wall, w_exp, w_inv, w_scale, act_inv = (table(n, 2) for n in (
            "wmax", "wall", "w_exp", "w_inv", "w_scale", "act_inv"))
        fbn, fmv = table("fbn", 4, 6), table("fmv", 4, 2)
        fvar, frstd, f_half = table("fvar", 4), table("frstd", 4), table("f_half", 4)

        att = ExitStack()
        for n in ("xT", "cT"):
            for part in ("hi", "lo"):
                T[f"{n}_{part}"] = sb(f"{n}_{part}", [P, KT, PAIR * P], F32R, att)
        for part in ("hi", "lo"):
            T[f"qT_{part}"] = sb(f"qT_{part}", [P, 2, CHUNKS, PAIR, P], F32R, att)
            T[f"kT_{part}"] = sb(f"kT_{part}", [P, 2, CHUNKS, PAIR, 2, P], F32R, att)
            T[f"v_{part}"] = sb(f"v_{part}", [P, PAIR, E], F32R, att)
            T[f"pT_{part}"] = sb(f"pT_{part}", [P, 2, UNIT_HEADS, P], F32R, att)
            T[f"oT_{part}"] = sb(f"oT_{part}", [P, E // P, PAIR, P], F32R, att)
        T["probs"] = sb("probs", [P, RING, UNIT_HEADS, P], F32, att)
        raw_w = [sb(f"raw_{n}", [P, KT * E], F32, att) for n in WEIGHT_NAMES]
        w_sb = []
        for n, (a, b) in zip(WEIGHT_NAMES, [(KT, E)] * 3 + [(E // P, D)]):
            w_sb += [sb(f"{n}_hi", [P, a, b], F32R, att), sb(f"{n}_lo", [P, a, b], F32R, att)]
        scan_w = sb("scan_w", [P, 2, KT, F], F32, att)
        att.close()

        wg = [sb(f"wg_{part}", [P, NX, KT, F], H16) for part in ("hi", "lo")]
        wu = [sb(f"wu_{part}", [P, NX, KT, F], H16) for part in ("hi", "lo")]
        wd = [sb(f"wd_{part}", [P, NX, FT, D], F32R) for part in ("hi", "lo")]
        raw_x = [[sb(f"raw_expert{i}_{n}", [P, KT * F]) for n in ("gate", "up", "down")] for i in range(2)]
        late = ExitStack()
        mine, mine2 = (table(n, TILES + 1, NX, stack=late) for n in ("mine", "mine2"))
        late.close()
        xrow = [sb(f"xrow{i}", [P, D]) for i in range(AHEAD)]
        xt16 = [[sb(f"xt16_{part}{i}", [P, KT, P], H16) for part in ("hi", "lo")] for i in range(2)]
        gated = sb("gated", [P, F])
        hid = [sb(f"hidden{i}", [P, F]) for i in range(2)]
        hidT = [sb(f"hiddenT_{part}", [P, FT, P], F32R) for part in ("hi", "lo")]
        yrow = [sb(f"yrow{i}", [P, D]) for i in range(2)]
        fin_in, fin_out = ([raw_x[i][n][:, :].rearrange("p (t d) -> p t d", d=D) for i in range(2)] for n in range(2))

        psum = [[ctx.enter_context(nc.psum_tensor(f"{n}{i}", [P, 512], F32)) for i in range(2)]
                for n in ("job", "scores", "probsT", "outT")]
        xt_ps, g_ps, u_ps, (ht_ps, y_ps) = psum

        w_in = [[sem(f"{tag}_{n}_in") for n in WEIGHT_NAMES] for tag in ("self", "cross")]
        w_hi_done, w_ready = sem("w_hi_done"), sem("w_ready")
        consts, zeroed, k_zeroed = sem("consts"), sem("zeroed"), sem("k_zeroed")
        tables, tables_pool = sem("tables"), sem("tables_pool")
        scan_in, scan_done, max_all, scale_ready = sem("scan_in"), sem("scan_done"), sem("max_all"), sem("scale_ready")
        wr_in = sem("wr_in")
        raw_in = [sem("raw_in_even"), sem("raw_in_odd")]
        raw_hi, raw_lo = sem("raw_hi"), sem("raw_lo")
        R_sems = {n: sem(n) for n in (
            "pool_chain", "dve_chain", "pool_step", "picked", "exp1_in", "exp1", "exp2_in", "exp2", "sums_ready",
            "ranks_ready", "dve_parts", "slots_ready", "wt_ready", "dispatched")}
        dispatched, pool_step = R_sems["dispatched"], R_sems["pool_step"]
        chain, plan_ready, slots_in = sem("chain"), sem("plan_ready"), sem("slots_in")
        get_ready, put_ready = sem("get_ready"), sem("put_ready")
        xt_mm, xt_hi, xt_lo = sem("xt_mm"), sem("xt_hi"), sem("xt_lo")
        x_gathered = [sem(f"x_gathered{i}") for i in range(AHEAD)]
        g_mm, u_mm, silu_done, hid_done, ht_mm, ht_hi, ht_lo = (
            sem("g_mm"), sem("u_mm"), sem("silu_done"), sem("hid_done"), sem("ht_mm"), sem("ht_hi"), sem("ht_lo"))
        y_mm, y_sb, y_added = sem("y_mm"), sem("y_sb"), sem("y_added")
        f_in, f_stats, f_mom, f_var, f_rstd, f_done, f_out = (
            sem("f_in"), sem("f_stats"), sem("f_mom"), sem("f_var"), sem("f_rstd"), sem("f_done"), sem("f_out"))

        def scan_load(sp, i):
            if not (isinstance(i, int) and i == 0):
                sp.wait_ge(scan_done, i)
            for n, w in enumerate((w_gate, w_up)):
                sp.dma_start(scan_w[:, n, :, :], w[i].rearrange("(k p) f -> p k f", p=P)).then_inc(scan_in, 16)

        def scan_max(dve, i):
            dve.wait_ge(scan_in, 32 * i + 32)
            dve.wait_ge(k_zeroed, 2)
            dve.tensor_reduce(absmax[:, i, :] if isinstance(i, int) else
                              absmax[:, bass.ds(i, 1), :].rearrange("p a b -> p (a b)"),
                              scan_w[:, :, :, :].rearrange("p n k f -> p n (k f)"), AX.X, ALU.max,
                              apply_absolute_value=True).then_inc(scan_done, 1)

        router_stage = Router(nc, R, R_sems, lists, KT, NX)
        self_att = attention_stage(nc, ctx, "self", False, x, x, w_sb, mask, ident, ident16, psum, T, [x1],
                                   (w_ready, 0), scan_load, scan_max)
        cross_att = attention_stage(nc, ctx, "cross", True, x1, ctxt, w_sb, mask, ident, ident16, psum, T,
                                    [t[0:TOK, :].rearrange("(b p) d -> b p d", p=S) for t in (x2, acc)],
                                    (w_ready, 4), route=router_stage)
        pe_end_self, pe_end_cross = self_att[5]["pe"], cross_att[5]["pe"]

        def load_weights(eng, ws, w_in):
            for n, w in enumerate(ws):
                k = KT if n < 3 else E // P
                eng.dma_start(raw_w[n][:, :].rearrange("p (k n) -> p k n", k=k),
                              w.rearrange("(k p) n -> p k n", p=P)).then_inc(w_in[n], 16)

        def flat(t):
            return t[:, :, :].rearrange("p k n -> p (k n)")

        def split_hi(act, stage):
            for n in range(4):
                act.wait_ge(w_in[stage][n], 16)
                act.activation(flat(w_sb[2 * n]), raw_w[n][:, :], ACT.Copy,
                               scale=DH ** -0.5 if n == 0 else 1.0).then_inc(w_hi_done, 1)

        def split_lo(dve, stage, n):
            dve.wait_ge(w_hi_done, stage * 4 + n + 1)
            dve.scalar_tensor_tensor(flat(w_sb[2 * n + 1]), raw_w[n][:, :], DH ** -0.5 if n == 0 else 1.0,
                                     flat(w_sb[2 * n]).bitcast(F32), ALU.mult, ALU.subtract).then_inc(w_ready, 1)

        def experts2(t, e):
            return t[:, e, :, :].rearrange("p k n -> p (k n)")

        SPLIT_FIRST = 3
        LOOP = TILES // AHEAD

        def expert_steps(eng, step):
            for j in range(AHEAD):
                step(j, j)
            with eng.Fori(1, LOOP) as m:
                for c in range(AHEAD):
                    step(m * AHEAD + c, c)
            for j in range(LOOP * AHEAD, TILES):
                step(j, j % AHEAD)

        def within(j):
            return not isinstance(j, int) or j < TILES

        def splits_at(j):
            if not isinstance(j, int) or j >= AHEAD:
                return []
            e = SPLIT_FIRST + j
            return list(range(e, NX)) if j == AHEAD - 1 else [e]
        assert LOOP * AHEAD + 1 < TILES

        block = ctx.enter_context(nc.Block())

        @block.sync
        def _(sp):
            load_weights(sp, (a_wq, a_wk, a_wv, a_wo), w_in[0])
            sp.dma_start(R["wr"][:, :, :], router.rearrange("(k p) e -> p k e", p=P)).then_inc(wr_in, 16)
            self_att[0](sp)
            cross_att[0](sp)
            sp.wait_ge(*pe_end_cross)
            for e in range(NX):
                if e >= 2:
                    sp.wait_ge(raw_lo, 3 * (e - 1))
                for n, w in enumerate((w_gate, w_up, w_down)):
                    k = KT if n < 2 else FT
                    sp.dma_start(raw_x[e % 2][n][:, :].rearrange("p (k f) -> p k f", k=k),
                                 w[e].rearrange("(k p) f -> p k f", p=P)).then_inc(raw_in[e % 2], 16)
            sp.wait_ge(y_added, 16 * TILES)
            fin_src = acc[0:TOK, :].rearrange("(c t p) d -> c p t d", p=P, t=4)
            fin_dst = out.rearrange("b p d -> (b p) d").rearrange("(c t p) d -> c p t d", p=P, t=4)
            NC = NT // 4
            for c in range(NC + 1):
                if c < NC:
                    if c >= 2:
                        sp.wait_ge(f_done, 4 * (c - 1))
                    sp.dma_start(fin_in[c % 2][:, :, :], fin_src[c]).then_inc(f_in, 16)
                    sp.wait_ge(f_in, 16 * (c + 1))
                if c >= 1:
                    sp.wait_ge(f_done, 4 * c)
                    if c >= 2:
                        sp.wait_ge(f_out, 16 * (c - 1))
                    sp.dma_start(fin_dst[c - 1], fin_out[(c - 1) % 2][:, :, :]).then_inc(f_out, 16)
            sp.wait_ge(f_out, 16 * NC)

        @block.gpsimd
        def _(pool):
            pool.memset(ident[:, :], 0.0).then_inc(zeroed, 1)
            pool.memset(ident16[:, :], 0.0).then_inc(zeroed, 1)
            pool.memset(mask[:, :], 0.0).then_inc(zeroed, 1)
            pool.wait_ge(zeroed, 3)
            for m in (ident, ident16):
                pool.affine_select(out=m[:, :], in_=m[:, :], compare_op=ALU.not_equal, fill=1.0, base=0,
                                   pattern=[[-1, P]], channel_multiplier=1).then_inc(consts, 1)
            pool.wait_ge(consts, 2)
            n = 3
            for s in range(P // SEG):
                for r in range(P // SEG):
                    if r != s:
                        for h in range(2):
                            pool.memset(mask[s * SEG:(s + 1) * SEG, h * P + r * SEG:h * P + (r + 1) * SEG],
                                        MASKED).then_inc(zeroed, 1)
                            n += 1
                            pool.wait_ge(zeroed, n)
            both_heads = mask[:, :].rearrange("p (h t) -> p h t", t=P)
            for d in range(-(P // DIL) + 1, P // DIL):
                pool.affine_select(out=both_heads, in_=both_heads, compare_op=ALU.not_equal, fill=0.0, base=DIL * d,
                                   pattern=[[0, 2], [-1, P]], channel_multiplier=1).then_inc(zeroed, 1)
                n += 1
                pool.wait_ge(zeroed, n)
            pool.memset(T["minus_half"][:, :], -0.5).then_inc(consts, 1)
            pool.memset(T["eps"][:, :], EPS).then_inc(consts, 1)
            pool.wait_ge(consts, 4)
            pool.wait_ge(w_ready, 4)
            load_weights(pool, (c_wq, c_wk, c_wv, c_wo), w_in[1])
            n = 0
            for t, pattern, base, per_partition in (
                    (e_of[:, :], [[1, NX]], 0, 0), (R["tie"][:, :], [[-1, NX]], NX, 0),
                    (edges[:, :], [[P, NT]], 0, 0), (tile_no[:, :], [[1, TILES + 1]], 0, 0),
                    (first_place[:, :], [[TOK, NX]], 0, 0), (R["base"][:, :], [[TOK, NX]], 0, 0),
                    (first_col[:, :], [[NT, NX]], -COLS, 0), (slot[:, :, 1].bitcast(I32), [[0, COLS + 1]], TOK, 1),
                    (R["token_f"][:, :], [[P, PAIR]], -PAIR * P, 1)):
                pool.iota(t, pattern, base=base, channel_multiplier=per_partition,
                          allow_small_or_imprecise_dtypes=True).then_inc(tables_pool, 1)
                n += 1
                pool.wait_ge(tables_pool, n)
            for t, v in ((below[:, :, :], 1.0), (R["earlier"][:, :], 1.0), (R["ones16"][:, :], 1.0),
                         (zero_row[:, :], 0.0), (slot[:, :, 0], 0.0), (R["ones"][:, :], 1.0),
                         (R["pair_tokens"][:, :], float(PAIR * P)), (f_half[:, :], -0.5)):
                pool.memset(t, v).then_inc(tables_pool, 1)
                n += 1
                pool.wait_ge(tables_pool, n)
            pool.affine_select(out=below[:, :, :], in_=below[:, :, :], compare_op=ALU.is_gt, fill=0.0, base=0,
                               pattern=[[1, NX], [-1, NX]], channel_multiplier=0).then_inc(tables_pool, 1)
            pool.affine_select(out=R["earlier"][:, :], in_=R["earlier"][:, :], compare_op=ALU.is_gt, fill=0.0, base=0,
                               pattern=[[1, P]], channel_multiplier=-1).then_inc(tables_pool, 1)
            n += 2
            pool.wait_ge(tables_pool, n)
            pool.dma_start(lists.rearrange("(p j) c -> p j c", p=P), slot[:, 0:COLS, :]).then_inc(dispatched, 16)
            pool.dma_start(x2[TOK:TOK + P, :], zero_row[:, :]).then_inc(dispatched, 16)
            pool.dma_start(acc[TOK:TOK + P, :], zero_row[:, :]).then_inc(dispatched, 16)
            pool.wait_ge(dispatched, 48)
            pool.sem_inc(tables, 1)
            self_att[4](pool)
            pool.wait_ge(max_all, 1)
            pool.partition_all_reduce(wall[:, :], wmax[:, :], P, bass.bass_isa.ReduceOp.max).then_inc(max_all, 1)
            cross_att[4](pool)

            pool.wait_ge(dispatched, 32 * NT + 48)
            pool.dma_start(slot[:, 0:COLS, :], lists.rearrange("(p j) c -> p j c", p=P)).then_inc(slots_in, 16)
            pool.wait_ge(plan_ready, 1)
            pool.wait_ge(slots_in, 16)
            pool.wait_ge(*cross_att[5]["stored"])

            def step():
                pool.sem_inc(pool_step, 1)

            def gather(j, c):
                if not isinstance(j, int) or j >= AHEAD:
                    pool.wait_ge(xt_mm, j - AHEAD + 1)
                col = pool.value_load(col_i[0:1, bass.ds(j, 1)], min_val=0, max_val=COLS)
                pool.tensor_copy(get_tok[c][:, :], slot[:, bass.ds(col, 1), 1].bitcast(I32)).then_inc(get_ready, 1)
                pool.tensor_copy(get_w[c][:, :], slot[:, bass.ds(col, 1), 0]).then_inc(get_ready, 1)
                pool.wait_ge(get_ready, j * 2 + 2)
                step()
                pool.indirect_dma_start(out=xrow[c][:, :], out_offset=None, in_=x2,
                                        in_offset=bass.IndirectOffsetOnAxis(ap=get_tok[c][:, :], axis=0))\
                    .then_inc(x_gathered[c], 16)

            def put(j, c):
                if not isinstance(j, int) or j >= 2:
                    pool.wait_ge(y_added, 16 * (j - 1))
                    step()
                pool.tensor_copy(put_tok[c % 2][:, :], get_tok[c][:, :]).then_inc(put_ready, 1)
                pool.tensor_copy(put_w[c % 2][:, :], get_w[c][:, :]).then_inc(put_ready, 1)
                pool.wait_ge(put_ready, j * 2 + 2)

            def add_rows(j, s):
                if not isinstance(j, int) or j >= 1:
                    pool.wait_ge(y_added, 16 * j)
                pool.wait_ge(y_sb, j + 1)
                step()
                pool.indirect_dma_start(out=acc, out_offset=bass.IndirectOffsetOnAxis(ap=put_tok[s][:, :], axis=0),
                                        in_=yrow[s][:, :], in_offset=None, compute_op=ALU.add).then_inc(y_added, 16)

            for c in range(AHEAD):
                gather(c, c)

            def expert_step(j, c):
                put(j, c)
                if within(j + AHEAD if isinstance(j, int) else j):
                    gather(j + AHEAD, c)
                add_rows(j, c % 2)

            expert_steps(pool, expert_step)
            for c in range(NT // 4):
                pool.wait_ge(f_var, c + 1)
                pool.tensor_tensor(frstd[:, :], fvar[:, :], f_half[:, :], ALU.pow).then_inc(f_rstd, 1)

        @block.scalar
        def _(act):
            split_hi(act, 0)
            self_att[2](act)
            act.wait_ge(*pe_end_self)
            split_hi(act, 1)
            cross_att[2](act)
            act.wait_ge(*pe_end_cross)

            act.wait_ge(scale_ready, 1)

            def expert_hi(e):
                act.wait_ge(raw_in[e % 2], 48 * (e // 2 + 1))
                for n, w in enumerate((wg, wu)):
                    act.activation(experts2(w[0], e), raw_x[e % 2][n][:, :], ACT.Copy,
                                   scale=w_scale[:, n:n + 1]).then_inc(raw_hi, 1)
                act.activation(experts2(wd[0], e), raw_x[e % 2][2][:, :], ACT.Copy).then_inc(raw_hi, 1)

            def turn_x(j, s):
                act.wait_ge(xt_mm, j + 1)
                if not isinstance(j, int) or j >= 2:
                    act.wait_ge(u_mm, j - 1)
                act.activation(xt16[s][0][:, :, :].rearrange("p k t -> p (k t)"), xt_ps[s][:, 0:KT * P], ACT.Copy,
                               scale=X_SCALE).then_inc(xt_hi, 1)

            def silu(j, s):
                act.wait_ge(g_mm, j + 1)
                if not isinstance(j, int) or j >= 1:
                    act.wait_ge(hid_done, j)
                act.activation(gated[:, :], g_ps[s][:, :], ACT.Silu, scale=act_inv[:, 0:1]).then_inc(silu_done, 1)

            def turn_h(j):
                act.wait_ge(ht_mm, j + 1)
                if not isinstance(j, int) or j >= 1:
                    act.wait_ge(y_mm, j)
                act.activation(hidT[0][:, :, :].rearrange("p k t -> p (k t)"), ht_ps[:, :], ACT.Copy)\
                    .then_inc(ht_hi, 1)

            for e in range(SPLIT_FIRST):
                expert_hi(e)
            turn_x(0, 0)
            turn_x(1, 1)
            silu(0, 0)

            def expert_step(j, c):
                for e in splits_at(j):
                    expert_hi(e)
                turn_h(j)
                if within(j + 1):
                    silu(j + 1, (c + 1) % 2)
                if within(j + 2):
                    turn_x(j + 2, c % 2)

            expert_steps(act, expert_step)

        @block.vector
        def _(dve):
            for part in ("hi", "lo"):
                dve.memset(T[f"kT_{part}"][:, :, :, :, :, :].rearrange("p a c b h t -> p (a c b h t)").bitcast(F32),
                           0.0).then_inc(k_zeroed, 1)
            dve.wait_ge(k_zeroed, 2)
            for n in range(4):
                split_lo(dve, 0, n)
            self_att[3](dve)
            for n in range(4):
                split_lo(dve, 1, n)
            link = Chain(dve, chain, 0, 0).link

            dve.wait_ge(scan_done, NX)
            dve.tensor_reduce(wmax[:, :], absmax[:, :, :].rearrange("p e n -> p n e"), AX.X, ALU.max)\
                .then_inc(max_all, 1)
            dve.wait_ge(max_all, 2)
            link(dve.tensor_scalar(w_exp[:, :], wall[:, :], TINY, None, ALU.max))
            link(dve.tensor_single_scalar(w_inv[:, :].bitcast(I32), w_exp[:, :].bitcast(I32), 0x7F800000,
                                          ALU.bitwise_and))
            link(dve.tensor_scalar(w_exp[:, :], w_inv[:, :], W_TOP, None, ALU.mult))
            link(dve.tensor_scalar(act_inv[:, :], w_exp[:, :], 1.0 / X_SCALE, None, ALU.mult))
            dve.reciprocal(w_scale[:, :], w_exp[:, :]).then_inc(scale_ready, 1)
            cross_att[3](dve)
            dve.wait_ge(*pe_end_cross)

            TTs = dve.tensor_tensor
            dve.wait_ge(R_sems["ranks_ready"], NX)
            link(TTs(ntok[:, :], R["base"][:, :], first_place[:, :], ALU.subtract))
            link(TTs(cmp16[:, :, :], over(ntok[:, :], NT), under(edges[:, :], NX), ALU.is_gt))
            link(dve.tensor_reduce(some[:, :], cmp16[:, :, :], AX.X, ALU.add))
            link(dve.tensor_scalar(tiles_e[:, :], some[:, :], 1.0, None, ALU.max))
            link(TTs(cmp8[:, :, :], below[:, :, :], under(tiles_e[:, :], NX), ALU.mult))
            link(dve.tensor_reduce(cum0[:, :], cmp8[:, :, :], AX.X, ALU.add))
            link(TTs(cum1[:, :], cum0[:, :], tiles_e[:, :], ALU.add))
            link(TTs(offset[:, :], first_col[:, :], cum0[:, :], ALU.subtract))
            N = TILES + 1
            link(TTs(mine[:, :, :], over(tile_no[:, :], NX), under(cum0[:, :], N), ALU.is_ge))
            link(TTs(mine2[:, :, :], over(tile_no[:, :], NX), under(cum1[:, :], N), ALU.is_ge))
            link(TTs(mine[:, :, :], mine[:, :, :], mine2[:, :, :], ALU.subtract))
            link(TTs(mine2[:, :, :], mine[:, :, :], under(e_of[:, :], N), ALU.mult))
            link(dve.tensor_reduce(expert_f[:, :], mine2[:, :, :], AX.X, ALU.add))
            link(dve.tensor_copy(expert_i[:, :], expert_f[:, :]))
            link(TTs(mine2[:, :, :], over(tile_no[:, :], NX), under(offset[:, :], N), ALU.add))
            link(TTs(mine2[:, :, :], mine2[:, :, :], mine[:, :, :], ALU.mult))
            link(dve.tensor_reduce(col_f[:, :], mine2[:, :, :], AX.X, ALU.add))
            dve.tensor_scalar(col_i[:, :], col_f[:, :], float(COLS), None, ALU.add).then_inc(plan_ready, 1)

            def expert_lo(e):
                for n, w in enumerate((wg, wu)):
                    dve.wait_ge(raw_hi, 3 * e + n + 1)
                    dve.scalar_tensor_tensor(experts2(w[1], e), raw_x[e % 2][n][:, :], w_scale[:, n:n + 1],
                                             experts2(w[0], e), ALU.mult, ALU.subtract).then_inc(raw_lo, 1)
                dve.wait_ge(raw_hi, 3 * e + 3)
                TTs(experts2(wd[1], e), raw_x[e % 2][2][:, :], experts2(wd[0], e).bitcast(F32),
                    ALU.subtract).then_inc(raw_lo, 1)

            def turn_x(j, s):
                dve.wait_ge(xt_hi, j + 1)
                dve.scalar_tensor_tensor(xt16[s][1][:, :, :].rearrange("p k t -> p (k t)"), xt_ps[s][:, 0:KT * P],
                                         X_SCALE, xt16[s][0][:, :, :].rearrange("p k t -> p (k t)"),
                                         ALU.mult, ALU.subtract).then_inc(xt_lo, 1)

            def hidden(j, s):
                dve.wait_ge(u_mm, j + 1)
                dve.wait_ge(silu_done, j + 1)
                dve.scalar_tensor_tensor(hid[s][:, :], u_ps[s][:, :], act_inv[:, 1:2], gated[:, :],
                                         ALU.mult, ALU.mult).then_inc(hid_done, 1)

            def turn_h(j):
                dve.wait_ge(ht_hi, j + 1)
                TTs(hidT[1][:, :, :].rearrange("p k t -> p (k t)"), ht_ps[:, :],
                    hidT[0][:, :, :].rearrange("p k t -> p (k t)").bitcast(F32), ALU.subtract).then_inc(ht_lo, 1)

            def weigh(j, s):
                if not isinstance(j, int) or j >= 2:
                    dve.wait_ge(y_added, 16 * (j - 1))
                dve.wait_ge(y_mm, j + 1)
                dve.wait_ge(put_ready, j * 2 + 2)
                dve.tensor_scalar(yrow[s][:, :], y_ps[:, 0:D], put_w[s][:, :], None, ALU.mult).then_inc(y_sb, 1)

            for e in range(SPLIT_FIRST):
                expert_lo(e)
            turn_x(0, 0)
            turn_x(1, 1)
            hidden(0, 0)

            def expert_step(j, c):
                for e in splits_at(j):
                    expert_lo(e)
                turn_h(j)
                if within(j + 1):
                    hidden(j + 1, (c + 1) % 2)
                if within(j + 2):
                    turn_x(j + 2, c % 2)
                weigh(j, c % 2)

            expert_steps(dve, expert_step)

            for c in range(NT // 4):
                src = fin_in[c % 2]
                dve.wait_ge(f_in, 16 * (c + 1))
                for t in range(4):
                    dve.bn_stats(fbn[:, t, :], src[:, t, :]).then_inc(f_stats, 1)
                dve.wait_ge(f_stats, 4 * (c + 1))
                for t in range(4):
                    dve.bn_aggr(fmv[:, t, :], fbn[:, t, :]).then_inc(f_mom, 1)
                dve.wait_ge(f_mom, 4 * (c + 1))
                dve.tensor_scalar(fvar[:, :], fmv[:, :, 1], EPS, None, ALU.add).then_inc(f_var, 1)
                dve.wait_ge(f_rstd, c + 1)
                if c >= 2:
                    dve.wait_ge(f_out, 16 * (c - 1))
                for t in range(4):
                    dve.tensor_scalar(fin_out[c % 2][:, t, :], src[:, t, :], fmv[:, t, 0:1], frstd[:, t:t + 1],
                                      ALU.subtract, ALU.mult).then_inc(f_done, 1)

        @block.tensor
        def _(pe):
            pe.wait_ge(consts, 4)
            self_att[1](pe)
            pe.wait_ge(wr_in, 16)
            pe.wait_ge(tables, 1)
            cross_att[1](pe)
            pe.wait_ge(*cross_att[5]["dve"])
            pe.wait_ge(plan_ready, 1)

            def turn_x(j, c):
                pe.wait_ge(x_gathered[c], (j - c) * (16 // AHEAD) + 16)
                if not isinstance(j, int) or j >= 2:
                    pe.wait_ge(xt_lo, j - 1)
                for k in range(KT):
                    mm = pe.transpose(xt_ps[c % 2][:, k * P:(k + 1) * P], xrow[c][:, k * P:(k + 1) * P], ident[:, :])
                mm.then_inc(xt_mm, 1)

            def gate_up(j, s):
                e = pe.value_load(expert_i[0:1, bass.ds(j, 1)], min_val=0, max_val=NX - 1)
                pe.wait_ge(raw_lo, e * 3 + 3)
                pe.wait_ge(xt_lo, j + 1)
                for ps, w, done in ((g_ps[s], wg, g_mm), (u_ps[s], wu, u_mm)):
                    n = 0
                    for k in range(KT):
                        for xx, ww in terms(xt16[s][0], xt16[s][1], w[0], w[1]):
                            mm = pe.matmul(ps[:, :], xx[:, k, :], ww[:, bass.ds(e, 1), k, :].rearrange("p a f -> p (a f)"),
                                           start=(n == 0), stop=(n == 3 * KT - 1))
                            n += 1
                    mm.then_inc(done, 1)

            def turn_h(j, s):
                pe.wait_ge(hid_done, j + 1)
                for k in range(FT):
                    mm = pe.transpose(ht_ps[:, k * P:(k + 1) * P], hid[s][:, k * P:(k + 1) * P], ident[:, :])
                mm.then_inc(ht_mm, 1)

            def down(j):
                e = pe.value_load(expert_i[0:1, bass.ds(j, 1)], min_val=0, max_val=NX - 1)
                pe.wait_ge(ht_lo, j + 1)
                if not isinstance(j, int) or j >= 1:
                    pe.wait_ge(y_sb, j)
                n = 0
                for k in range(FT):
                    for hh, ww in terms(hidT[0], hidT[1], wd[0], wd[1]):
                        mm = pe.matmul(y_ps[:, 0:D], hh[:, k, :], ww[:, bass.ds(e, 1), k, :].rearrange("p a d -> p (a d)"),
                                       start=(n == 0), stop=(n == 3 * FT - 1))
                        n += 1
                mm.then_inc(y_mm, 1)

            turn_x(0, 0)
            turn_x(1, 1)
            gate_up(0, 0)

            def expert_step(j, c):
                turn_h(j, c % 2)
                if within(j + 1):
                    gate_up(j + 1, (c + 1) % 2)
                if within(j + 2):
                    turn_x(j + 2, (c + 2) % AHEAD)
                down(j)

            expert_steps(pe, expert_step)


_INS = ["x", "ctx_1024", "L0_attn_w_q", "L0_attn_w_k", "L0_attn_w_v", "L0_attn_w_o", "L0_xattn_Wq", "L0_xattn_Wk",
        "L0_xattn_Wv", "L0_xattn_Wo", "L0_ffn_router_kernel_DE", "L0_ffn_kernel_gating_EDF", "L0_ffn_kernel_up_EDF",
        "L0_ffn_kernel_down_EFD"]
_OUTS = [((16, 128, 256), "float32")]


def kernel(**inputs):
    import numpy as _np
    import concourse.bacc as _bacc
    from concourse import mybir as _mybir
    from concourse.bass_utils import run_bass_kernel_spmd as _run

    nc = _bacc.Bacc("TRN2", target_bir_lowering=False, num_devices=1)
    arrays, args = {}, []
    for name in _INS:
        a = _np.ascontiguousarray(inputs[name])
        arrays[f"in_{name}_dram"] = a
        args.append(nc.dram_tensor(f"in_{name}_dram", a.shape, _mybir.dt.from_np(a.dtype), kind="ExternalInput").ap())
    outs = []
    for i, (shape, dtype) in enumerate(_OUTS):
        dt = _mybir.dt.from_np(_np.dtype(dtype))
        outs.append(nc.dram_tensor(f"out_{i}_dram", shape, dt, kind="ExternalOutput").ap())
    build(nc, args, outs[0])
    r = _run(nc, [arrays], core_ids=[0])
    got = tuple(r.results[0][f"out_{i}_dram"] for i in range(len(_OUTS)))
    return got[0]
```

```python
from contextlib import ExitStack

import concourse.bass as bass
from concourse import mybir

ALU = mybir.AluOpType
ACT = mybir.ActivationFunctionType
AX = mybir.AxisListType
F32 = mybir.dt.float32
F32R = mybir.dt.float32r
BF16 = mybir.dt.bfloat16

P = 128
HEADS = 16
DH = 64
SEG = 64
DIL = 4
EPS = 1e-5
OUT_SLOT = 3
NORM_SLOT = 4
MASKED = -1e30
PAIR = 2
UNIT_HEADS = 4
GROUPS = HEADS // UNIT_HEADS
UNITS = GROUPS * PAIR
RING = 4
JOB_BANKS = {False: 2, True: 3}
CHUNKS = UNIT_HEADS // 2


def terms(hi_a, lo_a, hi_b, lo_b):
    return ((hi_a, hi_b), (hi_a, lo_b), (lo_a, hi_b))


class Count:

    def __init__(self, before, first, per):
        self.before, self.first, self.per = before, first, per

    def at(self, it, n):
        if isinstance(it, int) and it == 0:
            return self.before + n
        return it * self.per + (self.before + self.first - self.per + n)


def schedule(cross, first, last):
    slots = [[("Q", 1), ("K", 1)],
             [("V", 1, 0)],
             [("Q", 2)],
             [("K", 2)],
             [("Q", 3), ("V", 0, 1)],
             [("XT", 0), ("K", 3), ("YT", 0), ("V", 1, 1), ("XT", 1), ("LG", 0)] if cross else
             [("K", 3), ("V", 1, 1), ("XT", 0)],
             [("Q", 0)] + ([("RK", 0)] if cross else []),
             [("K", 0), ("V", 0, 0)]]
    slots[OUT_SLOT - 1] += [("OUT", 0)] if cross else []
    slots[OUT_SLOT] += [("OUT", 1)] if cross else [("OUT", None)]
    if first:
        slots = [[j for j in s if j[0] not in ("OUT", "YT", "LG", "RK")] for s in slots]
    if last:
        slots = [[j for j in s if j[0] != "XT" and (k < 6 or j[0] == "RK")] for k, s in enumerate(slots)]
    return slots


def banked(cross, slots):
    full = [j for s in schedule(cross, False, False) for j in s]
    return [[(j, full.index(j) % JOB_BANKS[cross]) for j in s] for s in slots]


def hi_ops(job):
    return {"K": 2, "OUT": 0, "YT": 0, "LG": 0, "RK": 0}.get(job[0], 1)


def attention_stage(nc, ctx, tag, cross, x_dram, kv_dram, w_sb, mask, ident, ident16, psum, sb_of, y_drams, w_ready,
                    each_pass_sync=None, each_pass_vector=None, route=None, hooks=None):
    NJ = JOB_BANKS[cross]
    NIT = x_dram.shape[0] // PAIR
    D = x_dram.shape[2]
    KT = D // P
    full = [j for s in schedule(cross, False, False) for j in s]
    JOBS = len(full)
    OUTS = len([j for j in full if j[0] == "OUT"])
    PRE = [("XT", 0)] + ([("XT", 1)] if cross else []) + [("Q", 0), ("K", 0), ("V", 0, 0)]
    HIS = sum(map(hi_ops, full))

    def sem(name):
        return ctx.enter_context(nc.semaphore(f"{tag}_{name}"))

    x_in, kv_in, res_in = sem("x_in"), sem("kv_in"), sem("res_in")
    job_mm, job_hi, job_free = sem("job_mm"), sem("job_hi"), sem("job_free")
    scores_ready, max_ready, exp_done = sem("scores_ready"), sem("max_ready"), sem("exp_done")
    recip_ready, probs_ready = sem("recip_ready"), sem("probs_ready")
    tr_done, pt_hi_done, pt_lo_done = sem("tr_done"), sem("pt_hi_done"), sem("pt_lo_done")
    pv_done, o_hi_done, o_lo_done = sem("pv_done"), sem("o_hi_done"), sem("o_lo_done")
    var_ready, stats_ready, moments_ready, rstd_ready, y_ready, y_stored = (
        sem("var_ready"), sem("stats_ready"), sem("moments_ready"), sem("rstd_ready"), sem("y_ready"), sem("y_stored"))

    ROUTED = [j for j in full if j[0] in ("YT", "LG", "RK")]
    C_job = Count(len(PRE), JOBS - OUTS - len(ROUTED), JOBS)
    C_hi = Count(sum(map(hi_ops, PRE)), HIS, HIS)
    C_unit = Count(0, UNITS, UNITS)

    T = sb_of
    wq_hi, wq_lo, wk_hi, wk_lo, wv_hi, wv_lo, wo_hi, wo_lo = w_sb
    job_bank, S, PT, OT = psum

    x_pairs = x_dram.rearrange("(i b) p d -> i p b d", b=PAIR)
    kv_pairs = kv_dram.rearrange("(i b) p d -> i p b d", b=PAIR)
    y_pairs = [y.rearrange("(i b) p d -> i p b d", b=PAIR) for y in y_drams]
    STORED = 16 * len(y_pairs)
    xT = [(T["xT_hi"], T["xT_lo"])]
    xT.append((T["cT_hi"], T["cT_lo"]) if cross else xT[0])
    raw = [T["x_raw"], T["c_raw"]]
    raw_in = [x_in, kv_in]

    def passes(emit, epilogue, eng):
        emit(0, True, False)
        with eng.Fori(1, NIT - 1) as it:
            emit(it, False, False)
        emit(NIT - 1, False, True)
        epilogue()

    def lagged(it, k, lag, first):
        if k >= lag:
            return [(it, k - lag)]
        return [] if first else [(it - 1, k - lag + UNITS)]

    def numbered(first, last):
        n, out = 0, []
        for s in banked(cross, schedule(cross, first, last)):
            row = []
            for job, bank in s:
                row.append((n, job, bank))
                n += 1
            out.append(row)
        return out

    def bank_history(first, last):
        pre = [(j, full.index(j) % NJ) for j in PRE]
        seen = {}
        for k, (j, b) in enumerate(pre):
            seen[b] = k - len(pre)
        if not first:
            for was_first in (True, False):
                rows = numbered(was_first, False)
                total = sum(map(len, rows))
                for row in rows:
                    for n, job, b in row:
                        seen[b] = max(seen[b], n - total)
        before = {}
        for row in numbered(first, last):
            for n, job, b in row:
                before[n] = seen[b]
                seen[b] = n
        return before

    def preload(sp):
        sp.dma_start(raw[0][:, :, :], x_pairs[0]).then_inc(x_in, 16)
        if cross:
            sp.dma_start(raw[1][:, :, :], kv_pairs[0]).then_inc(kv_in, 16)

    def sync_program(sp):
        def xt_jobs(i, first):
            return C_job.at(i, [n for row in numbered(first, False) for n, j, _ in row if j[0] == "XT"][-1] + 1)

        def load_x(i):
            sp.dma_start(raw[0][:, :, :], x_pairs[i]).then_inc(x_in, 16)
            if cross:
                sp.dma_start(raw[1][:, :, :], kv_pairs[i]).then_inc(kv_in, 16)

        def store_y_load_res(i):
            sp.wait_ge(y_ready, i * PAIR)
            for y in y_pairs:
                sp.dma_start(y[i - 1], T["y_out"][:, :, :]).then_inc(y_stored, 16)
            sp.wait_ge(y_stored, i * STORED)
            sp.dma_start(T["x_res"][:, :, :], x_pairs[i]).then_inc(res_in, 16)

        def also(i):
            if each_pass_sync is not None:
                each_pass_sync(sp, i)

        if not cross:
            preload(sp)
            hooks["sync_start"](sp)
        sp.dma_start(T["x_res"][:, :, :], x_pairs[0]).then_inc(res_in, 16)
        sp.wait_ge(job_mm, len([j for j in PRE if j[0] == "XT"]))
        load_x(1)
        sp.wait_ge(job_mm, xt_jobs(0, True))
        load_x(2)
        also(0)
        store_y_load_res(1)
        also(1)
        with sp.Fori(2, NIT - 1) as i:
            sp.wait_ge(job_mm, xt_jobs(i - 1, False))
            load_x(i + 1)
            store_y_load_res(i)
            also(i)
        store_y_load_res(NIT - 1)
        also(NIT - 1)
        if not cross:
            hooks["sync_end"](sp)
        sp.wait_ge(y_ready, NIT * PAIR)
        for y in y_pairs:
            sp.dma_start(y[NIT - 1], T["y_out"][:, :, :]).then_inc(y_stored, 16)
        sp.wait_ge(y_stored, NIT * STORED)

    def free_of(it, kind):
        rows = numbered(isinstance(it, int) and it == 0, isinstance(it, int) and it == NIT - 1)
        return C_job.at(it, [n for row in rows for n, j, _ in row if j[0] == kind][0] + 1)

    DONE = C_job.at(NIT - 1, JOBS - len(PRE))
    LAST_JOBS = [j for j in full if j[0] == "OUT"] + ROUTED

    def tensor_program(pe):
        weight_of = {("Q", 0): 1, ("K", 0): 2, ("V", 0, 0): 3, [j for j in full if j[0] == "OUT"][0]: 4}

        def job_matmuls(job, bank, it, xt_of):
            ps = job_bank[bank]
            kind = job[0]
            if job in weight_of:
                pe.wait_ge(w_ready[0], w_ready[1] + weight_of.pop(job))
            if kind == "XT":
                src, n = job[1], xt_of
                pe.wait_ge(raw_in[src], 16 * n + 16)
                for k in range(KT):
                    for b in range(PAIR):
                        mm = pe.transpose(ps[:, (k * PAIR + b) * P:(k * PAIR + b + 1) * P],
                                          raw[src][:, b, k * P:(k + 1) * P], ident[:, :])
                return mm
            if kind in "QK":
                g = job[1]
                w_hi, w_lo = (wq_hi, wq_lo) if kind == "Q" else (wk_hi, wk_lo)
                t_hi, t_lo = xT[0] if kind == "Q" else xT[1]
                for c in range(CHUNKS):
                    cols = slice((g * CHUNKS + c) * P, (g * CHUNKS + c + 1) * P)
                    n = 0
                    for k in range(KT):
                        for w, t in terms(w_hi, w_lo, t_hi, t_lo):
                            mm = pe.matmul(ps[:, c * PAIR * P:(c + 1) * PAIR * P], w[:, k, cols], t[:, k, :],
                                           start=(n == 0), stop=(n == 3 * KT - 1))
                            n += 1
                return mm
            if kind == "V":
                _, b, half = job
                t_hi, t_lo = xT[1]
                n = 0
                for k in range(KT):
                    for t, w in terms(t_hi, t_lo, wv_hi, wv_lo):
                        mm = pe.matmul(ps[:, :], t[:, k, b * P:(b + 1) * P], w[:, k, half * 512:(half + 1) * 512],
                                       start=(n == 0), stop=(n == 3 * KT - 1))
                        n += 1
                return mm
            if kind == "YT":
                for k in range(KT):
                    for b in range(PAIR):
                        mm = pe.transpose(ps[:, (k * PAIR + b) * P:(k * PAIR + b + 1) * P],
                                          T["y_out"][:, b, k * P:(k + 1) * P], ident[:, :])
                return mm
            if kind in ("LG", "RK"):
                return route.tensor(pe, kind, ps)
            bs = range(PAIR) if job[1] is None else [job[1]]
            NC = GROUPS * CHUNKS
            for at, b in enumerate(bs):
                n = 0
                for c in range(NC):
                    for o, w in terms(T["oT_hi"], T["oT_lo"], wo_hi, wo_lo):
                        mm = pe.matmul(ps[:, at * D:(at + 1) * D], o[:, c, b, :], w[:, c, :],
                                       start=(n == 0), stop=(n == 3 * NC - 1))
                        n += 1
            return mm

        def qk(it, k):
            g, b = divmod(k, PAIR)
            n_k = K_jobs(it)[g]
            if b == 0:
                pe.wait_ge(job_free, n_k)
            if not (isinstance(it, int) and it == 0 and k < 2):
                pe.wait_ge(exp_done, C_unit.at(it, k - 1))
            for c in range(CHUNKS):
                out = S[k % 2][:, c * 2 * P:(c + 1) * 2 * P]
                n = 0
                for q, kk in terms(T["qT_hi"], T["qT_lo"], T["kT_hi"], T["kT_lo"]):
                    mm = pe.matmul(out, q[:, g % 2, c, b, :],
                                   kk[:, g % 2, c, b, :, :].rearrange("p h t -> p (h t)"),
                                   start=(n == 0), stop=(n == 2 and cross))
                    n += 1
                if not cross:
                    mm = pe.matmul(out, ident16[:, :], mask[:, :], start=False, stop=True)
            mm.then_inc(scores_ready, 1)

        def K_jobs(it):
            first, last = (isinstance(it, int) and it == 0), (isinstance(it, int) and it == NIT - 1)
            out = {0: C_job.at(it, 0)}
            for row in numbered(first, last):
                for n, j, _ in row:
                    if j[0] == "K" and j[1]:
                        out[j[1]] = C_job.at(it, n + 1)
            return out

        def transposes(it, k):
            pe.wait_ge(probs_ready, C_unit.at(it, k + 1))
            if not (isinstance(it, int) and it == 0 and k < 2):
                pe.wait_ge(pt_lo_done, C_unit.at(it, k - 1))
            for h in range(UNIT_HEADS):
                mm = pe.transpose(PT[k % 2][:, h * P:(h + 1) * P], T["probs"][:, k % RING, h, :], ident[:, :])
            mm.then_inc(tr_done, 1)

        def pv(it, k):
            g, b = divmod(k % UNITS, PAIR)
            pe.wait_ge(pt_lo_done, C_unit.at(it, k + 1))
            if not (isinstance(it, int) and it == 0 and k < len(OT)):
                pe.wait_ge(o_lo_done, C_unit.at(it, k + 1 - len(OT)))
            if k in (0, 1, UNITS // 2, UNITS // 2 + 1):
                first, last = (isinstance(it, int) and it == 0), (isinstance(it, int) and it == NIT - 1)
                n = [n for row in numbered(first, last) for n, j, _ in row
                     if j == ("V", b, k // (UNITS // 2)) and k]
                pe.wait_ge(job_free, C_job.at(it, n[0] + 1 if n else 0))
            for c in range(CHUNKS):
                cols = slice((g * CHUNKS + c) * P, (g * CHUNKS + c + 1) * P)
                n = 0
                for v, p in terms(T["v_hi"], T["v_lo"], T["pT_hi"], T["pT_lo"]):
                    mm = pe.matmul(OT[k % len(OT)][:, c * 2 * P:(c + 1) * 2 * P], v[:, b, cols],
                                   p[:, k % 2, 2 * c:2 * c + 2, :].rearrange("p h t -> p (h t)"),
                                   start=(n == 0), stop=(n == 2))
                    n += 1
            mm.then_inc(pv_done, 1)

        def run_job(it, n, job, bank, before, pre_xt=None):
            if before is not None:
                pe.wait_ge(job_free, C_job.at(it, before + 1))
            if job[0] == "OUT":
                pe.wait_ge(o_lo_done, C_unit.at(it, -1 if job[1] == 0 else 0))
            if job == ("Q", 0):
                pe.wait_ge(job_free, C_job.at(it, n))
            if job[0] == "YT":
                pe.wait_ge(y_ready, it * PAIR)
            if job[0] == "LG":
                pe.wait_ge(job_free, free_of(it, "YT"))
            if job[0] == "RK":
                route.tensor_wait(pe, it - 1)
            xt = None
            if job[0] == "XT":
                xt = 0 if pre_xt is not None else it + 1
            job_matmuls(job, bank, it, xt).then_inc(job_mm, 1)

        hist = {}
        for k, job in enumerate(PRE):
            bank = full.index(job) % NJ
            if bank in hist:
                pe.wait_ge(job_free, hist[bank] + 1)
            if job == ("Q", 0):
                pe.wait_ge(job_free, k)
            hist[bank] = k
            job_matmuls(job, bank, 0, 0).then_inc(job_mm, 1)

        def one_pass(it, first, last):
            before = bank_history(first, last)
            for k, row in enumerate(numbered(first, last)):
                qk(it, k)
                outs = [r for r in row if r[1][0] == "OUT"]
                for n, job, bank in row:
                    if job[0] != "OUT":
                        run_job(it, n, job, bank, before[n])
                for u in lagged(it, k, 2, first):
                    transposes(*u)
                for n, job, bank in outs:
                    run_job(it, n, job, bank, before[n])
                for u in lagged(it, k, 3, first):
                    pv(*u)

        def finish():
            last = NIT - 1
            transposes(last, UNITS - 2)
            pv(last, UNITS - 3)
            transposes(last, UNITS - 1)
            pv(last, UNITS - 2)
            pv(last, UNITS - 1)
            for k, j in enumerate(LAST_JOBS):
                pe.wait_ge(job_free, DONE + (0 if j[0] == "OUT" else k))
                if j[0] == "OUT":
                    pe.wait_ge(o_lo_done, UNITS * NIT)
                if j[0] == "YT":
                    pe.wait_ge(y_ready, NIT * PAIR)
                if j[0] == "RK":
                    route.tensor_wait(pe, last)
                job_matmuls(j, k % NJ, last, None).then_inc(job_mm, 1)

        passes(one_pass, finish, pe)

    def k_views(ps, half):
        rows = slice(half * DH, (half + 1) * DH)
        return rows, ps[rows, :].rearrange("p (c t) -> p c t", t=P)

    def job_dst(job):
        kind = job[0]
        if kind == "XT":
            hi, lo = xT[job[1]]
            return hi[:, :, :].rearrange("p k t -> p (k t)"), lo[:, :, :].rearrange("p k t -> p (k t)")
        if kind == "Q":
            return [t[:, job[1] % 2, :, :, :].rearrange("p c b t -> p (c b t)") for t in (T["qT_hi"], T["qT_lo"])]
        if kind == "V":
            _, b, half = job
            return [t[:, b, half * 512:(half + 1) * 512] for t in (T["v_hi"], T["v_lo"])]
        g = job[1]
        return [[t[h * DH:(h + 1) * DH, g % 2, :, :, h, :].rearrange("p c b t -> p (c b) t") for h in range(2)]
                for t in (T["kT_hi"], T["kT_lo"])]

    def scalar_program(act):
        def job_part(job, bank, number, it):
            if not hi_ops(job):
                return
            act.wait_ge(job_mm, number)
            ps = job_bank[bank]
            hi = job_dst(job)[0]
            if job[0] == "K":
                for h in range(2):
                    rows, src = k_views(ps, h)
                    act.activation(hi[h], src, ACT.Copy).then_inc(job_hi, 1)
            else:
                act.activation(hi, ps[:, :], ACT.Copy).then_inc(job_hi, 1)

        def exp(it, k):
            act.wait_ge(max_ready, C_unit.at(it, k + 1))
            if not (isinstance(it, int) and it == 0 and k < RING):
                act.wait_ge(tr_done, C_unit.at(it, k - RING + 1))
            for h in range(UNIT_HEADS):
                a = act.activation(T["probs"][:, k % RING, h, :], S[k % 2][:, h * P:(h + 1) * P], ACT.Exp,
                                   bias=T["neg_max"][:, k % RING, h:h + 1],
                                   accum_out=T["row_sum"][:, k % RING, h:h + 1])
            a.then_inc(exp_done, 1)

        def pt_hi(it, k):
            act.wait_ge(tr_done, C_unit.at(it, k + 1))
            if not (isinstance(it, int) and it == 0 and k < 2):
                act.wait_ge(pv_done, C_unit.at(it, k - 1))
            act.activation(T["pT_hi"][:, k % 2, :, :].rearrange("p h t -> p (h t)"), PT[k % 2][:, :],
                           ACT.Copy).then_inc(pt_hi_done, 1)

        def o_hi(it, k):
            g, b = divmod(k, PAIR)
            act.wait_ge(pv_done, C_unit.at(it, k + 1))
            src = OT[k % len(OT)][:, :].rearrange("p (c h t) -> p c h t", c=CHUNKS, h=2)
            for h in range(2):
                rows = slice(h * DH, (h + 1) * DH)
                act.activation(T["oT_hi"][rows, g * CHUNKS:(g + 1) * CHUNKS, b, :], src[rows, :, h, :],
                               ACT.Copy).then_inc(o_hi_done, 1)

        for k, job in enumerate(PRE):
            hooks["scalar_before"](act, job)
            job_part(job, full.index(job) % NJ, k + 1, 0)
        hooks["scalar_before"](act, None)

        def one_pass(it, first, last):
            for k, row in enumerate(numbered(first, last)):
                for u in lagged(it, k, 1, first):
                    exp(*u)
                for u in lagged(it, k, 4, first):
                    o_hi(*u)
                for n, job, bank in row:
                    job_part(job, bank, C_job.at(it, n + 1), it)
                for u in lagged(it, k, 2, first):
                    pt_hi(*u)
                if route is not None and not first:
                    route.scalar(act, k, it - 1)

        def finish():
            last = NIT - 1
            exp(last, UNITS - 1)
            o_hi(last, UNITS - 4)
            pt_hi(last, UNITS - 2)
            o_hi(last, UNITS - 3)
            pt_hi(last, UNITS - 1)
            o_hi(last, UNITS - 2)
            o_hi(last, UNITS - 1)
            hooks["scalar_end"](act)
            if route is not None:
                for k in (6, 7):
                    route.scalar(act, k, last)

        passes(one_pass, finish, act)

    def vector_program(dve):
        def job_lo(job, bank, his):
            ps = job_bank[bank]
            dve.wait_ge(job_hi, his)
            hi, lo = job_dst(job)
            if job[0] == "K":
                for h in range(2):
                    rows, src = k_views(ps, h)
                    v = dve.tensor_tensor(lo[h], src, hi[h].bitcast(F32), ALU.subtract)
                v.then_inc(job_free, 1)
            else:
                dve.tensor_tensor(lo, ps[:, :], hi.bitcast(F32), ALU.subtract).then_inc(job_free, 1)

        def out_part(job, bank, jobs_done, pair):
            bs = list(range(PAIR)) if job[1] is None else [job[1]]
            dve.wait_ge(job_mm, jobs_done)
            dve.wait_ge(res_in, 16 * pair + 16)
            dve.tensor_tensor(T["y_sum"][:, bs[0]:bs[-1] + 1, :],
                              job_bank[bank][:, 0:len(bs) * D].rearrange("p (b d) -> p b d", d=D),
                              T["x_res"][:, bs[0]:bs[-1] + 1, :], ALU.add).then_inc(job_free, 1)

        def row_stats():
            for b in range(PAIR):
                dve.bn_stats(T["bn"][:, b, :], T["y_sum"][:, b, :]).then_inc(stats_ready, 1)

        def moments():
            for b in range(PAIR):
                dve.bn_aggr(T["mv"][:, b, :], T["bn"][:, b, :]).then_inc(moments_ready, 1)

        def normalise(pair):
            dve.wait_ge(rstd_ready, pair + 1)
            for b in range(PAIR):
                dve.tensor_scalar(T["y_out"][:, b, :], T["y_sum"][:, b, :], T["mv"][:, b, 0:1], T["rstd"][:, b:b + 1],
                                  ALU.subtract, ALU.mult).then_inc(y_ready, 1)

        def neg_max(it, k):
            dve.wait_ge(scores_ready, C_unit.at(it, k + 1))
            dve.tensor_reduce(T["neg_max"][:, k % RING, :], S[k % 2][:, :].rearrange("p (h t) -> p h t", t=P),
                              AX.X, ALU.max, negate=True).then_inc(max_ready, 1)

        def recip(it, k):
            dve.wait_ge(exp_done, C_unit.at(it, k + 1))
            if not (isinstance(it, int) and it == 0 and k < RING):
                dve.wait_ge(probs_ready, C_unit.at(it, k - RING + 1))
            dve.reciprocal(T["row_inv"][:, k % RING, :], T["row_sum"][:, k % RING, :]).then_inc(recip_ready, 1)

        def pt_lo(it, k):
            dve.wait_ge(pt_hi_done, C_unit.at(it, k + 1))
            dve.tensor_tensor(T["pT_lo"][:, k % 2, :, :].rearrange("p h t -> p (h t)"), PT[k % 2][:, :],
                              T["pT_hi"][:, k % 2, :, :].rearrange("p h t -> p (h t)").bitcast(F32),
                              ALU.subtract).then_inc(pt_lo_done, 1)

        def o_lo(it, k):
            g, b = divmod(k, PAIR)
            dve.wait_ge(o_hi_done, C_unit.at(it, k + 1) * 2)
            src = OT[k % len(OT)][:, :].rearrange("p (c h t) -> p c h t", c=CHUNKS, h=2)
            for h in range(2):
                rows = slice(h * DH, (h + 1) * DH)
                v = dve.tensor_tensor(T["oT_lo"][rows, g * CHUNKS:(g + 1) * CHUNKS, b, :], src[rows, :, h, :],
                                      T["oT_hi"][rows, g * CHUNKS:(g + 1) * CHUNKS, b, :].bitcast(F32), ALU.subtract)
            v.then_inc(o_lo_done, 1)

        his = 0
        for k, job in enumerate(PRE):
            hooks["vector_before"](dve, job)
            his += hi_ops(job)
            job_lo(job, full.index(job) % NJ, his)
        hooks["vector_before"](dve, None)

        def one_pass(it, first, last):
            his = 0
            for k, row in enumerate(numbered(first, last)):
                if k == OUT_SLOT + 1 and not first:
                    dve.wait_ge(stats_ready, it * PAIR)
                neg_max(it, k)
                if k == OUT_SLOT + 1 and not first:
                    moments()
                for u in lagged(it, k, 4, first):
                    o_lo(*u)
                for u in lagged(it, k, 1, first):
                    recip(*u)
                if route is not None and not first and k == UNITS - 1:
                    route.vector_slots(dve, it - 1)
                for n, job, bank in row:
                    his += hi_ops(job)
                    if job in ROUTED:
                        dve.wait_ge(job_mm, C_job.at(it, n + 1))
                        route.vector_job(dve, job[0], job_bank[bank]).then_inc(job_free, 1)
                    elif job[0] != "OUT":
                        job_lo(job, bank, C_hi.at(it, his))
                for u in lagged(it, k, 2, first):
                    pt_lo(*u)
                if k == 5 and route is not None and not first:
                    route.vector_pick(dve, it - 1, job_free, free_of(it, "LG"))
                if k == UNITS - 1 and each_pass_vector is not None:
                    each_pass_vector(dve, it)
                outs = [r for r in row if r[1][0] == "OUT"]
                for n, job, bank in outs:
                    out_part(job, bank, C_job.at(it, n + 1), it - 1)
                if outs and k == OUT_SLOT:
                    ln_start(it)
                    row_stats()
                if k == NORM_SLOT and not first:
                    normalise(it - 1)
                if route is not None and not first and k == UNITS - 1:
                    route.vector_weights(dve, it - 1)

        def ln_start(it):
            dve.wait_ge(job_free, ln_count(it))

        def ln_count(it):
            first, last = False, (isinstance(it, int) and it == NIT - 1)
            n = [n for row in numbered(first, last) for n, j, _ in row if j[0] == "OUT"][-1]
            return C_job.at(it, n + 1)

        def finish():
            last = NIT - 1
            recip(last, UNITS - 1)
            o_lo(last, UNITS - 4)
            pt_lo(last, UNITS - 2)
            o_lo(last, UNITS - 3)
            pt_lo(last, UNITS - 1)
            o_lo(last, UNITS - 2)
            o_lo(last, UNITS - 1)
            if not cross:
                hooks["vector_end"](dve)
            for k, j in enumerate(LAST_JOBS[:OUTS]):
                out_part(j, k % NJ, DONE + k + 1, last)
            dve.wait_ge(job_free, DONE + OUTS)
            row_stats()
            dve.wait_ge(stats_ready, NIT * PAIR)
            moments()
            normalise(last)
            for k, j in enumerate(LAST_JOBS):
                if j in ROUTED:
                    dve.wait_ge(job_mm, DONE + k + 1)
                    route.vector_job(dve, j[0], job_bank[k % NJ]).then_inc(job_free, 1)
                    if j[0] == "LG":
                        route.vector_pick(dve, last, job_free, DONE + k + 1)
            if route is not None:
                route.vector_slots(dve, last)
                route.vector_weights(dve, last)

        passes(one_pass, finish, dve)

    def gpsimd_program(pool):
        def normalise_probs(it, k):
            pool.wait_ge(recip_ready, C_unit.at(it, k + 1))
            p = T["probs"][:, k % RING, :, :]
            pool.tensor_tensor(p, p, T["row_inv"][:, k % RING, :].unsqueeze(2).to_broadcast([P, UNIT_HEADS, P]),
                               ALU.mult).then_inc(probs_ready, 1)

        def rstd(pair):
            pool.wait_ge(moments_ready, pair * PAIR + PAIR)
            pool.tensor_tensor(T["var_eps"][:, :], T["mv"][:, :, 1], T["eps"][:, :], ALU.add).then_inc(var_ready, 1)
            pool.wait_ge(var_ready, pair + 1)
            pool.tensor_tensor(T["rstd"][:, :], T["var_eps"][:, :], T["minus_half"][:, :], ALU.pow)\
                .then_inc(rstd_ready, 1)

        def one_pass(it, first, last):
            for k in range(UNITS):
                if k == OUT_SLOT + 1 and not first:
                    rstd(it - 1)
                for u in lagged(it, k, 1, first):
                    normalise_probs(*u)
                if route is not None and not first:
                    if k == 0:
                        route.send(pool, it)
                    route.gpsimd(pool, k, it - 1, job_free, free_of(it, "RK"))

        def finish():
            normalise_probs(NIT - 1, UNITS - 1)
            if route is not None:
                route.send(pool, NIT)
            rstd(NIT - 1)
            if route is not None:
                for k in (5, 6):
                    route.gpsimd(pool, k, NIT - 1, job_free, DONE + OUTS + 3)
                route.send(pool, NIT + 1)

        passes(one_pass, finish, pool)

    finals = {"pe": (job_mm, DONE + len(LAST_JOBS)), "dve": (job_free, DONE + len(LAST_JOBS)),
              "stored": (y_stored, NIT * STORED), "projected": (job_mm, DONE), "out": (job_mm, DONE + OUTS)}
    return sync_program, tensor_program, scalar_program, vector_program, gpsimd_program, finals, preload


class Chain:

    def __init__(self, eng, sem, per, pair, steps=None):
        self.eng, self.sem, self.start, self.per, self.n, self.steps = eng, sem, pair * per, per, 0, steps

    def link(self, ins):
        self.n += 1
        ins.then_inc(self.sem, 1)
        self.eng.wait_ge(self.sem, self.start + self.n)

    def step(self):
        self.eng.sem_inc(self.steps, 1)

    def end(self):
        assert self.n == self.per, self.n


def over(t, n):
    return t.unsqueeze(2).to_broadcast([P, t.shape[1], n])


def under(t, m):
    return t.unsqueeze(1).to_broadcast([P, m, t.shape[1]])


class Router:
    POOL_LINKS = 6
    DVE_LINKS = 10

    def __init__(self, nc, R, sems, lists, KT, NX):
        self.nc, self.R, self.s, self.lists, self.KT, self.NX = nc, R, sems, lists, KT, NX

    def tensor_wait(self, pe, pair):
        pe.wait_ge(self.s["picked"], pair + 1)

    def tensor(self, pe, kind, ps):
        R, NX = self.R, self.NX
        if kind == "LG":
            for b in range(PAIR):
                for k in range(self.KT):
                    mm = pe.matmul(ps[:, b * NX:(b + 1) * NX], R["yT"][:, k * PAIR + b, :], R["wr"][:, k, :],
                                   start=(k == 0), stop=(k == self.KT - 1))
            return mm
        for b in range(PAIR):
            out = ps[:, b * NX:(b + 1) * NX]
            pe.matmul(out, R["earlier"][:, :], R["both16"][:, b, :], start=True, stop=(b == 0))
            for a in range(b):
                pe.matmul(out, R["ones16"][:, :], R["both16"][:, a, :], start=False, stop=(a == b - 1))
        for a in range(PAIR):
            mm = pe.matmul(ps[:, PAIR * NX:(PAIR + 1) * NX], R["ones16"][:, :], R["both16"][:, a, :],
                           start=(a == 0), stop=(a == PAIR - 1))
        return mm

    def vector_job(self, dve, kind, ps):
        R, NX = self.R, self.NX
        if kind == "YT":
            return dve.tensor_copy(R["yT"][:, :, :].rearrange("p k t -> p (k t)"), ps[:, :])
        if kind == "LG":
            return dve.tensor_copy(R["lg"][:, :, :].rearrange("p t e -> p (t e)"), ps[:, 0:PAIR * NX])
        return dve.tensor_copy(R["ranks"][:, :], ps[:, 0:(PAIR + 1) * NX])

    def vector_pick(self, dve, pair, job_free, logits):
        R, NX, s = self.R, self.NX, self.s
        """Ones at the experts of each token's two largest logits."""
        self.dchain = chain = Chain(dve, s["dve_chain"], self.DVE_LINKS, pair, s["dve_step"])
        dve.wait_ge(job_free, logits)
        chain.step()
        for t in range(PAIR):
            m = dve.max(R["top"][:, t, :], R["lg"][:, t, :])
        chain.link(m)
        chain.step()
        for t in range(PAIR):
            m = dve.max_index(R["index"][:, t, :], R["top"][:, t, :], R["lg"][:, t, :])
        chain.link(m)
        for w in range(2):
            m = dve.tensor_tensor(R["one"][:, w, :, :], under(R["e_of"][:, :], PAIR), over(R["index"][:, :, w], NX),
                                  ALU.is_equal)
        chain.link(m)
        dve.tensor_tensor(R["both16"][:, :, :], R["one"][:, 0, :, :], R["one"][:, 1, :, :], ALU.add)\
            .then_inc(s["picked"], 1)

    def gpsimd(self, pool, slot, pair, job_free, ranks):
        R, NX, s = self.R, self.NX, self.s
        TT = pool.tensor_tensor
        if slot == 5:
            self.chain = Chain(pool, s["pool_chain"], self.POOL_LINKS, pair, s["pool_step"])
            pool.wait_ge(s["picked"], pair + 1)
            top = R["top"]
            TT(R["less"][:, :, :], top[:, :, :], over(top[:, :, 0], NX), ALU.subtract).then_inc(s["exp1_in"], 1)
        if slot == 6:
            chain, link = self.chain, self.chain.link
            pool.wait_ge(s["exp1"], pair + 1)
            link(TT(R["drop"][:, :], R["exps"][:, :, 1], R["ones"][:, :], ALU.subtract))
            pool.sem_inc(s["sums_ready"], 1)
            pool.wait_ge(job_free, ranks)
            link(TT(R["rank"][:, :, :], R["ranks"][:, 0:PAIR * NX].rearrange("p (t e) -> p t e", e=NX),
                    under(R["base"][:, :], PAIR), ALU.add))
            link(TT(R["base"][:, :], R["base"][:, :], R["ranks"][:, PAIR * NX:(PAIR + 1) * NX], ALU.add))
            for w in range(2):
                m = TT(R["mine_of"][:, w, :, :], R["one"][:, w, :, :], R["rank"][:, :, :], ALU.mult)
            link(m)
            pool.wait_ge(s["dispatched"], (pair + 1) * (32 * PAIR) + 48)
            link(TT(R["token_f"][:, :], R["token_f"][:, :], R["pair_tokens"][:, :], ALU.add))
            chain.step()
            for w in range(2):
                m = pool.tensor_copy(R["meta"][:, w, :, 1].bitcast(mybir.dt.int32), R["token_f"][:, :])
            link(m)
            pool.sem_inc(s["ranks_ready"], 1)
            self.chain.end()

    def send(self, pool, n):
        R, s = self.R, self.s
        pool.wait_ge(s["slots_ready"], n)
        pool.wait_ge(s["wt_ready"], n)
        pool.sem_inc(s["pool_step"], 1)
        for w in range(2):
            for t in range(PAIR):
                pool.indirect_dma_start(out=self.lists, out_offset=bass.IndirectOffsetOnAxis(
                    ap=R["place_i"][:, w * PAIR + t:w * PAIR + t + 1], axis=0), in_=R["meta"][:, w, t, :],
                    in_offset=None).then_inc(s["dispatched"], 16)

    def scalar(self, act, slot, pair):
        R, s = self.R, self.s
        if slot == 6:
            act.wait_ge(s["exp1_in"], pair + 1)
            act.activation(R["exps"][:, :, :], R["less"][:, :, :], ACT.Exp).then_inc(s["exp1"], 1)
        if slot == 7:
            act.wait_ge(s["exp2_in"], pair + 1)
            act.activation(R["exp2"][:, :], R["diff"][:, :], ACT.Exp).then_inc(s["exp2"], 1)

    def vector_slots(self, dve, pair):
        R, s = self.R, self.s
        link = self.dchain.link
        dve.wait_ge(s["sums_ready"], pair + 1)
        link(dve.tensor_reduce(R["sum"][:, :], R["exps"][:, :, :], AX.X, ALU.add))
        link(dve.reciprocal(R["inv"][:, :], R["sum"][:, :]))
        dve.tensor_tensor(R["diff"][:, :], R["drop"][:, :], R["inv"][:, :], ALU.mult).then_inc(s["exp2_in"], 1)
        dve.wait_ge(s["ranks_ready"], pair + 1)
        link(dve.tensor_reduce(R["place_f"][:, :], R["mine_of"][:, :, :, :].rearrange("p w t e -> p (w t) e"),
                               AX.X, ALU.add))
        link(dve.tensor_copy(R["place_i"][:, :], R["place_f"][:, :]))
        dve.tensor_scalar(R["column"][:, :], R["place_i"][:, :], 7, None, ALU.logical_shift_right)\
            .then_inc(s["dve_parts"], 1)
        dve.tensor_scalar(R["row"][:, :], R["place_i"][:, :], P - 1, 7, ALU.bitwise_and, ALU.logical_shift_left)\
            .then_inc(s["dve_parts"], 1)
        dve.wait_ge(s["dve_parts"], pair * 2 + 2)
        dve.tensor_tensor(R["place_i"][:, :], R["row"][:, :], R["column"][:, :], ALU.bitwise_or).then_inc(s["slots_ready"], 1)

    def vector_weights(self, dve, pair):
        R, s = self.R, self.s
        link = self.dchain.link
        dve.wait_ge(s["exp2"], pair + 1)
        link(dve.tensor_scalar(R["inv"][:, :], R["exp2"][:, :], 1.0, None, ALU.add))
        link(dve.reciprocal(R["meta"][:, 0, :, 0], R["inv"][:, :]))
        link(dve.tensor_tensor(R["meta"][:, 1, :, 0], R["exp2"][:, :], R["meta"][:, 0, :, 0], ALU.mult))
        dve.sem_inc(s["wt_ready"], 1)
        self.dchain.end()


WEIGHT_NAMES = ("wq", "wk", "wv", "wo")
X_SCALE = 256.0
W_TOP = 2.0 ** -13
TINY = 2.0 ** -100


def build(nc, args, out):
    (x, ctxt, a_wq, a_wk, a_wv, a_wo, c_wq, c_wk, c_wv, c_wo, router, w_gate, w_up, w_down) = args
    B, S, D = x.shape
    KT = D // P
    E = HEADS * DH
    NX, _, F = w_gate.shape
    FT = F // P
    TOK = B * S
    NT = TOK // P
    TILES = (2 * TOK) // P + NX - 1
    AHEAD = 4
    META = 2
    H16 = mybir.dt.float16
    I32 = mybir.dt.int32
    assert B // PAIR == NX and P == S

    x1 = nc.dram_tensor("x1_scratch", (B, S, D), F32).ap()
    x2 = nc.dram_tensor("x2_scratch", (TOK + P, D), F32).ap()
    acc = nc.dram_tensor("acc_scratch", (TOK + P, D), F32).ap()
    COLS = NX * NT
    lists = nc.dram_tensor("lists_scratch", (P * (COLS + 2 * PAIR), META), F32).ap()

    with ExitStack() as ctx:
        def sb(name, shape, dt=F32, stack=ctx):
            return stack.enter_context(nc.sbuf_tensor(name, shape, dt))

        def sem(name):
            return ctx.enter_context(nc.semaphore(name))

        T = {}
        for n in ("x_raw", "c_raw", "x_res", "y_sum", "y_out"):
            T[n] = sb(n, [P, PAIR, D])
        T["neg_max"] = sb("neg_max", [P, RING, UNIT_HEADS])
        T["row_sum"] = sb("row_sum", [P, RING, UNIT_HEADS])
        T["row_inv"] = sb("row_inv", [P, RING, UNIT_HEADS])
        T["bn"] = sb("bn", [P, PAIR, 6])
        T["mv"] = sb("mv", [P, PAIR, 2])
        for n in ("rstd", "var_eps", "minus_half", "eps"):
            T[n] = sb(n, [P, PAIR])
        ident = sb("ident", [P, P])
        ident16 = sb("ident16", [P, P], BF16)
        mask = sb("mask", [P, 2 * P], BF16)
        absmax = sb("absmax", [P, NX, 2])

        def table(name, *shape, dt=F32, stack=ctx):
            return sb(name, [P, *shape], dt, stack)

        e_of = table("e_of", NX)
        below = table("below", NX, NX)
        edges = table("edges", NT)
        tile_no = table("tile_no", TILES + 1)
        first_place = table("first_place", NX)
        first_col = table("first_col", NX)
        zero_row = table("zero_row", D)
        slot = table("slot_meta", COLS + 1, META)
        R = {"wr": table("router_w", KT, NX), 
             "earlier": table("earlier", P, dt=BF16), "ones16": table("ones16", P, dt=BF16),
             "ones": table("ones", PAIR), "pair_tokens": table("pair_tokens", PAIR), "base": table("base", NX),
             "token_f": table("token_f", PAIR), "yT": table("yT", KT * PAIR, P), "lg": table("lg", PAIR, NX),
             "top": table("top", PAIR, NX), "index": table("index", PAIR, NX, dt=mybir.dt.uint32), "e_of": e_of,
             "one": table("one", 2, PAIR, NX),
             "both16": table("both16", PAIR, NX, dt=BF16), "less": table("less", PAIR, NX),
             "exps": table("exps", PAIR, NX), "drop": table("drop", PAIR), "sum": table("sum", PAIR),
             "inv": table("inv", PAIR), "diff": table("diff", PAIR), "exp2": table("exp2", PAIR),
             "ranks": table("ranks", (PAIR + 1) * NX), "rank": table("rank", PAIR, NX),
             "mine_of": table("mine_of", 2, PAIR, NX), "place_f": table("place_f", 2 * PAIR),
             "place_i": table("place_i", 2 * PAIR, dt=I32), "column": table("column", 2 * PAIR, dt=I32),
             "row": table("row", 2 * PAIR, dt=I32), "meta": table("meta", 2, PAIR, META)}
        ntok, some, tiles_e, cum0, cum1, offset = (table(n, NX) for n in (
            "ntok", "some", "tiles_e", "cum0", "cum1", "offset"))
        cmp16 = table("cmp16", NX, NT)
        cmp8 = table("cmp8", NX, NX)
        expert_f, col_f = table("expert_f", TILES + 1), table("col_f", TILES + 1)
        expert_i, col_i = table("expert_i", TILES + 1, dt=I32), table("col_i", TILES + 1, dt=I32)
        get_tok = [table(f"get_tok{i}", 1, dt=I32) for i in range(AHEAD)]
        get_w = [table(f"get_w{i}", 1) for i in range(AHEAD)]
        put_tok = [table(f"put_tok{i}", 1, dt=I32) for i in range(2)]
        put_w = [table(f"put_w{i}", 1) for i in range(2)]
        wmax, wall, w_exp, w_inv, w_scale, act_inv = (table(n, 2) for n in (
            "wmax", "wall", "w_exp", "w_inv", "w_scale", "act_inv"))
        fbn, fmv = table("fbn", NT, 6), table("fmv", NT, 2)
        fvar, frstd, fshift, f_half = (table(n, NT) for n in ("fvar", "frstd", "fshift", "f_half"))

        att = ExitStack()
        for n in ("xT", "cT"):
            for part in ("hi", "lo"):
                T[f"{n}_{part}"] = sb(f"{n}_{part}", [P, KT, PAIR * P], F32R, att)
        for part in ("hi", "lo"):
            T[f"qT_{part}"] = sb(f"qT_{part}", [P, 2, CHUNKS, PAIR, P], F32R, att)
            T[f"kT_{part}"] = sb(f"kT_{part}", [P, 2, CHUNKS, PAIR, 2, P], F32R, att)
            T[f"v_{part}"] = sb(f"v_{part}", [P, PAIR, E], F32R, att)
            T[f"pT_{part}"] = sb(f"pT_{part}", [P, 2, UNIT_HEADS, P], F32R, att)
            T[f"oT_{part}"] = sb(f"oT_{part}", [P, E // P, PAIR, P], F32R, att)
        T["probs"] = sb("probs", [P, RING, UNIT_HEADS, P], F32, att)
        w_sb = []
        for n, (a, b) in zip(WEIGHT_NAMES, [(KT, E)] * 3 + [(E // P, D)]):
            if n == "wo":
                raw_w = [sb(f"raw_{m}", [P, KT * E], F32, att) for m in WEIGHT_NAMES]
            w_sb += [sb(f"{n}_hi", [P, a, b], F32R, att), sb(f"{n}_lo", [P, a, b], F32R, att)]
        scan_w = sb("scan_w", [P, 2, KT, F], F32, att)
        att.close()

        wg = [sb(f"wg_{part}", [P, NX, KT, F], H16) for part in ("hi", "lo")]
        wu = [sb(f"wu_{part}", [P, NX, KT, F], H16) for part in ("hi", "lo")]
        wd = [sb(f"wd_{part}", [P, NX, FT, D], F32R) for part in ("hi", "lo")]
        raw_x = [[sb(f"raw_expert{i}_{n}", [P, KT * F]) for n in ("gate", "up", "down")] for i in range(2)]
        late = ExitStack()
        mine, mine2 = (table(n, TILES + 1, NX, stack=late) for n in ("mine", "mine2"))
        late.close()
        xrow = [sb(f"xrow{i}", [P, D]) for i in range(AHEAD)]
        xt16 = [[sb(f"xt16_{part}{i}", [P, KT, P], H16) for part in ("hi", "lo")] for i in range(2)]
        gated = sb("gated", [P, F])
        hid = [sb(f"hidden{i}", [P, F]) for i in range(2)]
        hidT = [sb(f"hiddenT_{part}", [P, FT, P], F32R) for part in ("hi", "lo")]
        yrow = [sb(f"yrow{i}", [P, D]) for i in range(2)]
        fin = [raw_x[c // 2][c % 2][:, :].rearrange("p (t d) -> p t d", d=D) for c in range(NT // 4)]

        banks = [ctx.enter_context(nc.psum_tensor(f"bank{i}", [P, 512], F32)) for i in range(8)]
        psum = [(banks[0:n], banks[3:5], banks[5:7], banks[n:3] + banks[7:8]) for n in (JOB_BANKS[False], JOB_BANKS[True])]
        xt_ps, g_ps, u_ps, (ht_ps, y_ps) = (banks[i:i + 2] for i in range(0, 8, 2))

        w_in = [[sem(f"{tag}_{n}_in") for n in WEIGHT_NAMES] for tag in ("self", "cross")]
        w_hi_done, w_ready = sem("w_hi_done"), sem("w_ready")
        distance = R["yT"][:, 0:2, :].bitcast(I32)
        distance_ready, mask_steps = sem("distance_ready"), sem("mask_steps")
        consts, zeroed, k_zeroed = sem("consts"), sem("zeroed"), sem("k_zeroed")
        tables, tables_pool = sem("tables"), sem("tables_pool")
        scan_in, scan_done, max_all, scale_ready = sem("scan_in"), sem("scan_done"), sem("max_all"), sem("scale_ready")
        wr_in = sem("wr_in")
        raw_in = [sem("raw_in_even"), sem("raw_in_odd")]
        raw_hi, raw_lo = sem("raw_hi"), sem("raw_lo")
        R_sems = {n: sem(n) for n in (
            "pool_chain", "dve_chain", "dve_step", "pool_step", "picked", "exp1_in", "exp1", "exp2_in", "exp2", "sums_ready",
            "ranks_ready", "dve_parts", "slots_ready", "wt_ready", "dispatched")}
        dispatched, pool_step = R_sems["dispatched"], R_sems["pool_step"]
        chain, plan_ready, slots_in = sem("chain"), sem("plan_ready"), sem("slots_in")
        get_ready, put_ready = sem("get_ready"), sem("put_ready")
        xt_mm, xt_hi, xt_lo = sem("xt_mm"), sem("xt_hi"), sem("xt_lo")
        x_gathered = [sem(f"x_gathered{i}") for i in range(AHEAD)]
        g_mm, u_mm, silu_done, hid_done, ht_mm, ht_hi, ht_lo = (
            sem("g_mm"), sem("u_mm"), sem("silu_done"), sem("hid_done"), sem("ht_mm"), sem("ht_hi"), sem("ht_lo"))
        y_mm, y_sb, y_added = sem("y_mm"), sem("y_sb"), sem("y_added")
        f_in = [sem(f"f_in{c}") for c in range(NT // 4)]
        f_stats, f_mom, f_var, f_rstd, f_done, f_out, f_shift = (
            sem("f_stats"), sem("f_mom"), sem("f_var"), sem("f_rstd"), sem("f_done"), sem("f_out"), sem("f_shift"))
        f_last = sem("f_last")

        def scan_load(sp, i):
            if not (isinstance(i, int) and i == 0):
                sp.wait_ge(scan_done, i)
            for n, w in enumerate((w_gate, w_up)):
                sp.dma_start(scan_w[:, n, :, :], w[i].rearrange("(k p) f -> p k f", p=P)).then_inc(scan_in, 16)

        def scan_max(dve, i):
            dve.wait_ge(scan_in, 32 * i + 32)
            dve.wait_ge(k_zeroed, 2)
            dve.tensor_reduce(absmax[:, i, :] if isinstance(i, int) else
                              absmax[:, bass.ds(i, 1), :].rearrange("p a b -> p (a b)"),
                              scan_w[:, :, :, :].rearrange("p n k f -> p n (k f)"), AX.X, ALU.max,
                              apply_absolute_value=True).then_inc(scan_done, 1)

        self_hooks, cross_hooks = {}, {}
        router_stage = Router(nc, R, R_sems, lists, KT, NX)
        self_att = attention_stage(nc, ctx, "self", False, x, x, w_sb, mask, ident, ident16, psum[0], T, [x1],
                                   (w_ready, 0), scan_load, scan_max, hooks=self_hooks)
        cross_att = attention_stage(nc, ctx, "cross", True, x1, ctxt, w_sb, mask, ident, ident16, psum[1], T,
                                    [t[0:TOK, :].rearrange("(b p) d -> b p d", p=S) for t in (x2, acc)],
                                    (w_ready, 4), route=router_stage, hooks=cross_hooks)
        pe_end_self, pe_end_cross = self_att[5]["pe"], cross_att[5]["pe"]

        def load_weights(eng, ws, w_in):
            for n, w in enumerate(ws):
                k = KT if n < 3 else E // P
                eng.dma_start(raw_w[n][:, :].rearrange("p (k n) -> p k n", k=k),
                              w.rearrange("(k p) n -> p k n", p=P)).then_inc(w_in[n], 16)

        def flat(t):
            return t[:, :, :].rearrange("p k n -> p (k n)")

        def split_hi(act, stage, which):
            for n in which:
                act.wait_ge(w_in[stage][n], 16)
                act.activation(flat(w_sb[2 * n]), raw_w[n][:, :], ACT.Copy,
                               scale=DH ** -0.5 if n == 0 else 1.0).then_inc(w_hi_done, 1)

        def split_lo(dve, stage, n):
            dve.wait_ge(w_hi_done, stage * 4 + n + 1)
            dve.scalar_tensor_tensor(flat(w_sb[2 * n + 1]), raw_w[n][:, :], DH ** -0.5 if n == 0 else 1.0,
                                     flat(w_sb[2 * n]).bitcast(F32), ALU.mult, ALU.subtract).then_inc(w_ready, 1)

        def experts2(t, e):
            return t[:, e, :, :].rearrange("p k n -> p (k n)")

        SPLIT_FIRST = 2
        LOOP = TILES // AHEAD

        PEELED = 2

        def expert_steps(eng, step):
            for j in range(PEELED * AHEAD):
                step(j, j % AHEAD)
            with eng.Fori(PEELED, LOOP) as m:
                for c in range(AHEAD):
                    step(m * AHEAD + c, c)
            for j in range(LOOP * AHEAD, TILES):
                step(j, j % AHEAD)

        def within(j):
            return not isinstance(j, int) or j < TILES

        def splits_at(j):
            e = SPLIT_FIRST + j if isinstance(j, int) else NX
            return [e] if e < NX else []
        assert LOOP * AHEAD + 1 < TILES

        def load_self_weights(sp):
            load_weights(sp, (a_wq, a_wk, a_wv, a_wo), w_in[0])
            sp.dma_start(R["wr"][:, :, :], router.rearrange("(k p) e -> p k e", p=P)).then_inc(wr_in, 16)

        def load_expert(sp, e):
            for n, w in enumerate((w_gate, w_up, w_down)):
                k = KT if n < 2 else FT
                sp.dma_start(raw_x[e % 2][n][:, :].rearrange("p (k f) -> p k f", k=k),
                             w[e].rearrange("(k p) f -> p k f", p=P)).then_inc(raw_in[e % 2], 16)

        def load_cross_rows(sp):
            sp.wait_ge(*self_att[5]["projected"])
            cross_att[6](sp)

        def cross_hi(act):
            act.wait_ge(*self_att[5]["projected"])
            split_hi(act, 1, range(3))

        def cross_lo(dve):
            for n in range(2):
                split_lo(dve, 1, n)

        def expert_hi(act, e, parts=range(3)):
            for n in parts:
                act.wait_ge(raw_in[e % 2], 48 * (e // 2 + 1))
                act.activation(experts2((wg, wu, wd)[n][0], e), raw_x[e % 2][n][:, :], ACT.Copy,
                               scale=1.0 if n == 2 else w_scale[:, n:n + 1]).then_inc(raw_hi, 1)

        def first_experts_hi(act):
            act.wait_ge(*cross_att[5]["out"])
            act.wait_ge(scale_ready, 1)
            for e in range(SPLIT_FIRST):
                expert_hi(act, e)

        def zeros_beside(part):
            return T[f"kT_{part}"][:, :, :, :, :, :].rearrange("p a c b h t -> p (a c b h t)").bitcast(F32)

        before = {("Q", 0): (0, 1), ("K", 0): (2,), None: (3,)}

        def self_scalar_before(act, job):
            if job == ("K", 0):
                act.wait_ge(k_zeroed, 2)
            split_hi(act, 0, before.get(job, ()))

        def self_vector_before(dve, job):
            for n in before.get(job, ()):
                split_lo(dve, 0, n)

        def cross_scalar_before(act, job):
            if job is None:
                act.wait_ge(*pe_end_self)
                split_hi(act, 1, [3])

        def cross_vector_before(dve, job):
            for n in before.get(job, ()):
                if n >= 2:
                    split_lo(dve, 1, n)
            if job is None:
                expert_scale(dve)

        plan_chain = Chain(None, chain, 0, 0)

        def expert_scale(dve):
            plan_chain.eng = dve
            dve.wait_ge(scan_done, NX)
            dve.tensor_reduce(wmax[:, :], absmax[:, :, :].rearrange("p e n -> p n e"), AX.X, ALU.max)\
                .then_inc(max_all, 1)
            dve.wait_ge(max_all, 2)
            plan_chain.link(dve.tensor_scalar(w_exp[:, :], wall[:, :], TINY, None, ALU.max))
            plan_chain.link(dve.tensor_single_scalar(w_inv[:, :].bitcast(I32), w_exp[:, :].bitcast(I32), 0x7F800000,
                                          ALU.bitwise_and))
            plan_chain.link(dve.tensor_scalar(w_exp[:, :], w_inv[:, :], W_TOP, None, ALU.mult))
            plan_chain.link(dve.tensor_scalar(act_inv[:, :], w_exp[:, :], 1.0 / X_SCALE, None, ALU.mult))
            dve.reciprocal(w_scale[:, :], w_exp[:, :]).then_inc(scale_ready, 1)

        self_hooks.update(scalar_before=self_scalar_before, vector_before=self_vector_before)
        cross_hooks.update(scalar_before=cross_scalar_before, vector_before=cross_vector_before)
        self_hooks.update(sync_start=load_self_weights, sync_end=load_cross_rows, scalar_end=cross_hi,
                          vector_end=cross_lo)
        cross_hooks.update(scalar_end=first_experts_hi)
        block = ctx.enter_context(nc.Block())

        @block.sync
        def _(sp):
            self_att[0](sp)
            sp.wait_ge(w_ready, 8)
            for e in range(2):
                load_expert(sp, e)
            cross_att[0](sp)
            for e in range(2, NX):
                sp.wait_ge(raw_lo, 3 * (e - 1))
                load_expert(sp, e)
            sp.wait_ge(y_added, 16 * TILES)
            fin_src = acc[0:TOK, :].rearrange("(c t p) d -> c p t d", p=P, t=4)
            fin_dst = out.rearrange("b p d -> (b p) d").rearrange("(c t p) d -> c p t d", p=P, t=4)
            for c in range(NT // 4):
                sp.dma_start(fin[c], fin_src[c]).then_inc(f_in[c], 16)
            for c in range(NT // 4):
                if c < NT // 4 - 1:
                    sp.wait_ge(f_done, 4 * (c + 1))
                else:
                    sp.wait_ge(f_last, 4)
                sp.dma_start(fin_dst[c], fin[c]).then_inc(f_out, 16)
            sp.wait_ge(f_out, 16 * (NT // 4))

        @block.gpsimd
        def _(pool):
            pool.memset(ident[:, :], 0.0).then_inc(zeroed, 1)
            pool.memset(ident16[:, :], 0.0).then_inc(zeroed, 1)
            pool.wait_ge(zeroed, 2)
            for m in (ident, ident16):
                pool.affine_select(out=m[:, :], in_=m[:, :], compare_op=ALU.not_equal, fill=1.0, base=0,
                                   pattern=[[-1, P]], channel_multiplier=1).then_inc(consts, 1)
            pool.iota(distance, [[0, 2], [-1, P]], base=P, channel_multiplier=1,
                      allow_small_or_imprecise_dtypes=True).then_inc(distance_ready, 1)
            pool.memset(zeros_beside("lo"), 0.0).then_inc(k_zeroed, 1)
            pool.memset(T["minus_half"][:, :], -0.5).then_inc(consts, 1)
            pool.memset(T["eps"][:, :], EPS).then_inc(consts, 1)
            pool.wait_ge(consts, 4)
            n = 0
            for t, pattern, base, per_partition in (
                    (e_of[:, :], [[1, NX]], 0, 0), 
                    (edges[:, :], [[P, NT]], 0, 0), (tile_no[:, :], [[1, TILES + 1]], 0, 0),
                    (first_place[:, :], [[TOK, NX]], 0, 0), (R["base"][:, :], [[TOK, NX]], 0, 0),
                    (first_col[:, :], [[NT, NX]], -COLS, 0), (slot[:, :, 1].bitcast(I32), [[0, COLS + 1]], TOK, 1),
                    (R["token_f"][:, :], [[P, PAIR]], -PAIR * P, 1),
                    (R["place_i"][:, :], [[P, 2 * PAIR]], P * COLS, 1)):
                pool.iota(t, pattern, base=base, channel_multiplier=per_partition,
                          allow_small_or_imprecise_dtypes=True).then_inc(tables_pool, 1)
                n += 1
                pool.wait_ge(tables_pool, n)
            for t, v in ((below[:, :, :], 1.0), (R["earlier"][:, :], 1.0), (R["ones16"][:, :], 1.0),
                         (zero_row[:, :], 0.0), (slot[:, :, 0], 0.0), (R["meta"][:, :, :, :], 0.0), (R["ones"][:, :], 1.0),
                         (R["pair_tokens"][:, :], float(PAIR * P)), (f_half[:, :], -0.5)):
                pool.memset(t, v).then_inc(tables_pool, 1)
                n += 1
                pool.wait_ge(tables_pool, n)
            pool.affine_select(out=below[:, :, :], in_=below[:, :, :], compare_op=ALU.is_gt, fill=0.0, base=0,
                               pattern=[[1, NX], [-1, NX]], channel_multiplier=0).then_inc(tables_pool, 1)
            pool.affine_select(out=R["earlier"][:, :], in_=R["earlier"][:, :], compare_op=ALU.is_gt, fill=0.0, base=0,
                               pattern=[[1, P]], channel_multiplier=-1).then_inc(tables_pool, 1)
            n += 2
            pool.wait_ge(tables_pool, n)
            pool.dma_start(lists[0:P * COLS, :].rearrange("(p j) c -> p j c", p=P), slot[:, 0:COLS, :]).then_inc(dispatched, 16)
            pool.dma_start(x2[TOK:TOK + P, :], zero_row[:, :]).then_inc(dispatched, 16)
            pool.dma_start(acc[TOK:TOK + P, :], zero_row[:, :]).then_inc(dispatched, 16)
            pool.wait_ge(dispatched, 48)
            pool.sem_inc(tables, 1)
            pool.wait_ge(w_ready, 4)
            load_weights(pool, (c_wq, c_wk, c_wv, c_wo), w_in[1])
            self_att[4](pool)
            pool.wait_ge(max_all, 1)
            pool.partition_all_reduce(wall[:, :], wmax[:, :], P, bass.bass_isa.ReduceOp.max).then_inc(max_all, 1)
            cross_att[4](pool)

            pool.wait_ge(dispatched, 32 * (NT + PAIR) + 48)
            pool.dma_start(slot[:, 0:COLS, :], lists[0:P * COLS, :].rearrange("(p j) c -> p j c", p=P)).then_inc(slots_in, 16)
            pool.wait_ge(plan_ready, 1)
            pool.wait_ge(slots_in, 16)
            pool.wait_ge(*cross_att[5]["stored"])

            def step():
                pool.sem_inc(pool_step, 1)

            def gather(j, c):
                if not isinstance(j, int) or j >= AHEAD:
                    pool.wait_ge(xt_mm, j - AHEAD + 1)
                col = pool.value_load(col_i[0:1, bass.ds(j, 1)], min_val=0, max_val=COLS)
                pool.tensor_copy(get_tok[c][:, :], slot[:, bass.ds(col, 1), 1].bitcast(I32)).then_inc(get_ready, 1)
                pool.tensor_copy(get_w[c][:, :], slot[:, bass.ds(col, 1), 0]).then_inc(get_ready, 1)
                pool.wait_ge(get_ready, j * 2 + 2)
                step()
                pool.indirect_dma_start(out=xrow[c][:, :], out_offset=None, in_=x2,
                                        in_offset=bass.IndirectOffsetOnAxis(ap=get_tok[c][:, :], axis=0))\
                    .then_inc(x_gathered[c], 16)

            def put(j, c):
                if not isinstance(j, int) or j >= 2:
                    pool.wait_ge(y_added, 16 * (j - 1))
                    step()
                pool.tensor_copy(put_tok[c % 2][:, :], get_tok[c][:, :]).then_inc(put_ready, 1)
                pool.tensor_copy(put_w[c % 2][:, :], get_w[c][:, :]).then_inc(put_ready, 1)
                pool.wait_ge(put_ready, j * 2 + 2)

            def add_rows(j, s):
                if not isinstance(j, int) or j >= 1:
                    pool.wait_ge(y_added, 16 * j)
                pool.wait_ge(y_sb, j + 1)
                step()
                pool.indirect_dma_start(out=acc, out_offset=bass.IndirectOffsetOnAxis(ap=put_tok[s][:, :], axis=0),
                                        in_=yrow[s][:, :], in_offset=None, compute_op=ALU.add).then_inc(y_added, 16)

            for c in range(AHEAD):
                gather(c, c)

            def expert_step(j, c):
                put(j, c)
                if within(j + AHEAD if isinstance(j, int) else j):
                    gather(j + AHEAD, c)
                add_rows(j, c % 2)

            expert_steps(pool, expert_step)
            for c in range(NT // 4):
                four = slice(4 * c, 4 * c + 4)
                pool.wait_ge(f_var, c + 1)
                pool.tensor_tensor(frstd[:, four], fvar[:, four], f_half[:, four], ALU.pow).then_inc(f_rstd, 1)

        @block.scalar
        def _(act):
            self_att[2](act)
            cross_att[2](act)

            def turn_x(j, s):
                act.wait_ge(xt_mm, j + 1)
                if not isinstance(j, int) or j >= 2:
                    act.wait_ge(u_mm, j - 1)
                act.activation(xt16[s][0][:, :, :].rearrange("p k t -> p (k t)"), xt_ps[s][:, 0:KT * P], ACT.Copy,
                               scale=X_SCALE).then_inc(xt_hi, 1)

            def silu(j, s):
                act.wait_ge(g_mm, j + 1)
                if not isinstance(j, int) or j >= 1:
                    act.wait_ge(hid_done, j)
                act.activation(gated[:, :], g_ps[s][:, :], ACT.Silu, scale=act_inv[:, 0:1]).then_inc(silu_done, 1)

            def turn_h(j):
                act.wait_ge(ht_mm, j + 1)
                if not isinstance(j, int) or j >= 1:
                    act.wait_ge(y_mm, j)
                act.activation(hidT[0][:, :, :].rearrange("p k t -> p (k t)"), ht_ps[:, :], ACT.Copy)\
                    .then_inc(ht_hi, 1)

            turn_x(0, 0)
            turn_x(1, 1)
            silu(0, 0)

            def expert_step(j, c):
                turn_h(j)
                for e in splits_at(j):
                    expert_hi(act, e, [0])
                if within(j + 1):
                    silu(j + 1, (c + 1) % 2)
                for e in splits_at(j):
                    expert_hi(act, e, [1])
                if within(j + 2):
                    turn_x(j + 2, c % 2)
                for e in splits_at(j):
                    expert_hi(act, e, [2])

            expert_steps(act, expert_step)
            for c in range(NT // 4 - 1):
                act.wait_ge(f_shift, c + 1)
                for t in range(4):
                    n = 4 * c + t
                    act.activation(fin[c][:, t, :], fin[c][:, t, :], ACT.Identity, bias=fshift[:, n:n + 1],
                                   scale=frstd[:, n:n + 1]).then_inc(f_done, 1)

        @block.vector
        def _(dve):
            dve.wait_ge(distance_ready, 1)
            dve.tensor_scalar(distance, distance, DIL - 1, None, ALU.bitwise_and).then_inc(mask_steps, 1)
            dve.wait_ge(mask_steps, 1)
            both_heads = mask[:, :].rearrange("p (h t) -> p h t", t=P)
            dve.tensor_scalar(both_heads, distance, 0, MASKED, ALU.is_gt, ALU.mult).then_inc(mask_steps, 1)
            dve.wait_ge(mask_steps, 2)
            for g in range(P // SEG):
                part = slice(g * SEG, (g + 1) * SEG)
                dve.memset(both_heads[part, :, part], 0.0).then_inc(mask_steps, 1)
            dve.memset(zeros_beside("hi"), 0.0).then_inc(k_zeroed, 1)
            self_att[3](dve)
            dve.sem_inc(R_sems["slots_ready"], 1)
            dve.sem_inc(R_sems["wt_ready"], 1)
            cross_att[3](dve)
            link = plan_chain.link

            TTs = dve.tensor_tensor

            def expert_lo(e, parts=range(3)):
                for n in parts:
                    dve.wait_ge(raw_hi, 3 * e + n + 1)
                    raw, (hi, lo) = raw_x[e % 2][n][:, :], (wg, wu, wd)[n]
                    if n < 2:
                        dve.scalar_tensor_tensor(experts2(lo, e), raw, w_scale[:, n:n + 1], experts2(hi, e),
                                                 ALU.mult, ALU.subtract).then_inc(raw_lo, 1)
                    else:
                        TTs(experts2(lo, e), raw, experts2(hi, e).bitcast(F32), ALU.subtract).then_inc(raw_lo, 1)

            expert_lo(0)

            dve.wait_ge(R_sems["ranks_ready"], NX)
            link(TTs(ntok[:, :], R["base"][:, :], first_place[:, :], ALU.subtract))
            link(TTs(cmp16[:, :, :], over(ntok[:, :], NT), under(edges[:, :], NX), ALU.is_gt))
            link(dve.tensor_reduce(some[:, :], cmp16[:, :, :], AX.X, ALU.add))
            link(dve.tensor_scalar(tiles_e[:, :], some[:, :], 1.0, None, ALU.max))
            link(TTs(cmp8[:, :, :], below[:, :, :], under(tiles_e[:, :], NX), ALU.mult))
            link(dve.tensor_reduce(cum0[:, :], cmp8[:, :, :], AX.X, ALU.add))
            link(TTs(cum1[:, :], cum0[:, :], tiles_e[:, :], ALU.add))
            link(TTs(offset[:, :], first_col[:, :], cum0[:, :], ALU.subtract))
            N = TILES + 1
            link(TTs(mine[:, :, :], over(tile_no[:, :], NX), under(cum0[:, :], N), ALU.is_ge))
            link(TTs(mine2[:, :, :], over(tile_no[:, :], NX), under(cum1[:, :], N), ALU.is_ge))
            link(TTs(mine[:, :, :], mine[:, :, :], mine2[:, :, :], ALU.subtract))
            link(TTs(mine2[:, :, :], mine[:, :, :], under(e_of[:, :], N), ALU.mult))
            link(dve.tensor_reduce(expert_f[:, :], mine2[:, :, :], AX.X, ALU.add))
            link(dve.tensor_copy(expert_i[:, :], expert_f[:, :]))
            link(TTs(mine2[:, :, :], over(tile_no[:, :], NX), under(offset[:, :], N), ALU.add))
            link(TTs(mine2[:, :, :], mine2[:, :, :], mine[:, :, :], ALU.mult))
            link(dve.tensor_reduce(col_f[:, :], mine2[:, :, :], AX.X, ALU.add))
            dve.tensor_scalar(col_i[:, :], col_f[:, :], float(COLS), None, ALU.add).then_inc(plan_ready, 1)

            def turn_x(j, s):
                dve.wait_ge(xt_hi, j + 1)
                dve.scalar_tensor_tensor(xt16[s][1][:, :, :].rearrange("p k t -> p (k t)"), xt_ps[s][:, 0:KT * P],
                                         X_SCALE, xt16[s][0][:, :, :].rearrange("p k t -> p (k t)"),
                                         ALU.mult, ALU.subtract).then_inc(xt_lo, 1)

            def hidden(j, s):
                dve.wait_ge(u_mm, j + 1)
                dve.wait_ge(silu_done, j + 1)
                dve.scalar_tensor_tensor(hid[s][:, :], u_ps[s][:, :], act_inv[:, 1:2], gated[:, :],
                                         ALU.mult, ALU.mult).then_inc(hid_done, 1)

            def turn_h(j):
                dve.wait_ge(ht_hi, j + 1)
                TTs(hidT[1][:, :, :].rearrange("p k t -> p (k t)"), ht_ps[:, :],
                    hidT[0][:, :, :].rearrange("p k t -> p (k t)").bitcast(F32), ALU.subtract).then_inc(ht_lo, 1)

            def weigh(j, s):
                if not isinstance(j, int) or j >= 2:
                    dve.wait_ge(y_added, 16 * (j - 1))
                dve.wait_ge(y_mm, j + 1)
                dve.wait_ge(put_ready, j * 2 + 2)
                dve.tensor_scalar(yrow[s][:, :], y_ps[:, 0:D], put_w[s][:, :], None, ALU.mult).then_inc(y_sb, 1)

            for e in range(1, SPLIT_FIRST):
                expert_lo(e)
            turn_x(0, 0)
            turn_x(1, 1)
            hidden(0, 0)

            def expert_step(j, c):
                turn_h(j)
                for e in splits_at(j):
                    expert_lo(e, [0])
                if within(j + 1):
                    hidden(j + 1, (c + 1) % 2)
                if within(j + 2):
                    turn_x(j + 2, c % 2)
                for e in splits_at(j):
                    expert_lo(e, [1])
                weigh(j, c % 2)
                for e in splits_at(j):
                    expert_lo(e, [2])

            expert_steps(dve, expert_step)

            def last_shift(c):
                four = slice(4 * c, 4 * c + 4)
                dve.wait_ge(f_rstd, c + 1)
                dve.scalar_tensor_tensor(fshift[:, four], fmv[:, four, 0], -1.0, frstd[:, four], ALU.mult, ALU.mult)\
                    .then_inc(f_shift, 1)

            for c in range(NT // 4):
                dve.wait_ge(f_in[c], 16)
                for t in range(4):
                    dve.bn_stats(fbn[:, 4 * c + t, :], fin[c][:, t, :]).then_inc(f_stats, 1)
                dve.wait_ge(f_stats, 4 * (c + 1))
                for t in range(4 * c, 4 * c + 4):
                    dve.bn_aggr(fmv[:, t, :], fbn[:, t, :]).then_inc(f_mom, 1)
                dve.wait_ge(f_mom, 4 * (c + 1))
                dve.tensor_scalar(fvar[:, 4 * c:4 * c + 4], fmv[:, 4 * c:4 * c + 4, 1], EPS, None, ALU.add)\
                    .then_inc(f_var, 1)
                if c:
                    last_shift(c - 1)
            last_shift(NT // 4 - 1)
            dve.wait_ge(f_shift, NT // 4)
            for n in range(NT - 4, NT):
                dve.tensor_scalar(fin[-1][:, n % 4, :], fin[-1][:, n % 4, :], frstd[:, n:n + 1], fshift[:, n:n + 1],
                                  ALU.mult, ALU.add).then_inc(f_last, 1)

        @block.tensor
        def _(pe):
            pe.wait_ge(consts, 2)
            pe.wait_ge(mask_steps, 2 + P // SEG)
            self_att[1](pe)
            pe.wait_ge(wr_in, 16)
            pe.wait_ge(tables, 1)
            pe.wait_ge(*self_att[5]["dve"])
            cross_att[1](pe)
            pe.wait_ge(*cross_att[5]["dve"])
            pe.wait_ge(plan_ready, 1)

            def turn_x(j, c):
                pe.wait_ge(x_gathered[c], (j - c) * (16 // AHEAD) + 16)
                if not isinstance(j, int) or j >= 2:
                    pe.wait_ge(xt_lo, j - 1)
                for k in range(KT):
                    mm = pe.transpose(xt_ps[c % 2][:, k * P:(k + 1) * P], xrow[c][:, k * P:(k + 1) * P], ident[:, :])
                mm.then_inc(xt_mm, 1)

            def gate_up(j, s):
                e = pe.value_load(expert_i[0:1, bass.ds(j, 1)], min_val=0, max_val=NX - 1)
                pe.wait_ge(raw_lo, e * 3 + 3)
                pe.wait_ge(xt_lo, j + 1)
                for ps, w, done in ((g_ps[s], wg, g_mm), (u_ps[s], wu, u_mm)):
                    n = 0
                    for k in range(KT):
                        for xx, ww in terms(xt16[s][0], xt16[s][1], w[0], w[1]):
                            mm = pe.matmul(ps[:, :], xx[:, k, :], ww[:, bass.ds(e, 1), k, :].rearrange("p a f -> p (a f)"),
                                           start=(n == 0), stop=(n == 3 * KT - 1))
                            n += 1
                    mm.then_inc(done, 1)

            def turn_h(j, s):
                pe.wait_ge(hid_done, j + 1)
                for k in range(FT):
                    mm = pe.transpose(ht_ps[:, k * P:(k + 1) * P], hid[s][:, k * P:(k + 1) * P], ident[:, :])
                mm.then_inc(ht_mm, 1)

            def down(j):
                e = pe.value_load(expert_i[0:1, bass.ds(j, 1)], min_val=0, max_val=NX - 1)
                pe.wait_ge(ht_lo, j + 1)
                if not isinstance(j, int) or j >= 1:
                    pe.wait_ge(y_sb, j)
                n = 0
                for k in range(FT):
                    for hh, ww in terms(hidT[0], hidT[1], wd[0], wd[1]):
                        mm = pe.matmul(y_ps[:, 0:D], hh[:, k, :], ww[:, bass.ds(e, 1), k, :].rearrange("p a d -> p (a d)"),
                                       start=(n == 0), stop=(n == 3 * FT - 1))
                        n += 1
                mm.then_inc(y_mm, 1)

            turn_x(0, 0)
            turn_x(1, 1)
            gate_up(0, 0)

            def expert_step(j, c):
                turn_h(j, c % 2)
                if within(j + 1):
                    gate_up(j + 1, (c + 1) % 2)
                if within(j + 2):
                    turn_x(j + 2, (c + 2) % AHEAD)
                down(j)

            expert_steps(pe, expert_step)


_INS = ["x", "ctx_1024", "L0_attn_w_q", "L0_attn_w_k", "L0_attn_w_v", "L0_attn_w_o", "L0_xattn_Wq", "L0_xattn_Wk",
        "L0_xattn_Wv", "L0_xattn_Wo", "L0_ffn_router_kernel_DE", "L0_ffn_kernel_gating_EDF", "L0_ffn_kernel_up_EDF",
        "L0_ffn_kernel_down_EFD"]
_OUTS = [((16, 128, 256), "float32")]


def kernel(**inputs):
    import numpy as _np
    import concourse.bacc as _bacc
    from concourse import mybir as _mybir
    from concourse.bass_utils import run_bass_kernel_spmd as _run

    nc = _bacc.Bacc("TRN2", target_bir_lowering=False, num_devices=1)
    arrays, args = {}, []
    for name in _INS:
        a = _np.ascontiguousarray(inputs[name])
        arrays[f"in_{name}_dram"] = a
        args.append(nc.dram_tensor(f"in_{name}_dram", a.shape, _mybir.dt.from_np(a.dtype), kind="ExternalInput").ap())
    outs = []
    for i, (shape, dtype) in enumerate(_OUTS):
        dt = _mybir.dt.from_np(_np.dtype(dtype))
        outs.append(nc.dram_tensor(f"out_{i}_dram", shape, dt, kind="ExternalOutput").ap())
    build(nc, args, outs[0])
    r = _run(nc, [arrays], core_ids=[0])
    got = tuple(r.results[0][f"out_{i}_dram"] for i in range(len(_OUTS)))
    return got[0]
```
